# Optimizing a Trainium2 kernel written in Bass

```python
import numpy as np
import jax
import jax.numpy as jnp

def _softmax(x, axis=-1):
    return jax.nn.softmax(x, axis=axis)

def _gelu(x):
    return jax.nn.gelu(x, approximate=True)

def _silu(x):
    return jax.nn.silu(x)

def _sigmoid(x):
    return jax.nn.sigmoid(x)

def _layernorm(x, axis=-1, eps=1e-05):
    m = jnp.mean(x, axis=axis, keepdims=True)
    v = jnp.var(x, axis=axis, keepdims=True)
    return (x - m) / jnp.sqrt(v + eps)

def _scatter_add(tgt, idx, src, axis=0):
    return tgt.at[idx].add(src)

def _segment_sum(src, seg, n):
    return jax.ops.segment_sum(src, seg, n)
kernel_name = 'mk_vit_tower_d1_tok_img768_r4_afa6cb'

def setup_inputs(seed: int=0):
    np.random.seed(seed)
    _w = jnp.asarray

    def _rec_inputs():
        import jax
        import jax.numpy as jnp
        _rk = jax.random.key(seed)
        x = -0.000348323 + 0.999952 * jax.random.normal(jax.random.fold_in(_rk, 1), (8, 3, 128, 128), jnp.float32)
        return x
    x = _rec_inputs()

    def _L0_tok_setup():
        import jax, jax.numpy as jnp
        import numpy as np
        PATCH = 16
        DIM = 192
        LN_EPS = 1e-05

        def _spt_forward(x, ln_gamma, ln_beta, w, b):
            B, C, H, W = x.shape
            p = PATCH
            x_right = jnp.pad(x, ((0, 0), (0, 0), (0, 0), (1, 0)))[:, :, :, :-1]
            x_left = jnp.pad(x, ((0, 0), (0, 0), (0, 0), (0, 1)))[:, :, :, 1:]
            x_down = jnp.pad(x, ((0, 0), (0, 0), (1, 0), (0, 0)))[:, :, :-1, :]
            x_up = jnp.pad(x, ((0, 0), (0, 0), (0, 1), (0, 0)))[:, :, 1:, :]
            xc = jnp.concatenate((x, x_right, x_left, x_down, x_up), axis=1)
            C5 = 5 * C
            h, wgrid = (H // p, W // p)
            tokens = xc.reshape(B, C5, h, p, wgrid, p)
            tokens = tokens.transpose(0, 2, 4, 3, 5, 1)
            tokens = tokens.reshape(B, h * wgrid, p * p * C5)
            mean = jnp.mean(tokens, axis=-1, keepdims=True)
            var = jnp.var(tokens, axis=-1, keepdims=True)
            normed = (tokens - mean) * jax.lax.rsqrt(var + LN_EPS) * ln_gamma + ln_beta
            return jnp.einsum('bnd,de->bne', normed, w) + b
        key = jax.random.key(seed)
        k1, k2 = jax.random.split(key)
        B, C, H, W = (32, 3, 96, 96)
        patch_dim = PATCH * PATCH * 5 * C
        x = jax.random.normal(k1, (B, C, H, W), dtype=jnp.float32)
        ln_gamma = jnp.ones((patch_dim,), dtype=jnp.float32)
        ln_beta = jnp.zeros((patch_dim,), dtype=jnp.float32)
        w = jax.random.normal(k2, (patch_dim, DIM), dtype=jnp.float32) * patch_dim ** (-0.5)
        b = jnp.zeros((DIM,), dtype=jnp.float32)
        return {'x': x, 'ln_gamma': ln_gamma, 'ln_beta': ln_beta, 'w': w, 'b': b}
    _L0_tok_all = _L0_tok_setup()
    _L0_tok_in = {k: v for k, v in _L0_tok_all.items() if k in ('ln_gamma', 'ln_beta', 'w', 'b')}
    del _L0_tok_all

    def _L0_attn_setup():
        import jax, jax.numpy as jnp
        import numpy as np
        B, S, D = (2, 512, 192)
        H, STRIDE = (12, 8)
        HD = D // H

        def _stride_mask(S, stride, causal):
            i = jnp.arange(S)[:, None]
            j = jnp.arange(S)[None, :]
            strided = j % stride == 0
            if causal:
                strided = strided & (j <= i)
            return strided | (j == i) | (j == i - 1)
        key = jax.random.key(seed)
        k0, k1, k2 = jax.random.split(key, 3)
        x = jax.random.normal(k0, (B, S, D), dtype=jnp.float32)
        qkv_w = jax.random.normal(k1, (3 * D, D), dtype=jnp.float32) * 0.02
        qkv_b = jnp.zeros((3 * D,), dtype=jnp.float32)
        out_w = jax.random.normal(k2, (D, D), dtype=jnp.float32) * 0.02
        out_b = jnp.zeros((D,), dtype=jnp.float32)
        return {'x': x, 'qkv_w': qkv_w, 'qkv_b': qkv_b, 'out_w': out_w, 'out_b': out_b}
    _L0_attn_all = _L0_attn_setup()
    _L0_attn_in = {k: v for k, v in _L0_attn_all.items() if k in ('qkv_w', 'qkv_b', 'out_w', 'out_b')}
    del _L0_attn_all

    def _L0_ffn_setup():
        import jax, jax.numpy as jnp
        import numpy as np
        E, C, F, K = (8, 192, 768, 2)
        key = jax.random.key(seed)
        k0, k1, k2, k3 = jax.random.split(key, 4)
        B, T = (8, 512)
        return {'x': jax.random.normal(k0, (B, T, C), jnp.float32), 'router_w': jax.random.normal(k1, (E, C), jnp.float32) * 0.02, 'w1': jax.random.normal(k2, (E, C, F), jnp.float32) * 0.02, 'b1': jnp.zeros((E, F), jnp.float32), 'w2': jax.random.normal(k3, (E, F, C), jnp.float32) * 0.02, 'b2': jnp.zeros((E, C), jnp.float32)}
    _L0_ffn_all = _L0_ffn_setup()
    _L0_ffn_in = {k: v for k, v in _L0_ffn_all.items() if k in ('router_w', 'w1', 'b1', 'w2', 'b2')}
    del _L0_ffn_all
    return {'x': x, 'L0_tok_ln_gamma': _L0_tok_in['ln_gamma'], 'L0_tok_ln_beta': _L0_tok_in['ln_beta'], 'L0_tok_w': _L0_tok_in['w'], 'L0_tok_b': _L0_tok_in['b'], 'L0_attn_qkv_w': _L0_attn_in['qkv_w'], 'L0_attn_qkv_b': _L0_attn_in['qkv_b'], 'L0_attn_out_w': _L0_attn_in['out_w'], 'L0_attn_out_b': _L0_attn_in['out_b'], 'L0_ffn_router_w': _L0_ffn_in['router_w'], 'L0_ffn_w1': _L0_ffn_in['w1'], 'L0_ffn_b1': _L0_ffn_in['b1'], 'L0_ffn_w2': _L0_ffn_in['w2'], 'L0_ffn_b2': _L0_ffn_in['b2']}

def reference(x, L0_tok_ln_gamma, L0_tok_ln_beta, L0_tok_w, L0_tok_b, L0_attn_qkv_w, L0_attn_qkv_b, L0_attn_out_w, L0_attn_out_b, L0_ffn_router_w, L0_ffn_w1, L0_ffn_b1, L0_ffn_w2, L0_ffn_b2):
    import jax
    import jax.numpy as jnp

    def _L0_tok_ref(x, ln_gamma, ln_beta, w, b):
        import jax, jax.numpy as jnp
        import numpy as np
        PATCH = 16
        DIM = 192
        LN_EPS = 1e-05

        def _spt_forward(x, ln_gamma, ln_beta, w, b):
            B, C, H, W = x.shape
            p = PATCH
            x_right = jnp.pad(x, ((0, 0), (0, 0), (0, 0), (1, 0)))[:, :, :, :-1]
            x_left = jnp.pad(x, ((0, 0), (0, 0), (0, 0), (0, 1)))[:, :, :, 1:]
            x_down = jnp.pad(x, ((0, 0), (0, 0), (1, 0), (0, 0)))[:, :, :-1, :]
            x_up = jnp.pad(x, ((0, 0), (0, 0), (0, 1), (0, 0)))[:, :, 1:, :]
            xc = jnp.concatenate((x, x_right, x_left, x_down, x_up), axis=1)
            C5 = 5 * C
            h, wgrid = (H // p, W // p)
            tokens = xc.reshape(B, C5, h, p, wgrid, p)
            tokens = tokens.transpose(0, 2, 4, 3, 5, 1)
            tokens = tokens.reshape(B, h * wgrid, p * p * C5)
            mean = jnp.mean(tokens, axis=-1, keepdims=True)
            var = jnp.var(tokens, axis=-1, keepdims=True)
            normed = (tokens - mean) * jax.lax.rsqrt(var + LN_EPS) * ln_gamma + ln_beta
            return jnp.einsum('bnd,de->bne', normed, w) + b
        return _spt_forward(x, ln_gamma, ln_beta, w, b)

    def _L0_attn_ref(x, qkv_w, qkv_b, out_w, out_b):
        import jax, jax.numpy as jnp
        import numpy as np
        B, S, D = (2, 512, 192)
        H, STRIDE = (12, 8)
        HD = D // H

        def _stride_mask(S, stride, causal):
            i = jnp.arange(S)[:, None]
            j = jnp.arange(S)[None, :]
            strided = j % stride == 0
            if causal:
                strided = strided & (j <= i)
            return strided | (j == i) | (j == i - 1)
        Bx, Sx, Dx = x.shape
        qkv = x @ qkv_w.T + qkv_b
        qkv = qkv.reshape(Bx, Sx, 3, H, HD)
        q, k, v = jnp.transpose(qkv, (2, 0, 3, 1, 4))
        scale = HD ** (-0.5)
        attn = jnp.einsum('bhid,bhjd->bhij', q, k) * scale
        mask = _stride_mask(Sx, STRIDE, True)
        attn = jnp.where(mask[None, None], attn, -jnp.inf)
        a = jax.nn.softmax(attn, axis=-1)
        a = jnp.nan_to_num(a, nan=0.0)
        out = jnp.einsum('bhij,bhjd->bhid', a, v)
        out = jnp.transpose(out, (0, 2, 1, 3)).reshape(Bx, Sx, Dx)
        return out @ out_w.T + out_b

    def _L0_ffn_ref(x, router_w, w1, b1, w2, b2):
        import jax, jax.numpy as jnp
        import numpy as np
        E, C, F, K = (8, 192, 768, 2)
        B, T, Cc = x.shape
        flat = x.reshape(-1, Cc)
        logits = flat @ router_w.T
        probs = jax.nn.softmax(logits.astype(jnp.float32), axis=-1)
        top_w, top_i = jax.lax.top_k(probs, K)
        top_w = (top_w / top_w.sum(-1, keepdims=True)).astype(x.dtype)
        out = jnp.zeros_like(flat)
        for e in range(E):
            w_e = jnp.sum(top_w * (top_i == e), axis=-1)[:, None]
            h = jax.nn.gelu(flat @ w1[e] + b1[e], approximate=False)
            out = out + w_e * (h @ w2[e] + b2[e])
        return out.reshape(B, T, Cc)
    h = _L0_tok_ref(x, L0_tok_ln_gamma, L0_tok_ln_beta, L0_tok_w, L0_tok_b)
    h = h + _L0_attn_ref(_layernorm(h, axis=-1), L0_attn_qkv_w, L0_attn_qkv_b, L0_attn_out_w, L0_attn_out_b)
    h = h + _L0_ffn_ref(_layernorm(h, axis=-1), L0_ffn_router_w, L0_ffn_w1, L0_ffn_b1, L0_ffn_w2, L0_ffn_b2)
    return h

_drawn_inputs = setup_inputs


def setup_inputs(seed=0):
    import zlib

    import numpy as np

    out = dict(_drawn_inputs(seed))
    spreads = {'L0_tok_ln_gamma': (1.0, 0.2),
     'L0_tok_ln_beta': (0.0, 0.1),
     'L0_tok_b': (0.0, 0.1),
     'L0_attn_qkv_b': (0.0, 0.288),
     'L0_attn_out_b': (0.0, 0.1),
     'L0_ffn_b1': (0.0, 0.39),
     'L0_ffn_b2': (0.0, 0.1)}
    factors = {}
    for name, (base, spread) in spreads.items():
        noise = np.random.default_rng([zlib.crc32(name.encode()), seed]).standard_normal(out[name].shape)
        drawn = base * np.exp(spread * noise) if base else spread * noise
        out[name] = jnp.asarray(drawn.astype(out[name].dtype))
    for name, factor in factors.items():
        out[name] = (out[name] * factor).astype(out[name].dtype)
    return out
```

```python
from contextlib import ExitStack

import concourse.bass as bass
from concourse import mybir

F32 = mybir.dt.float32
F32R = mybir.dt.float32r
U32 = mybir.dt.uint32
ALU = mybir.AluOpType
ACT = mybir.ActivationFunctionType
AX_X = mybir.AxisListType.X

P = 128
PATCH = 16
LN_EPS = 1e-5
HEADS = 12
STRIDE = 8
NEG = -1e30


def vit_tower(nc, x, tok_gamma, tok_beta, tok_w, tok_b, qkv_w, qkv_b, out_w, out_b,
              router_w, w1, b1, w2, b2, out):
    B, C, IMG, _ = x.shape
    D = tok_w.shape[1]
    E, _, F = w1.shape
    GRID = IMG // PATCH
    S = GRID * GRID
    T = B * S
    TT = T // P
    HD = D // HEADS
    NK = S // STRIDE
    SHIFTS = 5
    FEAT = SHIFTS * C * PATCH * PATCH
    QR = PATCH // 2
    REM = D - P
    FC = F // P
    SPAN = 3 * D + D + E
    OUT0, ROUT0 = 3 * D, 4 * D
    WROWS = 96
    HALO = 112
    NX = 8
    LMH = 2 * D + 2
    HIGH0 = D + 2
    STAGE = 2 * F + FC * D
    assert (D, HD, S, T, E, F) == (192, 16, 64, 512, 8, 768)

    with ExitStack() as ctx:
        def sb(name, shape, dt=F32):
            return ctx.enter_context(nc.sbuf_tensor(name, shape, dt))

        def sem(name):
            return ctx.enter_context(nc.semaphore(name))

        ps = ctx.enter_context(nc.psum_tensor("ps", [P, 8, 512], F32))

        BAND0 = 160
        band = sb("band", [P, 432])
        from_right = sb("from_right", [P, P])
        from_left = sb("from_left", [P, P])
        ident = band[:, BAND0:BAND0 + P]
        ones_f = sb("ones_f", [P, P])
        ones_r = sb("ones_r", [P, P], F32R)
        neg_half = sb("neg_half", [P, 4])
        group = sb("group", [P, 16])
        group8 = sb("group8", [P, 8])
        tri = sb("tri", [P, NK, 8])
        tri_p = sb("tri_p", [P, NK, 8])
        near = sb("near", [P, 2, 16])
        mask = sb("mask", [P, NK + 2])
        head_of_row = sb("head_of_row", [P, 8])
        head_of_key = sb("head_of_key", [P, HEADS])
        key_rep = sb("key_rep", [S, B, NK, HEADS])
        v_s = sb("v_s", [S, D])
        iota_e = sb("iota_e", [P, E])

        early = sb("early", [P, C * QR * IMG + 2 * GRID * HALO])
        img = early[:, 0:C * QR * IMG].rearrange("p (c q w) -> p c q w", c=C, q=QR)
        halo_g = early[:, C * QR * IMG:].rearrange("p (k w r) -> p k w r", k=2, w=GRID)
        gb_nat = sb("gb_nat", [P, 2, 3, SHIFTS * C])
        gb = sb("gb", [P, 2, SHIFTS, 3 * C])
        gb_halo = sb("gb_halo", [P, 2, 2])
        shifted = sb("shifted", [P, SHIFTS * 2 * C * D])
        wsh = shifted[:, :].rearrange("p (s h n) -> p s h n", s=SHIFTS, h=2)
        merge = sb("merge", [P, (2 * C + 4) * D])
        w_sum = merge[:, 0:2 * C * D].rearrange("p (h c n) -> p h c n", h=2, c=C)
        w_halo = merge[:, 2 * C * D:(2 * C + 2) * D].rearrange("p (k n) -> p k n", k=2)
        wm_halo = merge[:, (2 * C + 2) * D:].rearrange("p (k n) -> p k n", k=2)
        big_r = sb("big_r", [P, 2 * NX * T], F32R)
        xh = big_r[:, 0:NX * T].rearrange("p (k t) -> p k t", k=NX)
        xl = big_r[:, NX * T:].rearrange("p (k t) -> p k t", k=NX)
        sq = sb("sq", [P, 3, 2, T])
        halo = sb("halo", [P, 4 * T])
        x_halo = halo[:, 0:2 * T].rearrange("p (k t) -> p k t", k=2)
        sq_halo = halo[:, 2 * T:].rearrange("p (k t) -> p k t", k=2)
        W1H, W1L, W1R, W2S = 0, F, 2 * F, 3 * F
        wsplit = [sb(f"wsplit{i}", [P, 3 * F + FC * 2 * D], F32R) for i in range(2)]
        wlmh = wsplit[1][:, 0:NX * LMH].rearrange("p (k n) -> p k n", k=NX)
        stage0 = sb("stage0", [P, STAGE])
        staged = [stage0[:, :], early[:, 0:STAGE]]
        mcol = sb("mcol", [P, 2, 2])
        u_part = sb("u_part", [P, D])
        u_sum = sb("u_sum", [P, D])
        bias_row = sb("bias_row", [P, D])
        tokb_row = sb("tokb_row", [P, D])
        qkvb_row = sb("qkvb_row", [P, 3 * D])
        outb_row = sb("outb_row", [P, D])
        st4 = sb("st4", [P, 6, TT])
        h = sb("h", [P, TT, D])
        t_a = sb("t_a", [P, TT, D])

        raw = sb("raw", [P, 9 * 2 * P])
        wraw = raw[0:WROWS, :].rearrange("p (n d) -> p n d", n=9)
        t_b, hb, acc = (raw[:, n * TT * D:(n + 1) * TT * D].rearrange("p (t d) -> p t d", t=TT) for n in range(3))
        wat = sb("wat", [P, 3, SPAN], F32R)
        b1raw = sb("b1raw", [E * FC, P])
        b1t = sb("b1t", [P, E * FC])
        b2sb = sb("b2sb", [E, D])
        bqk = sb("bqk", [P, 4])

        bn = sb("bn", [P, 2, TT, 6])
        mv = sb("mv", [P, 2, TT, 2])
        ve = sb("ve", [P, 2, TT])
        rs = sb("rs", [P, 2, TT])
        norm = sb("norm", [P, TT * 2 * P])
        n1 = n2 = norm[:, :].rearrange("p (t n) -> p t n", t=TT)
        tiles = [a.rearrange("p (w q x) -> p w q x", w=GRID, q=QR)
                 for a in (stage0[:, 0:TT * 2 * P], stage0[:, TT * 2 * P:2 * TT * 2 * P], norm[:, :])]
        NT0 = 2
        nt = sb("nt", [P, 4, NT0 + T], F32R)

        kv = shifted[:, 0:TT * 4 * D].rearrange("p (t s n) -> p t s n", t=TT, s=2)
        vbd = shifted[:, TT * 4 * D:TT * 4 * D + B * D].rearrange("p (b n) -> p b n", b=B)
        qtok = shifted[:, TT * 4 * D + B * D:TT * 4 * D + B * D + TT * D].rearrange("p (t n) -> p t n", t=TT)
        kb = halo[:, 0:4 * D].rearrange("p (r s n) -> p r s n", r=2, s=2)
        prod = halo[:, 4 * D:8 * D].rearrange("p (r s n) -> p r s n", r=2, s=2)
        qb = halo[:, 8 * D:10 * D].rearrange("p (r n) -> p r n", r=2)
        qt = sq[:, 0, :, :]
        kts = sq[:, 1, 0, 0:2 * S].rearrange("p (k n) -> p k n", k=2)
        kbd_a = sq[:, 1, 1, :].rearrange("p (b g j) -> p b g j", b=B, g=8)
        kbd_b = sq[:, 2, 0, 0:B * 4 * NK].rearrange("p (b g j) -> p b g j", b=B, g=4)
        NS = NK + 2
        sc = sb("sc", [P, TT, NS, HEADS])
        pr = sb("pr", [P, TT, NS, HEADS])
        mx = sb("mx", [P, TT, HEADS])
        den = sb("den", [P, TT, HEADS])
        rden = sb("rden", [P, TT, HEADS])
        ptsb = sb("ptsb", [WROWS, 2, P])
        ao = merge[:, 0:TT * 2 * P].rearrange("p (t n) -> p t n", t=TT)
        aot = big_r[:, 0:4 * T].rearrange("p (k t) -> p k t", k=4)
        h2 = merge[:, TT * 2 * P:TT * (2 * P + D)].rearrange("p (t n) -> p t n", t=TT)

        n2t = big_r[:, 4 * T:8 * T].rearrange("p (k t) -> p k t", k=4)
        g_hi = big_r[:, 8 * T:12 * T].rearrange("p (k t) -> p k t", k=4)
        g_lo = big_r[:, 12 * T:16 * T].rearrange("p (k t) -> p k t", k=4)
        NG = 4
        gf = early[:, STAGE:STAGE + NG * T].rearrange("p (k t) -> p k t", k=NG)
        lg = sb("lg", [P, TT, E])
        ex = sb("ex", [P, TT, E])
        top = sb("top", [P, TT, 8])
        topi = sb("topi", [P, TT, 8], U32)
        topf = sb("topf", [P, TT, 8])
        oh = sb("oh", [P, 2, TT, E])
        gs = sb("gs", [P, 2, TT])
        gates = sb("gates", [P, TT, E])
        gt = halo[0:E, 0:T].rearrange("e (t p) -> e t p", t=TT)

        d_img, d_gb, d_halo_w = sem("d_img"), sem("d_gb"), sem("d_halo_w")
        d_wsh = [sem("d_wsh0"), sem("d_wsh1")]
        d_rows, d_small = sem("d_rows"), sem("d_small")
        d_stage = [sem("d_stage0"), sem("d_stage1")]
        d_out = sem("d_out")
        c_halo0, c_gath0, c_pool, c_band, c_shiftm, c_ones, c_mask = (
            sem(n) for n in ("c_halo0", "c_gath0", "c_pool", "c_band", "c_shiftm", "c_ones", "c_mask"))
        s_gbps, s_gb, s_m, s_gather = sem("s_gbps"), sem("s_gb"), sem("s_m"), sem("s_gather")
        s_xt, s_xhi, s_xlo, s_xsq, s_sqsum = (sem(n) for n in ("s_xt", "s_xhi", "s_xlo", "s_xsq", "s_sqsum"))
        s_ht, s_hcopy, s_hedge, s_hhi, s_hlo, s_hsq = (
            sem(n) for n in ("s_ht", "s_hcopy", "s_hedge", "s_hhi", "s_hlo", "s_hsq"))
        s_merge, s_whi, s_wlo = sem("s_merge"), sem("s_whi"), sem("s_wlo")
        s_watps, s_wathi, s_watlo = sem("s_watps"), sem("s_wathi"), sem("s_watlo")
        s_beta, s_emb, s_sumsq = sem("s_beta"), sem("s_emb"), sem("s_sumsq")
        s_stat, s_pow, s_u, s_urow = sem("s_stat"), sem("s_pow"), sem("s_u"), sem("s_urow")
        s_t1, s_t2, s_h = sem("s_t1"), sem("s_t2"), sem("s_h")
        s_bn, s_mv, s_ve, s_rs, s_n = (sem(n) for n in ("s_bn", "s_mv", "s_ve", "s_rs", "s_n"))
        s_hb, s_tile, s_vs, s_vssb = sem("s_hb"), sem("s_tile"), sem("s_vs"), sem("s_vssb")
        s_nt, s_nhi, s_nlo = sem("s_nt"), sem("s_nhi"), sem("s_nlo")
        s_qt, s_qtsb, s_kbd = sem("s_qt"), sem("s_qtsb"), sem("s_kbd")
        s_vps, s_vbd = sem("s_vps"), sem("s_vbd")
        s_tok, s_kvsb = sem("s_tok"), sem("s_kvsb")
        s_kb, s_prod, s_near, s_sps, s_sc, s_mx, s_sub, s_exp = (
            sem(n) for n in ("s_kb", "s_prod", "s_near", "s_sps", "s_sc", "s_mx", "s_sub", "s_exp"))
        s_rden, s_ptps, s_pt, s_pv, s_pvn, s_o = (
            sem(n) for n in ("s_rden", "s_ptps", "s_pt", "s_pv", "s_pvn", "s_o"))
        s_ao = sem("s_ao")
        s_at, s_ahi, s_alo, s_op, s_h2 = (sem(n) for n in ("s_at", "s_ahi", "s_alo", "s_op", "s_h2"))
        s_n2t, s_n2hi, s_n2lo = sem("s_n2t"), sem("s_n2hi"), sem("s_n2lo")
        s_rt, s_gmax, s_gsub, s_gexp, s_gtop, s_gidx, s_goh, s_gden, s_gate = (
            sem(n) for n in ("s_rt", "s_gmax", "s_gsub", "s_gexp", "s_gtop", "s_gidx", "s_goh", "s_gden", "s_gate"))
        s_gtps, s_gt, s_b2, s_acc0 = sem("s_gtps"), sem("s_gt"), sem("s_b2"), sem("s_acc0")
        s_mm1, s_gelu, s_ghi, s_glo, s_mm2 = (sem(n) for n in ("s_mm1", "s_gelu", "s_ghi", "s_glo", "s_mm2"))
        s_w1hi, s_w2hi, s_w1lo, s_w2lo = (sem(n) for n in ("s_w1hi", "s_w2hi", "s_w1lo", "s_w2lo"))
        s_acc = sem("s_acc")
        s_evl, s_w1m, s_dve = sem("s_evl"), sem("s_w1m"), sem("s_dve")

        block = ctx.enter_context(nc.Block())

        XB = [1, 2, 3, 4, 5, 6]
        HB = [1, 2, 3, 4]
        WB = [5, 6, 0, 5]
        EMB0, SQB, UB, BETAB = 1, 6, 0, 7
        LAG = 3
        HPB = [0, 1, 2, 3]
        AB = [4, 5, 6, 7]
        WGROUPS = [(0, 0, 4, 0), (1, 0, 4, 0), (0, 4, 4, 384), (1, 4, 4, 384)]
        XGROUPS = 2 * C

        def gather_halo(eng, k):
            px = img.rearrange("p c q (w x) -> p w c q x", x=PATCH)
            g = nc.gpsimd if k == 0 else nc.vector
            q_edge = QR - 1 if k == 0 else 0
            g.tensor_copy(halo_g[:, k, 1:GRID, 0:3 * QR].rearrange("p w (c q) -> p w c q", c=C),
                          px[:, 0:GRID - 1, :, :, PATCH - 1]).then_inc(s_gather, 1)
            g.tensor_copy(halo_g[:, k, 0:GRID - 1, 3 * QR:6 * QR].rearrange("p w (c q) -> p w c q", c=C),
                          px[:, 1:GRID, :, :, 0]).then_inc(s_gather, 1)
            g.tensor_copy(halo_g[:, k, :, 64:HALO].rearrange("p w (c x) -> p w c x", c=C),
                          px[:, :, :, q_edge, :]).then_inc(s_gather, 1)
        GATHERS = 3

        def retile(copy_op, c):
            copy_op(tiles[c], img[:, c].rearrange("p q (w x) -> p w q x", x=PATCH)).then_inc(s_tile, 1)

        def split_low(pool, e, slot):
            st, ws = staged[slot], wsplit[slot]
            pool.wait_ge(s_w1hi, e * 2 + 2)
            nc.gpsimd.tensor_tensor(ws[:, W1L:W1L + F], st[:, 0:F], ws[:, W1H:W1H + F].bitcast(F32),
                                    ALU.subtract).then_inc(s_w1m, 1)
            pool.wait_ge(s_w1m, e + 1)
            nc.gpsimd.tensor_tensor(ws[REM:P, W1R:W1R + F], st[REM:P, F:2 * F],
                                    ws[REM:P, W1R:W1R + F].bitcast(F32), ALU.subtract).then_inc(s_w1lo, 1)
            pool.wait_ge(s_w1lo, e + 1)
            pool.wait_ge(s_w2hi, e + 1)
            w2v = ws[:, W2S:].rearrange("p (c n) -> p c n", c=FC)
            nc.gpsimd.tensor_tensor(w2v[:, :, 0:D], st[:, 2 * F:].rearrange("p (c n) -> p c n", c=FC),
                                    w2v[:, :, D:].bitcast(F32), ALU.subtract).then_inc(s_w2lo, 1)

        def copy(o, a):
            return nc.scalar.activation(o, a, ACT.Copy)

        def split_high_w1(slot):
            st, ws = staged[slot], wsplit[slot]
            copy(ws[:, W1H:W1H + F], st[:, 0:F]).then_inc(s_w1hi, 1)
            copy(ws[:, W1R:W1R + F], st[:, F:2 * F]).then_inc(s_w1hi, 1)

        def split_high_w2(slot):
            st, ws = staged[slot], wsplit[slot]
            copy(ws[:, W2S:].rearrange("p (c n) -> p c n", c=FC)[:, :, D:],
                 st[:, 2 * F:].rearrange("p (c n) -> p c n", c=FC)).then_inc(s_w2hi, 1)

        def small_dmas(act):
            def every(ap):
                return ap.unsqueeze(0).broadcast_to([P, ap.shape[0]])
            act.wait_ge(c_halo0, 2)
            for gi, vec in enumerate((tok_gamma, tok_beta)):
                v = vec.rearrange("(y x s c) -> y x s c", y=PATCH, x=PATCH, s=SHIFTS)
                for k in range(2):
                    for r0, n, src in halo_rows_of(v, k):
                        act.dma_start(gb_halo[r0:r0 + n, gi, k:k + 1], src.unsqueeze(1),
                                      allow_slow_non_contiguous=True).then_inc(d_halo_w, 16)
            wv = qkv_w.rearrange("(n p) d -> p n d", p=WROWS)
            ov = out_w.rearrange("(n p) d -> p n d", p=WROWS)
            for dst, src in ((wraw[:, 0:6], wv), (wraw[:, 6:8], ov)):
                act.dma_start(dst[:, :, 0:D], src).then_inc(d_small, 16)
                act.dma_start(dst[:, :, D:], src[:, :, P:D]).then_inc(d_small, 16)
            act.dma_start(wraw[0:E, 8, 0:D], router_w).then_inc(d_small, 16)
            act.dma_start(wraw[0:E, 8, D:], router_w[:, P:D]).then_inc(d_small, 16)
            act.dma_start(b1raw[:], b1.rearrange("e (c p) -> (e c) p", p=P)).then_inc(d_small, 16)
            act.dma_start(b2sb[:], b2).then_inc(d_small, 16)
            for n, (o, m) in enumerate(((0, P), (P, REM), (D, P), (D + P, REM))):
                act.dma_start(bqk[0:m, n:n + 1], qkv_b[o:o + m].unsqueeze(1),
                              allow_slow_non_contiguous=True).then_inc(d_small, 16)
            act.dma_start(tokb_row[:], every(tok_b)).then_inc(d_rows, 16)
            act.dma_start(qkvb_row[:], every(qkv_b)).then_inc(d_rows, 16)
            act.dma_start(outb_row[:], every(out_b)).then_inc(d_rows, 16)
        SMALL_DMAS = 12
        GB_HALO_DMAS = 2 * 2 * 3 * C

        def triple(dst, x_of, w_of, x_stationary):
            order = ((0, 0), (0, 1), (1, 0), (2, 2), (3, 2)) if x_stationary else \
                ((0, 0), (1, 0), (0, 1), (2, 2), (3, 2))
            for n, (a, b) in enumerate(order):
                lhs, rhs = (x_of(a), w_of(b)) if x_stationary else (w_of(b), x_of(a))
                mm = nc.tensor.matmul(dst, lhs, rhs, start=(n == 0), stop=(n == 4))
            return mm

        WSH_DMAS = [7, 7]
        HALO_W_DMAS = 2 * 3 * C

        def load_expert(sp, e, slot):
            st = staged[slot]
            w1e, w2e = w1[bass.ds(e, 1)], w2[bass.ds(e, 1)]
            sp.dma_start(st[:, 0:F], w1e[:, 0:P, :].rearrange("o p f -> (o p) f")).then_inc(d_stage[slot], 16)
            for half in range(2):
                sp.dma_start(st[half * REM:half * REM + REM, F:2 * F],
                             w1e[:, P:D, :].rearrange("o p f -> (o p) f")).then_inc(d_stage[slot], 16)
            sp.dma_start(st[:, 2 * F:].rearrange("p (c n) -> p c n", c=FC),
                         w2e.rearrange("o (c p) n -> (o p) c n", p=P)).then_inc(d_stage[slot], 16)
        STAGE_DMAS = 4

        def halo_rows_of(v, k):
            y, s = ((0, 3), (PATCH - 1, 4))[k]
            for c in range(C):
                yield QR * c, QR, v[k * QR:(k + 1) * QR, 0, 1, c]
                yield 3 * QR + QR * c, QR, v[k * QR:(k + 1) * QR, PATCH - 1, 2, c]
                yield 64 + PATCH * c, PATCH, v[y, :, s, c]

        @block.sync
        def _(sp):
            wv = tok_w.rearrange("(p k) e -> p (k e)", k=SHIFTS * C)
            for b in range(B):
                sp.dma_start(img[b * 2 * GRID:(b + 1) * 2 * GRID],
                             x[b].rearrange("c (r q) w -> r c q w", q=QR)).then_inc(d_img, 16)
            OFF = [0, 1, -1, PATCH, -PATCH]
            for half in range(2):
                for s in range(SHIFTS):
                    lo = half * P + OFF[s]
                    first, last = max(0, lo), min(2 * P, lo + P)
                    a, z = first - lo, last - lo
                    cols = slice(s * C * D, (s + 1) * C * D)
                    sp.dma_start(wsh[a:z, s, half], wv[first:last, cols]).then_inc(d_wsh[half], 16)
                    if a > 0:
                        sp.dma_start(wsh[0:a, s, half], wv[0:a, cols]).then_inc(d_wsh[half], 16)
                    if z < P:
                        sp.dma_start(wsh[z:P, s, half], wv[0:P - z, cols]).then_inc(d_wsh[half], 16)
            sp.wait_ge(c_halo0, 2)
            pv = tok_w.rearrange("(y x s c) e -> y x s c e", y=PATCH, x=PATCH, s=SHIFTS)
            for k in range(2):
                for r0, n, src in halo_rows_of(pv, k):
                    sp.dma_start(w_halo[r0:r0 + n, k], src).then_inc(d_halo_w, 16)
            sp.wait_ge(s_xt, XGROUPS)
            load_expert(sp, 0, 0)
            sp.wait_ge(s_ht, 4)
            load_expert(sp, 1, 1)
            with sp.Fori(1, E // 2) as i:
                for slot in range(2):
                    sp.wait_ge(s_w1lo, i * 2 + slot - 1)
                    sp.wait_ge(s_w2lo, i * 2 + slot - 1)
                    load_expert(sp, i * 2 + slot, slot)
            for t in range(TT):
                sp.wait_ge(s_acc, E * TT + t + 1)
                sp.dma_start(out[t * 2:t * 2 + 2].rearrange("b s d -> (b s) d"),
                             acc[:, t]).then_inc(d_out, 16)
            sp.wait_ge(d_out, 16 * TT)


        @block.gpsimd
        def _(pool):
            nc.gpsimd.memset(w_halo[:], 0.0).then_inc(c_halo0, 1)
            nc.gpsimd.memset(gb_halo[:], 0.0).then_inc(c_halo0, 1)
            nc.gpsimd.memset(halo_g, 0.0).then_inc(c_gath0, 1)
            nc.gpsimd.memset(gb_nat[:, :, 2, :], 1.0).then_inc(c_ones, 1)
            step = [0]

            def then(ins):
                step[0] += 1
                ins.then_inc(c_pool, 1)
                pool.wait_ge(c_pool, step[0])

            then(nc.gpsimd.memset(band[:], 0.0))
            then(nc.gpsimd.affine_select(out=band[:], in_=band[:], compare_op=ALU.not_equal, fill=1.0,
                                         base=BAND0, pattern=[[-1, 432]], channel_multiplier=1))
            nc.gpsimd.tensor_copy(from_right[:], band[:, BAND0 + 1:BAND0 + 1 + P]).then_inc(c_band, 1)
            then(nc.gpsimd.tensor_copy(from_left[:], band[:, BAND0 - 1:BAND0 - 1 + P]))
            pool.wait_ge(c_band, 1)
            nc.gpsimd.memset(from_right[:, :].rearrange("p (q x) -> p q x", x=PATCH)[:, :, PATCH - 1:PATCH],
                             0.0).then_inc(c_shiftm, 1)
            nc.gpsimd.memset(from_left[:, :].rearrange("p (q x) -> p q x", x=PATCH)[:, :, 0:1],
                             0.0).then_inc(c_shiftm, 1)
            pool.wait_ge(d_img, 16 * B)
            retile(nc.gpsimd.tensor_copy, 2)
            gather_halo(pool, 0)
            nc.gpsimd.memset(ones_f[:], 1.0).then_inc(c_ones, 1)
            nc.gpsimd.memset(neg_half[:], -0.5).then_inc(c_ones, 1)
            nc.gpsimd.memset(nt[:, :, 0:NT0].bitcast(F32), 0.0).then_inc(c_ones, 1)
            for tile, n, w in ((head_of_row, 8, HD),):
                then(nc.gpsimd.memset(tile[:], 1.0))
                then(nc.gpsimd.affine_select(out=tile[:], in_=tile[:], compare_op=ALU.is_ge, fill=0.0,
                                             base=0, pattern=[[-w, n]], channel_multiplier=1))
                then(nc.gpsimd.affine_select(out=tile[:], in_=tile[:], compare_op=ALU.is_ge, fill=0.0,
                                             base=w - 1, pattern=[[w, n]], channel_multiplier=-1))
            then(nc.gpsimd.memset(head_of_key[:], 0.0))
            for j in range(NK):
                then(nc.gpsimd.affine_select(out=head_of_key[:], in_=head_of_key[:], compare_op=ALU.not_equal,
                                             fill=1.0, base=-HEADS * j, pattern=[[-1, HEADS]],
                                             channel_multiplier=1))
            then(nc.gpsimd.memset(key_rep[:], 0.0))
            then(nc.gpsimd.affine_select(out=key_rep[:], in_=key_rep[:], compare_op=ALU.not_equal, fill=1.0,
                                         base=0, pattern=[[-NK, B], [-1, NK], [0, HEADS]],
                                         channel_multiplier=1))
            then(nc.gpsimd.memset(group[:], 1.0))
            then(nc.gpsimd.affine_select(out=group[:], in_=group[:], compare_op=ALU.is_ge, fill=0.0,
                                         base=0, pattern=[[-8, 16]], channel_multiplier=1))
            then(nc.gpsimd.affine_select(out=group[:], in_=group[:], compare_op=ALU.is_ge, fill=0.0,
                                         base=7, pattern=[[8, 16]], channel_multiplier=-1))
            then(nc.gpsimd.tensor_tensor(group8[:], group[:, 0:8], group[:, 8:16], ALU.add))
            then(nc.gpsimd.memset(tri[:], 0.0))
            then(nc.gpsimd.affine_select(out=tri[:], in_=tri[:], compare_op=ALU.is_ge, fill=NEG,
                                         base=0, pattern=[[-1, NK], [1, 8]], channel_multiplier=0))
            then(nc.gpsimd.tensor_tensor(tri_p[:], tri[:],
                                         group8[:, :].unsqueeze(1).broadcast_to([P, NK, 8]), ALU.mult))
            then(nc.gpsimd.memset(near[:], 0.0))
            then(nc.gpsimd.affine_select(out=near[:], in_=near[:], compare_op=ALU.not_equal, fill=NEG,
                                         base=0, pattern=[[-1, 2], [-8, 16]], channel_multiplier=1))
            then(nc.gpsimd.affine_select(out=near[:, 1], in_=near[:, 1], compare_op=ALU.not_equal, fill=NEG,
                                         base=0, pattern=[[-S, 16]], channel_multiplier=1))
            for e in range(E):
                nc.gpsimd.memset(iota_e[:, e:e + 1], float(e)).then_inc(c_mask, 1)

            for c in range(1, C):
                pool.wait_ge(s_xsq, 2 * c + 2)
                for half in range(2):
                    if c > 1:
                        pool.wait_ge(s_sqsum, 2 * (c - 2) + half + 1)
                    nc.gpsimd.tensor_tensor(sq[:, 0, half], sq[:, 0, half], sq[:, c, half],
                                            ALU.add).then_inc(s_sqsum, 1)
            pool.wait_ge(s_hsq, 1)
            nc.gpsimd.tensor_tensor(sq_halo[0:HALO, 0], sq_halo[0:HALO, 0], sq_halo[0:HALO, 1],
                                    ALU.add).then_inc(s_sqsum, 1)
            pool.wait_ge(c_ones, 4)
            pool.wait_ge(s_stat, 1)
            nc.gpsimd.tensor_tensor(st4[:, 5], st4[:, 4], neg_half[:], ALU.pow).then_inc(s_pow, 1)
            for t in range(TT):
                pool.wait_ge(s_ve, t + 1)
                nc.gpsimd.tensor_tensor(rs[:, 0, t:t + 1], ve[:, 0, t:t + 1], neg_half[:, 0:1],
                                        ALU.pow).then_inc(s_rs, 1)
            split_low(pool, 0, 0)
            pool.wait_ge(d_rows, 16 * 3)
            pool.wait_ge(s_h, TT)
            nc.gpsimd.tensor_tensor(hb[:], h[:], outb_row[:, :].unsqueeze(1).broadcast_to([P, TT, D]),
                                    ALU.add).then_inc(s_hb, 1)
            for t in range(TT):
                pool.wait_ge(s_ve, TT + t + 1)
                nc.gpsimd.tensor_tensor(rs[:, 1, t:t + 1], ve[:, 1, t:t + 1], neg_half[:, 0:1],
                                        ALU.pow).then_inc(s_rs, 1)
            split_low(pool, 1, 1)
            with pool.Fori(1, E // 2) as i:
                for slot in range(2):
                    split_low(pool, i * 2 + slot, slot)

        @block.scalar
        def _(act):
            gv = tok_gamma.rearrange("(h p k) -> p h k", h=2, k=SHIFTS * C)
            bv = tok_beta.rearrange("(h p k) -> p h k", h=2, k=SHIFTS * C)
            act.dma_start(gb_nat[:, :, 0, :], gv).then_inc(d_gb, 16)
            act.dma_start(gb_nat[:, :, 1, :], bv).then_inc(d_gb, 16)
            small_dmas(act)

            act.wait_ge(d_img, 16 * B)
            retile(copy, 1)
            for g in range(XGROUPS):
                c, wh = g // 2, g % 2
                act.wait_ge(s_xt, g + 1)
                src = ps[:, XB[g], :].rearrange("p (w r k) -> p k r w", w=4, k=2)
                for out_t, s_done in ((xh, s_xhi), (sq, s_xsq)):
                    if out_t is xh:
                        dst = xh[:, c:2 * C:C, :]
                    else:
                        dst = sq[:, c]
                    dst = dst.rearrange("p k (r w) -> p k r w", w=GRID)[:, :, :, 4 * wh:4 * wh + 4]
                    nc.scalar.activation(dst, src, ACT.Copy if out_t is xh else ACT.Square).then_inc(s_done, 1)
            for k in range(2):
                for wh in range(2):
                    act.wait_ge(s_ht, 2 * k + wh + 1)
                    src = ps[:, HB[2 * k + wh], :].rearrange("p (w b y h) -> p h b y w", w=4, b=B, h=2)
                    dst = x_halo[:, k].rearrange("p (b y w) -> p b y w", b=B, y=GRID)[:, :, :, 4 * wh:4 * wh + 4]
                    copy(dst[0:64], src[0:64, k]).then_inc(s_hcopy, 1)
                    to, of = ((1, 0), (0, 1))[k]
                    rows = GRID - 1
                    copy(dst[64:HALO, :, to:to + rows], src[64:HALO, 1 - k, :, of:of + rows]).then_inc(s_hcopy, 1)
            act.wait_ge(s_hcopy, 8)
            act.wait_ge(s_hedge, 2)
            copy(xh[0:HALO, 2 * C:NX], x_halo[0:HALO]).then_inc(s_hhi, 1)
            nc.scalar.activation(sq_halo[0:HALO], x_halo[0:HALO], ACT.Square).then_inc(s_hsq, 1)
            for n, (rem, _, _, col) in enumerate(WGROUPS):
                act.wait_ge(s_watps, n + 1)
                width = 384 if col == 0 else SPAN - 384
                copy(wat[:, 2 if rem else 0, col:col + width], ps[:, WB[n], 0:width]).then_inc(s_wathi, 1)
                if n == 3:
                    copy(b1t[:], ps[:, WB[n], 400:400 + E * FC]).then_inc(s_wathi, 1)
            for half in range(2):
                act.wait_ge(s_merge, C * SHIFTS * (half + 1))
                copy(wlmh[:, half * C:half * C + C, HIGH0:], w_sum[:, half]).then_inc(s_whi, 1)
            act.wait_ge(s_merge, 2 * C * SHIFTS + 2)
            copy(wlmh[0:HALO, 2 * C:NX, HIGH0:], wm_halo[0:HALO]).then_inc(s_whi, 1)
            act.wait_ge(d_stage[0], 16 * STAGE_DMAS)
            split_high_w1(0)
            split_high_w2(0)
            act.wait_ge(s_emb, 2)
            copy(u_part[:], ps[:, UB, 0:D]).then_inc(s_u, 1)

            def high_parts(ps_ready, banks, dst, done):
                act.wait_ge(ps_ready, 1)
                copy(dst[:, 0], ps[:, banks[0], :]).then_inc(done, 1)
                act.wait_ge(ps_ready, 2)
                copy(dst[:, 2], ps[:, banks[1], :]).then_inc(done, 1)

            high_parts(s_nt, (5, 6), nt[:, :, NT0:], s_nhi)
            act.wait_ge(s_qt, 1)
            nc.scalar.activation(qt[:, 0], ps[:, 1, :], ACT.Identity, bias=bqk[:, 0:1]).then_inc(s_qtsb, 1)
            act.wait_ge(s_qt, 2)
            nc.scalar.activation(qt[0:REM, 1], ps[0:REM, 2, :], ACT.Identity,
                                 bias=bqk[0:REM, 1:2]).then_inc(s_qtsb, 1)
            act.wait_ge(s_qt, 3)
            nc.scalar.activation(kts[:, 0], ps[:, 3, 0:S], ACT.Identity, bias=bqk[:, 2:3]).then_inc(s_qtsb, 1)
            nc.scalar.activation(kts[0:REM, 1], ps[0:REM, 3, S:2 * S], ACT.Identity,
                                 bias=bqk[0:REM, 3:4]).then_inc(s_qtsb, 1)
            act.wait_ge(s_vs, 1)
            copy(v_s[:], ps[0:S, 4, 0:D]).then_inc(s_vssb, 1)
            for t in range(TT):
                b0 = 3 * (t % 2)
                act.wait_ge(s_tok, t + 1)
                copy(kv[:, t, 0], ps[:, b0, 0:2 * D]).then_inc(s_kvsb, 1)
                copy(kv[:, t, 1], ps[:, b0 + 1, 0:2 * D]).then_inc(s_kvsb, 1)
                copy(qtok[:, t], ps[:, b0 + 2, 0:D]).then_inc(s_kvsb, 1)
            for t in range(TT):
                act.wait_ge(s_sub, t + 1)
                nc.scalar.activation(pr[:, t], sc[:, t], ACT.Exp, scale=float(HD) ** -0.5).then_inc(s_exp, 1)
                act.wait_ge(s_ptps, t + 1)
                if t >= 2:
                    act.wait_ge(s_pv, t - 1)
                copy(ptsb[:, t % 2], ps[0:WROWS, 7, 0:P]).then_inc(s_pt, 1)
                if t >= 1:
                    act.wait_ge(s_o, t)
                    copy(ao[:, t - 1, D:], ao[:, t - 1, P:D]).then_inc(s_ao, 1)
            act.wait_ge(s_o, TT)
            copy(ao[:, TT - 1, D:], ao[:, TT - 1, P:D]).then_inc(s_ao, 1)
            high_parts(s_at, (0, 1), aot, s_ahi)
            high_parts(s_n2t, (0, 1), n2t, s_n2hi)
            act.wait_ge(s_gsub, 1)
            nc.scalar.activation(ex[:], lg[:], ACT.Exp).then_inc(s_gexp, 1)
            act.wait_ge(s_gtps, 1)
            copy(gt[:], ps[0:E, 4, :].rearrange("e (t p) -> e t p", t=TT)).then_inc(s_gt, 1)

            def pair(i, last):
                for j in range(2 * FC):
                    k, f, slot = i * (2 * FC) + j, j % FC, j // FC
                    act.wait_ge(s_mm1, k + 1)
                    nc.scalar.activation(gf[:, j % NG], ps[:, HPB[j % 4], :], ACT.Gelu,
                                         bias=b1t[:, bass.ds(k, 1)]).then_inc(s_gelu, 1)
                    act.wait_ge(s_gelu, k + 1)
                    copy(g_hi[:, j % NG], gf[:, j % NG]).then_inc(s_ghi, 1)
                    if last and slot == 1:
                        continue
                    if f == 1:
                        act.wait_ge(d_stage[1 - slot], (i + 1 + slot) * (16 * STAGE_DMAS))
                        split_high_w1(1 - slot)
                    if f == 4:
                        split_high_w2(1 - slot)

            with act.Fori(0, E // 2 - 1) as i:
                pair(i, False)
            pair(E // 2 - 1, True)

        @block.tensor
        def _(pe):
            pe.wait_ge(d_gb, 32)
            pe.wait_ge(c_ones, 1)
            pe.wait_ge(c_pool, 3)
            pe.wait_ge(c_shiftm, 2)

            def shift(n):
                return band[:, BAND0 + n:BAND0 + n + P]

            for half in range(2):
                for s in range(SHIFTS):
                    dst = ps[:, 0, (half * SHIFTS + s) * 9:(half * SHIFTS + s) * 9 + 9]
                    mats = [[(half, ident)], [(half, from_right[:])], [(half, from_left[:])],
                            [(half, shift(PATCH))], [(half, shift(-PATCH))]][s]
                    if s == 3 and half == 0:
                        mats = mats + [(1, shift(PATCH - P))]
                    if s == 4 and half == 1:
                        mats = mats + [(0, shift(P - PATCH))]
                    for n, (src, m) in enumerate(mats):
                        mm = nc.tensor.matmul(dst, m, gb_nat[:, src, :, s * C:(s + 1) * C],
                                              start=(n == 0), stop=(n == len(mats) - 1))
            mm.then_inc(s_gbps, 1)
            pe.wait_ge(s_tile, C)
            for g in range(XGROUPS):
                c, wh = g // 2, g % 2
                for w in range(4):
                    wx = 4 * wh + w
                    mm = nc.tensor.transpose(ps[:, XB[g], w * P:(w + 1) * P],
                                             tiles[c][:, wx].rearrange("p q x -> p (q x)"), ident)
                mm.then_inc(s_xt, 1)
            pe.wait_ge(s_gather, 2 * GATHERS)
            for n in range(4):
                k, wh = n // 2, n % 2
                pe.wait_ge(s_xsq, n + 1)
                pe.wait_ge(s_xlo, n + 1)
                for w in range(4):
                    mm = nc.tensor.transpose(ps[0:HALO, HB[n], w * P:(w + 1) * P], halo_g[:, k, 4 * wh + w, :], ident)
                mm.then_inc(s_ht, 1)
            pe.wait_ge(d_small, 16 * SMALL_DMAS)
            for n, (rem, r0, nr, _) in enumerate(WGROUPS):
                if n < 2:
                    pe.wait_ge(s_xsq, 5 + n)
                    pe.wait_ge(s_xlo, 5 + n)
                if n == 2:
                    pe.wait_ge(s_gb, 1)
                if n == 3:
                    pe.wait_ge(s_watlo, 1)
                for r in range(nr):
                    mm = nc.tensor.transpose(ps[:, WB[n], r * WROWS:(r + 1) * WROWS],
                                             wraw[:, r0 + r, rem * P:(rem + 1) * P], ident[0:WROWS, 0:WROWS])
                if r0:
                    mm = nc.tensor.transpose(ps[:, WB[n], 384:384 + E], wraw[0:E, 8, rem * P:(rem + 1) * P],
                                             ident[0:E, 0:E])
                if n == 3:
                    mm = nc.tensor.transpose(ps[:, WB[n], 400:400 + E * FC], b1raw[:], ident[0:E * FC, 0:E * FC])
                mm.then_inc(s_watps, 1)
            pe.wait_ge(s_gb, 1)
            for half in range(2):
                pe.wait_ge(d_wsh[half], 16 * WSH_DMAS[half])
                for s in range(SHIFTS):
                    for c in range(C):
                        nc.tensor.matmul(ps[:, BETAB, 0:D],
                                         gb[:, half, s, C + c:C + c + 1].broadcast_to([P, P]),
                                         wsh[:, s, half, c * D:(c + 1) * D],
                                         start=(half + s + c == 0), stop=False)
            pe.wait_ge(d_halo_w, 16 * (HALO_W_DMAS + GB_HALO_DMAS))
            for k in range(2):
                mm = nc.tensor.matmul(ps[:, BETAB, 0:D], gb_halo[0:HALO, 1, k:k + 1].broadcast_to([HALO, P]),
                                      w_halo[0:HALO, k], start=False, stop=(k == 1))
            mm.then_inc(s_beta, 1)
            pe.wait_ge(s_hcopy, 8)
            pe.wait_ge(s_xlo, XGROUPS)
            pe.wait_ge(s_xhi, XGROUPS)
            pe.wait_ge(s_wathi, 3)
            pe.wait_ge(s_watlo, 3)
            pe.wait_ge(s_m, 4)
            for ch in range(NX):
                if ch % C == 0:
                    pe.wait_ge(s_wlo, ch // C + 1)
                if ch == 2 * C:
                    pe.wait_ge(s_hhi, 1)
                    pe.wait_ge(s_hlo, 1)
                K = P if ch < 2 * C else HALO
                for t in range(TT):
                    tok = slice(t * P, (t + 1) * P)
                    nc.tensor.matmul(ps[:, EMB0 + t, 0:LMH], xh[0:K, ch, tok], wlmh[0:K, ch, :],
                                     start=(ch == 0), stop=False)
                    mm = nc.tensor.matmul(ps[:, EMB0 + t, D:LMH], xl[0:K, ch, tok], wlmh[0:K, ch, D:],
                                          start=False, stop=(ch == NX - 1))
                if ch == NX - 1:
                    mm.then_inc(s_emb, 1)
                mm = nc.tensor.matmul(ps[:, UB, 0:LMH], ones_r[0:K, :], wlmh[0:K, ch, :],
                                      start=(ch == 0), stop=(ch == NX - 1))
            mm.then_inc(s_emb, 1)
            pe.wait_ge(s_sqsum, 5)
            for t in range(TT):
                tok = slice(t * P, (t + 1) * P)
                for n in range(3):
                    lhs = sq[:, 0, n, tok] if n < 2 else sq_halo[0:HALO, 0, tok]
                    rhs = mcol[:, n, :] if n < 2 else ones_f[0:HALO, 0:2]
                    mm = nc.tensor.matmul(ps[:, SQB, 2 * t:2 * t + 2], lhs, rhs, start=(n == 0), stop=(n == 2))
            mm.then_inc(s_sumsq, 1)

            def transposes(src, ready, count, banks, done):
                for r in range(2):
                    for t in range(TT):
                        if r == 0:
                            pe.wait_ge(ready, count(t))
                        mm = nc.tensor.transpose(ps[:, banks[r], t * P:(t + 1) * P], src[:, t, r * P:(r + 1) * P],
                                                 ident)
                    mm.then_inc(done, 1)

            pe.wait_ge(s_watlo, 4)
            pe.wait_ge(s_wathi, 5)
            pe.wait_ge(s_stat, 1)
            transposes(n1, s_n, lambda t: 2 * t + 2, (5, 6), s_nt)

            def nx(cols):
                return lambda a: nt[:, a, cols]

            def wx_(cols):
                return lambda b: wat[:, b, cols]

            every = slice(NT0, NT0 + T)
            pe.wait_ge(s_h, TT)
            pe.wait_ge(s_nhi, 2)
            pe.wait_ge(s_nlo, 2)
            triple(ps[:, 1, :], nx(every), wx_(slice(0, P)), False).then_inc(s_qt, 1)
            triple(ps[:, 2, :], nx(every), wx_(slice(P, 2 * P)), False).then_inc(s_qt, 1)
            strided = slice(NT0, NT0 + T, STRIDE)
            triple(ps[:, 3, 0:S], nx(strided), wx_(slice(D, D + P)), False)
            triple(ps[:, 3, S:2 * S], nx(strided), wx_(slice(D + P, D + 2 * P)), False).then_inc(s_qt, 1)
            triple(ps[0:S, 4, 0:D], nx(strided), wx_(slice(2 * D, 3 * D)), True).then_inc(s_vs, 1)

            def token_major(t):
                b0 = 3 * (t % 2)
                if t == 0:
                    pe.wait_ge(s_urow, 2)
                    pe.wait_ge(s_qtsb, 4)
                if t == 1:
                    pe.wait_ge(s_vssb, 1)
                if t >= 2:
                    pe.wait_ge(s_kvsb, 3 * (t - 1))
                own = slice(NT0 + t * P, NT0 + (t + 1) * P)
                before = slice(NT0 + t * P - 1, NT0 + (t + 1) * P - 1)
                triple(ps[:, b0, 0:2 * D], nx(own), wx_(slice(D, 3 * D)), True)
                triple(ps[:, b0 + 1, 0:2 * D], nx(before), wx_(slice(D, 3 * D)), True)
                triple(ps[:, b0 + 2, 0:D], nx(own), wx_(slice(0, D)), True).then_inc(s_tok, 1)

            token_major(0)
            token_major(1)
            pe.wait_ge(s_vssb, 1)
            for b in range(B):
                bank, off = 6 + (b // 2) % 2, (b % 2) * D
                if b >= 4 and b % 2 == 0:
                    pe.wait_ge(s_vbd, b // 2 - 1)
                mm = nc.tensor.matmul(ps[0:WROWS, bank, off:off + D], key_rep[:, b].rearrange("p j g -> p (j g)"),
                                      v_s[:], start=True, stop=True)
                if b % 2:
                    mm.then_inc(s_vps, 1)
            token_major(2)
            token_major(3)
            pe.wait_ge(s_vbd, 4)
            pe.wait_ge(s_kbd, 2)
            for t in range(TT):
                if t >= 1:
                    pe.wait_ge(s_pvn, t)
                for n in range(2):
                    b = 2 * t + n
                    tok = slice(b * S, (b + 1) * S)
                    rows = slice(n * S, (n + 1) * S)
                    nc.tensor.matmul(ps[rows, 6, 0:64], qt[:, 0, tok],
                                     kbd_a[:, b].rearrange("p g j -> p (g j)"), start=True, stop=True)
                    mm = nc.tensor.matmul(ps[rows, 6, 64:96], qt[0:REM, 1, tok],
                                          kbd_b[0:REM, b].rearrange("p g j -> p (g j)"), start=True, stop=True)
                mm.then_inc(s_sps, 1)
                pe.wait_ge(s_exp, t + 1)
                if t >= 1:
                    pe.wait_ge(s_pt, t)
                nc.tensor.transpose(ps[0:WROWS, 7, 0:P], pr[:, t, 0:NK].rearrange("p j g -> p (j g)"), ident).then_inc(s_ptps, 1)
                pe.wait_ge(s_pt, t + 1)
                for n in range(2):
                    b = 2 * t + n
                    mm = nc.tensor.matmul(ps[n * S:(n + 1) * S, 6, 128:128 + D], ptsb[:, t % 2, n * S:(n + 1) * S],
                                          vbd[0:WROWS, b], start=True, stop=True)
                mm.then_inc(s_pv, 1)
            transposes(ao, s_ao, lambda t: t + 1, (0, 1), s_at)
            pe.wait_ge(s_ahi, 2)
            pe.wait_ge(s_alo, 2)
            for t in range(TT):
                tok = slice(t * P, (t + 1) * P)
                triple(ps[:, 2 + t, 0:D], lambda a: aot[:, a, tok], wx_(slice(OUT0, OUT0 + D)), True)\
                    .then_inc(s_op, 1)
            transposes(n2, s_n, lambda t: 2 * TT + 2 * t + 2, (0, 1), s_n2t)
            pe.wait_ge(s_n2hi, 2)
            pe.wait_ge(s_n2lo, 2)
            for t in range(TT):
                tok = slice(t * P, (t + 1) * P)
                mm = triple(ps[:, 7, t * E:(t + 1) * E], lambda a: n2t[:, a, tok],
                            wx_(slice(ROUT0, ROUT0 + E)), True)
            mm.then_inc(s_rt, 1)

            def layer1(i, j):
                ws = wsplit[j // FC]
                c0 = (j % FC) * P
                if j % FC == 0:
                    pe.wait_ge(s_w1m, i * 2 + j // FC + 1)
                    pe.wait_ge(s_w1lo, i * 2 + j // FC + 1)
                offs = (W1H, W1L, W1R)
                triple(ps[:, HPB[j % 4], :], lambda a: n2t[:, a, :],
                       lambda b: ws[:, offs[b] + c0:offs[b] + c0 + P], False).then_inc(s_mm1, 1)

            def layer2(i, j):
                f, slot = j % FC, j // FC
                w2c = wsplit[slot][:, W2S + f * 2 * D:W2S + (f + 1) * 2 * D]
                if f == 0:
                    pe.wait_ge(s_w2lo, i * 2 + slot + 1)
                pe.wait_ge(s_glo, i * (2 * FC) + j + 1)
                for t in range(TT):
                    tok = slice(t * P, (t + 1) * P)
                    if f == 0:
                        pe.wait_ge(s_acc, (i * 2 + slot) * TT + t + 1)
                    nc.tensor.matmul(ps[:, AB[t], 0:2 * D], g_hi[:, j % NG, tok], w2c,
                                     start=(f == 0), stop=False)
                    nc.tensor.matmul(ps[:, AB[t], D:2 * D], g_lo[:, j % NG, tok], w2c[:, D:],
                                     start=False, stop=(f == FC - 1)).then_inc(s_mm2, 1)

            for j in range(LAG):
                layer1(0, j)
            pe.wait_ge(s_gate, 1)
            for t in range(TT):
                mm = nc.tensor.transpose(ps[0:E, AB[0], t * P:(t + 1) * P], gates[:, t], ident)
            mm.then_inc(s_gtps, 1)
            pe.wait_ge(s_gt, 1)
            for t in range(TT):
                nc.tensor.matmul(ps[:, AB[t], 0:D], gt[:, t], b2sb[:], start=True, stop=True).then_inc(s_b2, 1)

            def steps(i, last):
                for j in range(2 * FC):
                    if j + LAG < 2 * FC:
                        layer1(i, j + LAG)
                    elif not last:
                        layer1(i + 1, j + LAG - 2 * FC)
                    layer2(i, j)

            with pe.Fori(0, E // 2 - 1) as i:
                steps(i, False)
            steps(E // 2 - 1, True)


        @block.vector
        def _(dve):
            def tt(o, a, b, op):
                return nc.vector.tensor_tensor(o, a, b, op)

            dve.wait_ge(s_gbps, 1)
            nc.vector.tensor_copy(gb[:, :, :, :].rearrange("p h s k -> p (h s k)"),
                                  ps[:, 0, 0:2 * SHIFTS * 9]).then_inc(s_gb, 1)
            dve.wait_ge(s_gb, 1)
            nc.vector.tensor_reduce(mcol[:], gb[:, :, :, 6:8].rearrange("p h s k -> p h k s"), AX_X,
                                    ALU.add).then_inc(s_m, 1)
            dve.wait_ge(s_m, 1)
            nc.vector.tensor_copy(wlmh[:, 0:2 * C, D:D + 2].rearrange("p (h c) k -> p h c k", h=2),
                                  mcol[:, :, :].unsqueeze(2).broadcast_to([P, 2, C, 2])).then_inc(s_m, 1)
            dve.wait_ge(c_ones, 4)
            nc.vector.tensor_copy(wlmh[0:HALO, 2 * C:NX, D:D + 2],
                                  ones_f[0:HALO, 0:4].rearrange("p (k n) -> p k n", k=2)).then_inc(s_m, 1)
            nc.vector.tensor_copy(ones_r[:], ones_f[:]).then_inc(s_m, 1)
            dve.wait_ge(d_img, 16 * B)
            dve.wait_ge(c_gath0, 1)
            retile(nc.vector.tensor_copy, 0)
            gather_halo(dve, 1)
            halo_rows = x_halo[64:HALO].rearrange("p k (b y w) -> p k b y w", b=B, y=GRID)
            nc.vector.memset(halo_rows[:, 0, :, 0], 0.0).then_inc(s_hedge, 1)
            nc.vector.memset(halo_rows[:, 1, :, GRID - 1], 0.0).then_inc(s_hedge, 1)
            for g in range(XGROUPS):
                c, wh = g // 2, g % 2
                dve.wait_ge(s_xt, g + 1)
                dve.wait_ge(s_xhi, g + 1)
                dve.wait_ge(s_xsq, g + 1)
                src = ps[:, XB[g], :].rearrange("p (w r k) -> p k r w", w=4, k=2)

                def part(tensor):
                    return tensor[:, c:2 * C:C, :].rearrange("p k (r w) -> p k r w", w=GRID)[
                        :, :, :, 4 * wh:4 * wh + 4]
                tt(part(xl), src, part(xh).bitcast(F32), ALU.subtract).then_inc(s_xlo, 1)
            dve.wait_ge(s_hhi, 1)
            tt(xl[0:HALO, 2 * C:NX], x_halo[0:HALO], xh[0:HALO, 2 * C:NX].bitcast(F32),
               ALU.subtract).then_inc(s_hlo, 1)
            for n, (rem, _, _, col) in enumerate(WGROUPS):
                width = 384 if col == 0 else SPAN - 384
                dve.wait_ge(s_wathi, n + 1 + (n == 3))
                rows = slice(REM, P) if rem else slice(0, P)
                tt(wat[rows, 2 if rem else 1, col:col + width], ps[rows, WB[n], 0:width],
                   wat[rows, 2 if rem else 0, col:col + width].bitcast(F32), ALU.subtract).then_inc(s_watlo, 1)
            for half in range(2):
                dve.wait_ge(d_wsh[half], 16 * WSH_DMAS[half])
                for s in range(SHIFTS):
                    for c in range(C):
                        src = wsh[:, s, half, c * D:(c + 1) * D]
                        dst = w_sum[:, half, c]
                        gam = gb[:, half, s, c:c + 1]
                        if s == 0:
                            ins = nc.vector.tensor_scalar(dst, src, gam, None, ALU.mult)
                        else:
                            dve.wait_ge(s_merge, half * C * SHIFTS + (s - 1) * C + c + 1)
                            ins = nc.vector.scalar_tensor_tensor(out=dst, in0=src, scalar=gam, in1=dst,
                                                                 op0=ALU.mult, op1=ALU.add)
                        ins.then_inc(s_merge, 1)
                if half == 1:
                    dve.wait_ge(d_halo_w, 16 * (HALO_W_DMAS + GB_HALO_DMAS))
                    for k in range(2):
                        nc.vector.tensor_scalar(wm_halo[0:HALO, k], w_halo[0:HALO, k], gb_halo[0:HALO, 0, k:k + 1],
                                                None, ALU.mult).then_inc(s_merge, 1)
                dve.wait_ge(s_whi, half + 1)
                ch = slice(half * C, half * C + C)
                tt(wlmh[:, ch, 0:D], w_sum[:, half], wlmh[:, ch, HIGH0:].bitcast(F32),
                   ALU.subtract).then_inc(s_wlo, 1)
            dve.wait_ge(s_whi, 3)
            ch = slice(2 * C, NX)
            tt(wlmh[0:HALO, ch, 0:D], wm_halo[0:HALO], wlmh[0:HALO, ch, HIGH0:].bitcast(F32),
               ALU.subtract).then_inc(s_wlo, 1)

            n_chain = [0]

            def link(ins):
                n_chain[0] += 1
                ins.then_inc(s_dve, 1)
                dve.wait_ge(s_dve, n_chain[0])

            dve.wait_ge(s_beta, 1)
            dve.wait_ge(d_rows, 16 * 3)
            tt(bias_row[:], ps[:, BETAB, 0:D], tokb_row[:], ALU.add).then_inc(s_urow, 1)
            dve.wait_ge(s_emb, 2)
            link(nc.vector.tensor_scalar(st4[:, 0].unsqueeze(2), ps[:, EMB0:EMB0 + TT, D:D + 1], -1.0 / FEAT, None,
                                         ALU.mult))
            dve.wait_ge(s_u, 1)
            tt(u_sum[:], ps[:, UB, HIGH0:LMH], u_part[:], ALU.add).then_inc(s_urow, 1)
            dve.wait_ge(s_sumsq, 1)
            link(nc.vector.tensor_scalar(st4[:, 1], ps[:, SQB, 0:2 * TT:2], 1.0 / FEAT, None, ALU.mult))
            link(tt(st4[:, 2], st4[:, 0], st4[:, 0], ALU.mult))
            link(tt(st4[:, 3], st4[:, 1], st4[:, 2], ALU.subtract))
            nc.vector.tensor_scalar(st4[:, 4], st4[:, 3], LN_EPS, None, ALU.add).then_inc(s_stat, 1)
            dve.wait_ge(s_urow, 2)
            for t in range(TT):
                nc.vector.scalar_tensor_tensor(out=t_a[:, t], in0=u_sum[:], scalar=st4[:, 0, t:t + 1],
                                               in1=ps[:, EMB0 + t, HIGH0:LMH], op0=ALU.mult,
                                               op1=ALU.add).then_inc(s_t1, 1)
            for t in range(TT):
                dve.wait_ge(s_t1, t + 1)
                tt(t_b[:, t], t_a[:, t], ps[:, EMB0 + t, 0:D], ALU.add).then_inc(s_t2, 1)
            dve.wait_ge(s_pow, 1)
            for t in range(TT):
                dve.wait_ge(s_t2, t + 1)
                nc.vector.scalar_tensor_tensor(out=h[:, t], in0=t_b[:, t], scalar=st4[:, 5, t:t + 1],
                                               in1=bias_row[:], op0=ALU.mult, op1=ALU.add).then_inc(s_h, 1)

            def layer_norm(which, src, ready, dst):
                base = which * TT
                for t in range(TT):
                    dve.wait_ge(ready, t + 1)
                    nc.vector.bn_stats(bn[:, which, t], src[:, t]).then_inc(s_bn, 1)
                for t in range(TT):
                    dve.wait_ge(s_bn, base + t + 1)
                    nc.vector.bn_aggr(mv[:, which, t], bn[:, which, t]).then_inc(s_mv, 1)
                for t in range(TT):
                    dve.wait_ge(s_mv, base + t + 1)
                    nc.vector.tensor_scalar(ve[:, which, t:t + 1], mv[:, which, t, 1:2], LN_EPS, None,
                                            ALU.add).then_inc(s_ve, 1)
                for t in range(TT):
                    dve.wait_ge(s_rs, base + t + 1)
                    for o, a, n in ((0, 0, D), (D, P, REM)):
                        nc.vector.tensor_scalar(dst[:, t, o:o + n], src[:, t, a:a + n], mv[:, which, t, 0:1],
                                                rs[:, which, t:t + 1], ALU.subtract, ALU.mult).then_inc(s_n, 1)

            def low_parts(hi_ready, banks, dst, done):
                for r in range(2):
                    dve.wait_ge(hi_ready, r + 1)
                    tt(dst[:, 2 * r + 1], ps[:, banks[r], :], dst[:, 2 * r].bitcast(F32), ALU.subtract)\
                        .then_inc(done, 1)

            dve.wait_ge(c_mask, E)
            link(nc.vector.tensor_reduce(mask[:, 0:NK], tri_p[:], AX_X, ALU.add))
            link(nc.vector.tensor_reduce(mask[:, NK:], near[:], AX_X, ALU.min))

            layer_norm(0, h, s_h, n1)
            low_parts(s_nhi, (5, 6), nt[:, :, NT0:], s_nlo)
            dve.wait_ge(s_qtsb, 4)
            for kbd, m, n, g in ((kbd_a, P, 0, 8), (kbd_b, REM, 1, 4)):
                tt(kbd[0:m], kts[0:m, n].rearrange("p (b j) -> p b j", b=B).unsqueeze(2).broadcast_to([m, B, g, NK]),
                   head_of_row[0:m, 0:g].unsqueeze(1).unsqueeze(3).broadcast_to([m, B, g, NK]),
                   ALU.mult).then_inc(s_kbd, 1)

            def near_scores(t):
                dve.wait_ge(s_kvsb, 3 * t + 3)
                r = t % 2
                tt(kb[:, r], kv[:, t, :, 0:D], qkvb_row[:, D:2 * D].unsqueeze(1).broadcast_to([P, 2, D]),
                   ALU.add).then_inc(s_kb, 1)
                tt(qb[:, r], qtok[:, t], qkvb_row[:, 0:D], ALU.add).then_inc(s_kb, 1)
                dve.wait_ge(s_kb, 2 * t + 2)
                tt(prod[:, r], kb[:, r], qb[:, r].unsqueeze(1).broadcast_to([P, 2, D]),
                   ALU.mult).then_inc(s_prod, 1)
                dve.wait_ge(s_prod, t + 1)
                nc.vector.tensor_reduce(sc[:, t, NK:],
                                        prod[:, r].rearrange("p s (g d) -> p s g d", d=HD), AX_X,
                                        ALU.add).then_inc(s_near, 1)

            def v_blocks(n):
                dve.wait_ge(s_vps, n + 1)
                tt(vbd[0:WROWS, 2 * n:2 * n + 2].rearrange("p b (g d) -> p b g d", d=HD),
                   ps[0:WROWS, 6 + n % 2, 0:2 * D].rearrange("p (b g d) -> p b g d", b=2, d=HD),
                   head_of_key[0:WROWS, :].unsqueeze(1).unsqueeze(3).broadcast_to([WROWS, 2, HEADS, HD]),
                   ALU.mult).then_inc(s_vbd, 1)

            near_scores(0)
            v_blocks(0)
            v_blocks(1)
            near_scores(1)
            v_blocks(2)
            v_blocks(3)
            near_scores(2)
            near_scores(3)
            for t in range(TT):
                dve.wait_ge(s_sps, t + 1)
                dve.wait_ge(s_near, t + 1)
                m3 = mask[:, :].unsqueeze(2).broadcast_to([P, NS, HEADS])
                tt(sc[:, t, 0:NK], ps[:, 6, 0:HEADS * NK].rearrange("p (g j) -> p j g", j=NK), m3[:, 0:NK],
                   ALU.add).then_inc(s_sc, 1)
                tt(sc[:, t, NK:], sc[:, t, NK:], m3[:, NK:], ALU.add).then_inc(s_sc, 1)
                dve.wait_ge(s_sc, 2 * t + 2)
                nc.vector.tensor_reduce(mx[:, t], sc[:, t].rearrange("p s g -> p g s"), AX_X,
                                        ALU.max).then_inc(s_mx, 1)
                dve.wait_ge(s_mx, t + 1)
                tt(sc[:, t], sc[:, t], mx[:, t].unsqueeze(1).broadcast_to([P, NS, HEADS]),
                   ALU.subtract).then_inc(s_sub, 1)
                dve.wait_ge(s_exp, t + 1)
                link(nc.vector.tensor_reduce(den[:, t], pr[:, t].rearrange("p s g -> p g s"), AX_X, ALU.add))
                nc.vector.reciprocal(rden[:, t], den[:, t]).then_inc(s_rden, 1)
                link(tt(prod[:, t % 2].rearrange("p s (g d) -> p s g d", d=HD),
                        kv[:, t, :, D:].rearrange("p s (g d) -> p s g d", d=HD),
                        pr[:, t, NK:].unsqueeze(3).broadcast_to([P, 2, HEADS, HD]),
                        ALU.mult))
                link(tt(prod[:, t % 2, 0], prod[:, t % 2, 0], prod[:, t % 2, 1], ALU.add))
                dve.wait_ge(s_pv, t + 1)
                tt(prod[:, t % 2, 1], prod[:, t % 2, 0], ps[:, 6, 128:128 + D], ALU.add).then_inc(s_pvn, 1)
                dve.wait_ge(s_pvn, t + 1)
                dve.wait_ge(s_rden, t + 1)
                link(tt(prod[:, t % 2, 0].rearrange("p (g d) -> p g d", d=HD),
                        prod[:, t % 2, 1].rearrange("p (g d) -> p g d", d=HD),
                        rden[:, t].unsqueeze(2).broadcast_to([P, HEADS, HD]), ALU.mult))
                tt(ao[:, t, 0:D], prod[:, t % 2, 0], qkvb_row[:, 2 * D:], ALU.add).then_inc(s_o, 1)
            low_parts(s_ahi, (0, 1), aot, s_alo)
            dve.wait_ge(s_hb, 1)
            for t in range(TT):
                dve.wait_ge(s_op, t + 1)
                tt(h2[:, t], hb[:, t], ps[:, 2 + t, 0:D], ALU.add).then_inc(s_h2, 1)
            layer_norm(1, h2, s_h2, n2)
            low_parts(s_n2hi, (0, 1), n2t, s_n2lo)

            dve.wait_ge(s_rt, 1)
            link(nc.vector.tensor_copy(lg[:, :, :], ps[:, 7, 0:TT * E].rearrange("p (t e) -> p t e", t=TT)))
            link(nc.vector.tensor_reduce(gs[:, 0], lg[:], AX_X, ALU.max))
            tt(lg[:], lg[:], gs[:, 0].unsqueeze(2).broadcast_to([P, TT, E]), ALU.subtract).then_inc(s_gsub, 1)
            dve.wait_ge(s_gexp, 1)
            for t in range(TT):
                nc.vector.max(top[:, t], ex[:, t]).then_inc(s_gtop, 1)
            for t in range(TT):
                dve.wait_ge(s_gtop, t + 1)
                nc.vector.max_index(topi[:, t], top[:, t], ex[:, t]).then_inc(s_gidx, 1)
            dve.wait_ge(s_gidx, TT)
            link(nc.vector.tensor_copy(topf[:], topi[:]))
            iota3 = iota_e[:, :].unsqueeze(1).broadcast_to([P, TT, E])
            for n in range(2):
                link(tt(oh[:, n], iota3, topf[:, :, n:n + 1].broadcast_to([P, TT, E]), ALU.is_equal))
                link(tt(oh[:, n], oh[:, n], top[:, :, n:n + 1].broadcast_to([P, TT, E]), ALU.mult))
            link(tt(oh[:, 0], oh[:, 0], oh[:, 1], ALU.add))
            link(tt(gs[:, 0], top[:, :, 0], top[:, :, 1], ALU.add))
            link(nc.vector.reciprocal(gs[:, 1], gs[:, 0]))
            tt(gates[:], oh[:, 0], gs[:, 1].unsqueeze(2).broadcast_to([P, TT, E]), ALU.mult).then_inc(s_gate, 1)

            for t in range(TT):
                dve.wait_ge(s_b2, t + 1)
                tt(acc[:, t], h2[:, t], ps[:, AB[t], 0:D], ALU.add).then_inc(s_acc, 1)

            def low_hidden(i, j):
                dve.wait_ge(s_ghi, i * (2 * FC) + j + 1)
                tt(g_lo[:, j % NG], gf[:, j % NG], g_hi[:, j % NG].bitcast(F32), ALU.subtract).then_inc(s_glo, 1)

            def add_expert(e):
                for t in range(TT):
                    dve.wait_ge(s_mm2, e * (FC * TT) + (FC - 1) * TT + t + 1)
                    gate = gates[:, t, bass.ds(e, 1)]
                    nc.vector.scalar_tensor_tensor(out=t_a[:, t], in0=ps[:, AB[t], 0:D], scalar=gate,
                                                   in1=acc[:, t], op0=ALU.mult, op1=ALU.add).then_inc(s_evl, 1)
                    dve.wait_ge(s_evl, e * TT + t + 1)
                    nc.vector.scalar_tensor_tensor(out=acc[:, t], in0=ps[:, AB[t], D:2 * D], scalar=gate,
                                                   in1=t_a[:, t], op0=ALU.mult, op1=ALU.add).then_inc(s_acc, 1)

            def pair(i, last):
                for slot in range(2):
                    for j in range(LAG, FC + LAG):
                        if not (last and slot == 1 and j >= FC):
                            low_hidden(i, slot * FC + j)
                    add_expert(i * 2 + slot)

            for j in range(LAG):
                low_hidden(0, j)
            with dve.Fori(0, E // 2 - 1) as i:
                pair(i, False)
            pair(E // 2 - 1, True)


_INS = ["x", "L0_tok_ln_gamma", "L0_tok_ln_beta", "L0_tok_w", "L0_tok_b", "L0_attn_qkv_w", "L0_attn_qkv_b",
        "L0_attn_out_w", "L0_attn_out_b", "L0_ffn_router_w", "L0_ffn_w1", "L0_ffn_b1", "L0_ffn_w2", "L0_ffn_b2"]


def kernel(**inputs):
    import numpy as np
    import concourse.bacc as bacc
    from concourse.bass_utils import run_bass_kernel_spmd

    nc = bacc.Bacc("TRN2", target_bir_lowering=False, num_devices=1)
    arrays, args = {}, []
    for name in _INS:
        a = np.ascontiguousarray(inputs[name])
        arrays[f"in_{name}"] = a
        args.append(nc.dram_tensor(f"in_{name}", a.shape, mybir.dt.from_np(a.dtype), kind="ExternalInput").ap())
    b = inputs["x"].shape[0]
    d = inputs["L0_tok_w"].shape[1]
    s = (inputs["x"].shape[2] // PATCH) ** 2
    out = nc.dram_tensor("out", (b, s, d), F32, kind="ExternalOutput").ap()
    vit_tower(nc, *args, out)
    r = run_bass_kernel_spmd(nc, [arrays], core_ids=[0])
    return r.results[0]["out"]
```

```python
from contextlib import ExitStack

import concourse.bass as bass
from concourse import mybir

F32 = mybir.dt.float32
F32R = mybir.dt.float32r
U32 = mybir.dt.uint32
ALU = mybir.AluOpType
ACT = mybir.ActivationFunctionType
AX_X = mybir.AxisListType.X

P = 128
PATCH = 16
LN_EPS = 1e-5
HEADS = 12
STRIDE = 8
NEG = -1e30


def vit_tower(nc, x, tok_gamma, tok_beta, tok_w, tok_b, qkv_w, qkv_b, out_w, out_b,
              router_w, w1, b1, w2, b2, out):
    B, C, IMG, _ = x.shape
    D = tok_w.shape[1]
    E, _, F = w1.shape
    GRID = IMG // PATCH
    S = GRID * GRID
    T = B * S
    TT = T // P
    HD = D // HEADS
    NK = S // STRIDE
    SHIFTS = 5
    FEAT = SHIFTS * C * PATCH * PATCH
    QR = PATCH // 2
    REM = D - P
    FC = F // P
    SPAN = 3 * D + D + E
    OUT0, ROUT0 = 3 * D, 4 * D
    WROWS = 96
    HALO = 112
    NX = 8
    LMH = 2 * D + 2
    HIGH0 = D + 2
    STAGE = 2 * F + FC * D
    assert (D, HD, S, T, E, F) == (192, 16, 64, 512, 8, 768)

    with ExitStack() as ctx:
        def sb(name, shape, dt=F32):
            return ctx.enter_context(nc.sbuf_tensor(name, shape, dt))

        def sem(name):
            return ctx.enter_context(nc.semaphore(name))

        ps = ctx.enter_context(nc.psum_tensor("ps", [P, 8, 512], F32))

        BAND0 = 160
        band = sb("band", [P, 432])
        from_right = sb("from_right", [P, P])
        from_left = sb("from_left", [P, P])
        ident = band[:, BAND0:BAND0 + P]
        ones_f = sb("ones_f", [P, P])
        ones_r = sb("ones_r", [P, P], F32R)
        neg_half = sb("neg_half", [P, 4])
        group = sb("group", [P, 16])
        group8 = sb("group8", [P, 8])
        tri = sb("tri", [P, NK, 8])
        tri_p = sb("tri_p", [P, NK, 8])
        near = sb("near", [P, 2, 16])
        mask = sb("mask", [P, NK + 2])
        head_of_row = sb("head_of_row", [P, 8])
        head_of_key = sb("head_of_key", [P, HEADS])
        key_rep = sb("key_rep", [S, B, NK, HEADS])
        v_s = sb("v_s", [S, D])
        iota_e = sb("iota_e", [P, E])

        early = sb("early", [P, C * QR * IMG + 2 * GRID * HALO])
        img = early[:, 0:C * QR * IMG].rearrange("p (c q w) -> p c q w", c=C, q=QR)
        halo_g = early[:, C * QR * IMG:].rearrange("p (k w r) -> p k w r", k=2, w=GRID)
        gb_nat = sb("gb_nat", [P, 2, 3, SHIFTS * C])
        gb = sb("gb", [P, 2, SHIFTS, 3 * C])
        gb_halo = sb("gb_halo", [P, 2, 2])
        shifted = sb("shifted", [P, SHIFTS * 2 * C * D])
        wsh = shifted[:, :].rearrange("p (s h n) -> p s h n", s=SHIFTS, h=2)
        merge = sb("merge", [P, (2 * C + 4) * D])
        w_sum = merge[:, 0:2 * C * D].rearrange("p (h c n) -> p h c n", h=2, c=C)
        w_halo = merge[:, 2 * C * D:(2 * C + 2) * D].rearrange("p (k n) -> p k n", k=2)
        wm_halo = merge[:, (2 * C + 2) * D:].rearrange("p (k n) -> p k n", k=2)
        big_r = sb("big_r", [P, 2 * NX * T], F32R)
        xh = big_r[:, 0:NX * T].rearrange("p (k t) -> p k t", k=NX)
        xl = big_r[:, NX * T:].rearrange("p (k t) -> p k t", k=NX)
        sq = sb("sq", [P, 3, 2, T])
        halo = sb("halo", [P, 4 * T])
        x_halo = halo[:, 0:2 * T].rearrange("p (k t) -> p k t", k=2)
        sq_halo = halo[:, 2 * T:].rearrange("p (k t) -> p k t", k=2)
        W1H, W1L, W1R, W2S = 0, F, 2 * F, 3 * F
        wsplit = [sb(f"wsplit{i}", [P, 3 * F + FC * 2 * D], F32R) for i in range(2)]
        wlmh = wsplit[1][:, 0:NX * LMH].rearrange("p (k n) -> p k n", k=NX)
        stage0 = sb("stage0", [P, STAGE])
        staged = [stage0[:, :], early[:, 0:STAGE]]
        mcol = sb("mcol", [P, 2, 2])
        u_part = sb("u_part", [P, D])
        u_sum = sb("u_sum", [P, D])
        bias_row = sb("bias_row", [P, D])
        tokb_row = sb("tokb_row", [P, D])
        qkvb_row = sb("qkvb_row", [P, 3 * D])
        outb_row = sb("outb_row", [P, D])
        st4 = sb("st4", [P, 6, TT])
        h_raw = sb("h", [P, TT * D])
        h = h_raw[:, :].rearrange("p (t d) -> p t d", t=TT)
        PICK0, PICKW = HALO - QR, 2 * HALO - QR
        pick_left, pick_right, pick_last = (h_raw[:, n * PICKW:(n + 1) * PICKW] for n in range(3))
        t_a = sb("t_a", [P, TT, D])

        raw = sb("raw", [P, 9 * 2 * P])
        wraw = raw[0:WROWS, :].rearrange("p (n d) -> p n d", n=9)
        hb = raw[:, 0:TT * D].rearrange("p (t d) -> p t d", t=TT)
        wat = sb("wat", [P, 3, SPAN], F32R)
        b1raw = sb("b1raw", [E * FC, P])
        b1t = sb("b1t", [P, E * FC])
        b2sb = sb("b2sb", [E, D])
        bqk = sb("bqk", [P, 4])

        bn = sb("bn", [P, 2, TT, 6])
        mv = sb("mv", [P, 2, TT, 2])
        ve = sb("ve", [P, 2, TT])
        rs = sb("rs", [P, 2, TT])
        norm = sb("norm", [P, TT * 2 * P])
        n1 = n2 = norm[:, :].rearrange("p (t n) -> p t n", t=TT)
        tiles = [a.rearrange("p (w q x) -> p w q x", w=GRID, q=QR)
                 for a in (stage0[:, 0:TT * 2 * P], stage0[:, TT * 2 * P:2 * TT * 2 * P], norm[:, :])]
        NT0 = 2
        nt = sb("nt", [P, 4, NT0 + T], F32R)

        kv = shifted[:, 0:TT * 4 * D].rearrange("p (t s n) -> p t s n", t=TT, s=2)
        vbd = shifted[:, TT * 4 * D:TT * 4 * D + B * D].rearrange("p (b n) -> p b n", b=B)
        qtok = shifted[:, TT * 4 * D + B * D:TT * 4 * D + B * D + TT * D].rearrange("p (t n) -> p t n", t=TT)
        kb = halo[:, 0:4 * D].rearrange("p (r s n) -> p r s n", r=2, s=2)
        prod = halo[:, 4 * D:8 * D].rearrange("p (r s n) -> p r s n", r=2, s=2)
        qb = halo[:, 8 * D:10 * D].rearrange("p (r n) -> p r n", r=2)
        qt = sq[:, 0, :, :]
        kts = sq[:, 1, 0, 0:2 * S].rearrange("p (k n) -> p k n", k=2)
        kbd_a = sq[:, 1, 1, :].rearrange("p (b g j) -> p b g j", b=B, g=8)
        kbd_b = sq[:, 2, 0, 0:B * 4 * NK].rearrange("p (b g j) -> p b g j", b=B, g=4)
        NS = NK + 2
        sc = sb("sc", [P, TT, NS, HEADS])
        pr = sb("pr", [P, TT, NS, HEADS])
        mx = sb("mx", [P, TT, HEADS])
        den = sb("den", [P, TT, HEADS])
        rden = sb("rden", [P, TT, HEADS])
        ptsb = sb("ptsb", [WROWS, 2, P])
        ao = merge[:, 0:TT * 2 * P].rearrange("p (t n) -> p t n", t=TT)
        aot = big_r[:, 0:4 * T].rearrange("p (k t) -> p k t", k=4)
        h2 = merge[:, TT * 2 * P:TT * (2 * P + D)].rearrange("p (t n) -> p t n", t=TT)
        acc = h2

        n2t = big_r[:, 4 * T:8 * T].rearrange("p (k t) -> p k t", k=4)
        g_hi = big_r[:, 8 * T:12 * T].rearrange("p (k t) -> p k t", k=4)
        g_lo = big_r[:, 12 * T:16 * T].rearrange("p (k t) -> p k t", k=4)
        NG = 4
        gf = early[:, STAGE:STAGE + NG * T].rearrange("p (k t) -> p k t", k=NG)
        lg = sb("lg", [P, TT, E])
        ex = sb("ex", [P, TT, E])
        top = sb("top", [P, TT, 8])
        topi = sb("topi", [P, TT, 8], U32)
        topf = sb("topf", [P, TT, 8])
        oh = sb("oh", [P, 2, TT, E])
        gs = sb("gs", [P, 2, TT])
        gates = sb("gates", [P, TT, E])
        gt = halo[0:E, 0:T].rearrange("e (t p) -> e t p", t=TT)
        lgt = halo[0:E, T:2 * T]

        d_img, d_gb, d_halo_w = sem("d_img"), sem("d_gb"), sem("d_halo_w")
        d_wsh = [[sem(f"d_wsh{half}_{s}") for s in range(SHIFTS)] for half in range(2)]
        d_bqk, c_edge, c_pick, s_wdup = sem("d_bqk"), sem("c_edge"), sem("c_pick"), sem("s_wdup")
        d_rows, d_small = sem("d_rows"), sem("d_small")
        d_stage = [sem("d_stage0"), sem("d_stage1")]
        d_out = sem("d_out")
        c_halo0, c_gath0, c_pool, c_band, c_shiftm, c_ones, c_mask = (
            sem(n) for n in ("c_halo0", "c_gath0", "c_pool", "c_band", "c_shiftm", "c_ones", "c_mask"))
        s_gbps, s_gb, s_m, s_gather = sem("s_gbps"), sem("s_gb"), sem("s_m"), sem("s_gather")
        s_xt, s_xhi, s_xlo, s_xsq, s_sqsum = (sem(n) for n in ("s_xt", "s_xhi", "s_xlo", "s_xsq", "s_sqsum"))
        s_ht, s_hcopy, s_hedge, s_hhi, s_hlo, s_hsq = (
            sem(n) for n in ("s_ht", "s_hcopy", "s_hedge", "s_hhi", "s_hlo", "s_hsq"))
        s_merge, s_whi, s_wlo = sem("s_merge"), sem("s_whi"), sem("s_wlo")
        s_watps, s_wathi, s_watlo = sem("s_watps"), sem("s_wathi"), sem("s_watlo")
        s_beta, s_emb, s_sumsq = sem("s_beta"), sem("s_emb"), sem("s_sumsq")
        s_stat, s_pow, s_u, s_urow = sem("s_stat"), sem("s_pow"), sem("s_u"), sem("s_urow")
        s_t1, s_t2, s_h = sem("s_t1"), sem("s_t2"), sem("s_h")
        s_bn, s_mv, s_ve, s_rs, s_n = (sem(n) for n in ("s_bn", "s_mv", "s_ve", "s_rs", "s_n"))
        s_hb, s_tile, s_vs, s_vssb = sem("s_hb"), sem("s_tile"), sem("s_vs"), sem("s_vssb")
        s_nt, s_nhi, s_nlo = sem("s_nt"), sem("s_nhi"), sem("s_nlo")
        s_qt, s_qtsb, s_kbd = sem("s_qt"), sem("s_qtsb"), sem("s_kbd")
        s_vps, s_vbd = sem("s_vps"), sem("s_vbd")
        s_tok, s_kvsb = sem("s_tok"), sem("s_kvsb")
        s_kb, s_prod, s_near, s_sps, s_sc, s_mx, s_sub, s_exp = (
            sem(n) for n in ("s_kb", "s_prod", "s_near", "s_sps", "s_sc", "s_mx", "s_sub", "s_exp"))
        s_rden, s_ptps, s_pt, s_pv, s_pvn, s_o = (
            sem(n) for n in ("s_rden", "s_ptps", "s_pt", "s_pv", "s_pvn", "s_o"))
        s_ao = sem("s_ao")
        s_at, s_ahi, s_alo, s_op, s_h2 = (sem(n) for n in ("s_at", "s_ahi", "s_alo", "s_op", "s_h2"))
        s_n2t, s_n2hi, s_n2lo = sem("s_n2t"), sem("s_n2hi"), sem("s_n2lo")
        s_rt, s_gmax, s_gsub, s_gexp, s_gtop, s_gidx, s_goh, s_gden, s_gate = (
            sem(n) for n in ("s_rt", "s_gmax", "s_gsub", "s_gexp", "s_gtop", "s_gidx", "s_goh", "s_gden", "s_gate"))
        s_gtps, s_gt, s_b2, s_acc0 = sem("s_gtps"), sem("s_gt"), sem("s_b2"), sem("s_acc0")
        s_mm1, s_gelu, s_ghi, s_glo, s_mm2 = (sem(n) for n in ("s_mm1", "s_gelu", "s_ghi", "s_glo", "s_mm2"))
        s_w1hi, s_w2hi, s_w1lo, s_w2lo = (sem(n) for n in ("s_w1hi", "s_w2hi", "s_w1lo", "s_w2lo"))
        s_acc = sem("s_acc")
        s_rl, s_rlsb = sem("s_rl"), sem("s_rlsb")
        s_b2add = sem("s_b2add")
        s_evl, s_w1m, s_dve = sem("s_evl"), sem("s_w1m"), sem("s_dve")

        block = ctx.enter_context(nc.Block())

        XB = [1, 2, 3, 4, 5, 6]
        HB = [1, 2, 3, 4]
        WB = [5, 6, 5, 6]
        EMB0, SQB, UB, BETAB = 1, 7, 0, 7
        SQ0 = 256
        GBH0 = 96
        LAG = 3
        HPB = [0, 1, 2, 3]
        GTB = HPB[(2 * FC - LAG - 1) % 4]
        AB = [4, 5, 6, 7]
        WGROUPS = [(0, 0, 4, 0), (1, 0, 4, 0), (0, 4, 4, 384), (1, 4, 4, 384)]
        XGROUPS = 2 * C

        def gather_halo(eng, k):
            px = img.rearrange("p c q (w x) -> p w c q x", x=PATCH)
            g = nc.vector
            q_edge = QR - 1 if k == 0 else 0
            g.tensor_copy(halo_g[:, k, 1:GRID, 0:3 * QR].rearrange("p w (c q) -> p w c q", c=C),
                          px[:, 0:GRID - 1, :, :, PATCH - 1]).then_inc(s_gather, 1)
            g.tensor_copy(halo_g[:, k, 0:GRID - 1, 3 * QR:6 * QR].rearrange("p w (c q) -> p w c q", c=C),
                          px[:, 1:GRID, :, :, 0]).then_inc(s_gather, 1)
            g.tensor_copy(halo_g[:, k, :, 64:HALO].rearrange("p w (c x) -> p w c x", c=C),
                          px[:, :, :, q_edge, :]).then_inc(s_gather, 1)
        GATHERS = 3

        def retile(copy_op, c):
            copy_op(tiles[c], img[:, c].rearrange("p q (w x) -> p w q x", x=PATCH)).then_inc(s_tile, 1)

        def split_low(pool, e, slot):
            st, ws = staged[slot], wsplit[slot]
            pool.wait_ge(s_w1hi, e * 2 + 1)
            nc.gpsimd.tensor_tensor(ws[:, W1L:W1L + F], st[:, 0:F], ws[:, W1H:W1H + F].bitcast(F32),
                                    ALU.subtract).then_inc(s_w1m, 1)
            pool.wait_ge(s_w1m, e + 1)
            pool.wait_ge(s_w1hi, e * 2 + 2)
            nc.gpsimd.tensor_tensor(ws[REM:P, W1R:W1R + F], st[REM:P, F:2 * F],
                                    ws[REM:P, W1R:W1R + F].bitcast(F32), ALU.subtract).then_inc(s_w1lo, 1)
            pool.wait_ge(s_w1lo, e + 1)
            pool.wait_ge(s_w2hi, e * 2 + 2)
            w2v = ws[:, W2S:].rearrange("p (c n) -> p c n", c=FC)
            nc.gpsimd.tensor_tensor(w2v[:, :, 0:D], st[:, 2 * F:].rearrange("p (c n) -> p c n", c=FC),
                                    w2v[:, :, D:].bitcast(F32), ALU.subtract).then_inc(s_w2lo, 1)

        def copy(o, a):
            return nc.scalar.activation(o, a, ACT.Copy)

        def split_high(slot, part):
            st, ws = staged[slot], wsplit[slot]
            if part < 2:
                to = (W1H, W1R)[part]
                copy(ws[:, to:to + F], st[:, part * F:(part + 1) * F]).then_inc(s_w1hi, 1)
            else:
                c = slice((part - 2) * FC // 2, (part - 1) * FC // 2)
                copy(ws[:, W2S:].rearrange("p (c n) -> p c n", c=FC)[:, c, D:],
                     st[:, 2 * F:].rearrange("p (c n) -> p c n", c=FC)[:, c]).then_inc(s_w2hi, 1)

        def small_dmas(sp):
            def every(ap):
                return ap.unsqueeze(0).broadcast_to([P, ap.shape[0]])
            sp.dma_start(wraw[:, 0:6, 0:D], qkv_w.rearrange("(n p) d -> p n d", p=WROWS)).then_inc(d_small, 16)
            sp.dma_start(wraw[:, 6:8, 0:D], out_w.rearrange("(n p) d -> p n d", p=WROWS)).then_inc(d_small, 16)
            sp.dma_start(wraw[0:E, 8, 0:D], router_w).then_inc(d_small, 16)
            sp.dma_start(b1raw[:], b1.rearrange("e (c p) -> (e c) p", p=P)).then_inc(d_small, 16)
            sp.dma_start(tokb_row[:], every(tok_b)).then_inc(d_rows, 16)
            sp.dma_start(qkvb_row[:], every(qkv_b)).then_inc(d_rows, 16)
            sp.dma_start(outb_row[:], every(out_b)).then_inc(d_rows, 16)
            for n, (o, m) in enumerate(((0, P), (P, REM), (D, P), (D + P, REM))):
                sp.dma_start(bqk[0:m, n:n + 1], qkv_b[o:o + m].unsqueeze(1),
                             allow_slow_non_contiguous=True).then_inc(d_bqk, 16)
            sp.dma_start(b2sb[:], b2).then_inc(d_bqk, 16)
        SMALL_DMAS, BQK_DMAS = 4, 5

        def triple(dst, x_of, w_of, x_stationary):
            order = ((0, 0), (0, 1), (1, 0), (2, 2), (3, 2)) if x_stationary else \
                ((0, 0), (1, 0), (0, 1), (2, 2), (3, 2))
            for n, (a, b) in enumerate(order):
                lhs, rhs = (x_of(a), w_of(b)) if x_stationary else (w_of(b), x_of(a))
                mm = nc.tensor.matmul(dst, lhs, rhs, start=(n == 0), stop=(n == 4))
            return mm

        HALO_W_DMAS = 3 * C

        def load_expert(sp, e, slot):
            st = staged[slot]
            w1e, w2e = w1[bass.ds(e, 1)], w2[bass.ds(e, 1)]
            sp.dma_start(st[:, 0:F], w1e[:, 0:P, :].rearrange("o p f -> (o p) f")).then_inc(d_stage[slot], 16)
            for half in range(2):
                sp.dma_start(st[half * REM:half * REM + REM, F:2 * F],
                             w1e[:, P:D, :].rearrange("o p f -> (o p) f")).then_inc(d_stage[slot], 16)
            sp.dma_start(st[:, 2 * F:].rearrange("p (c n) -> p c n", c=FC),
                         w2e.rearrange("o (c p) n -> (o p) c n", p=P)).then_inc(d_stage[slot], 16)
        STAGE_DMAS = 4

        @block.sync
        def _(sp):
            wv = tok_w.rearrange("(p k) e -> p (k e)", k=SHIFTS * C)
            for b in range(B):
                sp.dma_start(img[b * 2 * GRID:(b + 1) * 2 * GRID],
                             x[b].rearrange("c (r q) w -> r c q w", q=QR)).then_inc(d_img, 16)
            OFF = [0, 1, -1, PATCH, -PATCH]
            sp.wait_ge(c_edge, 4)
            for half in range(2):
                for s in range(SHIFTS):
                    lo = half * P + OFF[s]
                    first, last = max(0, lo), min(2 * P, lo + P)
                    sp.dma_start(wsh[first - lo:last - lo, s, half],
                                 wv[first:last, s * C * D:(s + 1) * C * D]).then_inc(d_wsh[half][s], 16)
            sp.wait_ge(c_halo0, 1)
            pv = tok_w.rearrange("(k y x s c) e -> y x s c k e", k=2, x=PATCH, s=SHIFTS, c=C)
            last_row = ((PATCH - 1) * PATCH * SHIFTS + 1) * C
            for c in range(C):
                sp.dma_start(w_halo[QR * c:QR * (c + 1)], pv[:, 0, 1, c]).then_inc(d_halo_w, 16)
                sp.dma_start(w_halo[QR * (C + c):QR * (C + c + 1)], pv[:, PATCH - 1, 2, c]).then_inc(d_halo_w, 16)
                above_below = bass.AP(tensor=tok_w.tensor, offset=(3 * C + c) * D,
                                      ap=[[SHIFTS * C * D, PATCH], [last_row * D, 2], [1, D]])
                sp.dma_start(w_halo[64 + PATCH * c:64 + PATCH * (c + 1)], above_below).then_inc(d_halo_w, 16)
            small_dmas(sp)
            sp.wait_ge(s_xt, XGROUPS)
            load_expert(sp, 0, 0)
            sp.wait_ge(s_ht, 4)
            load_expert(sp, 1, 1)
            with sp.Fori(1, E // 2) as i:
                for slot in range(2):
                    sp.wait_ge(s_w1lo, i * 2 + slot - 1)
                    sp.wait_ge(s_w2lo, i * 2 + slot - 1)
                    load_expert(sp, i * 2 + slot, slot)
            for t in range(TT):
                sp.wait_ge(s_acc, E * TT + t + 1)
                sp.dma_start(out[t * 2:t * 2 + 2].rearrange("b s d -> (b s) d"),
                             acc[:, t]).then_inc(d_out, 16)
            sp.wait_ge(d_out, 16 * TT)


        @block.gpsimd
        def _(pool):
            nc.gpsimd.memset(gb_nat[:, :, 2, :], 1.0).then_inc(c_ones, 1)
            step = [0]

            def then(ins):
                step[0] += 1
                ins.then_inc(c_pool, 1)
                pool.wait_ge(c_pool, step[0])

            then(nc.gpsimd.memset(band[:], 0.0))
            then(nc.gpsimd.affine_select(out=band[:], in_=band[:], compare_op=ALU.not_equal, fill=1.0,
                                         base=BAND0, pattern=[[-1, 432]], channel_multiplier=1))
            nc.gpsimd.tensor_copy(from_right[:], band[:, BAND0 + 1:BAND0 + 1 + P]).then_inc(c_band, 1)
            then(nc.gpsimd.tensor_copy(from_left[:], band[:, BAND0 - 1:BAND0 - 1 + P]))
            pool.wait_ge(c_band, 1)
            nc.gpsimd.memset(from_right[:, :].rearrange("p (q x) -> p q x", x=PATCH)[:, :, PATCH - 1:PATCH],
                             0.0).then_inc(c_shiftm, 1)
            nc.gpsimd.memset(from_left[:, :].rearrange("p (q x) -> p q x", x=PATCH)[:, :, 0:1],
                             0.0).then_inc(c_shiftm, 1)
            then(nc.gpsimd.memset(h_raw[:, 0:3 * PICKW], 0.0))
            for pick, base, per in ((pick_left, PICK0 * PATCH, PATCH),
                                    (pick_right, PICK0 * PATCH - (PATCH - 1), PATCH),
                                    (pick_last, PICK0 - (P - PATCH), 1)):
                nc.gpsimd.affine_select(out=pick, in_=pick, compare_op=ALU.not_equal, fill=1.0, base=base,
                                        pattern=[[-per, PICKW]], channel_multiplier=1).then_inc(c_pick, 1)
            pool.wait_ge(c_pick, 3)
            nc.gpsimd.memset(pick_last[:, 0:PICK0], 0.0).then_inc(c_pick, 1)
            nc.gpsimd.memset(halo_g, 0.0).then_inc(c_gath0, 1)
            nc.gpsimd.memset(ones_f[:], 1.0).then_inc(c_ones, 1)
            nc.gpsimd.memset(neg_half[:], -0.5).then_inc(c_ones, 1)
            nc.gpsimd.memset(nt[:, :, 0:NT0].bitcast(F32), 0.0).then_inc(c_ones, 1)
            for tile, n, w in ((head_of_row, 8, HD),):
                then(nc.gpsimd.memset(tile[:], 1.0))
                then(nc.gpsimd.affine_select(out=tile[:], in_=tile[:], compare_op=ALU.is_ge, fill=0.0,
                                             base=0, pattern=[[-w, n]], channel_multiplier=1))
                then(nc.gpsimd.affine_select(out=tile[:], in_=tile[:], compare_op=ALU.is_ge, fill=0.0,
                                             base=w - 1, pattern=[[w, n]], channel_multiplier=-1))
            then(nc.gpsimd.memset(head_of_key[:], 0.0))
            for j in range(NK):
                then(nc.gpsimd.affine_select(out=head_of_key[:], in_=head_of_key[:], compare_op=ALU.not_equal,
                                             fill=1.0, base=-HEADS * j, pattern=[[-1, HEADS]],
                                             channel_multiplier=1))
            then(nc.gpsimd.memset(key_rep[:], 0.0))
            then(nc.gpsimd.affine_select(out=key_rep[:], in_=key_rep[:], compare_op=ALU.not_equal, fill=1.0,
                                         base=0, pattern=[[-NK, B], [-1, NK], [0, HEADS]],
                                         channel_multiplier=1))
            then(nc.gpsimd.memset(group[:], 1.0))
            then(nc.gpsimd.affine_select(out=group[:], in_=group[:], compare_op=ALU.is_ge, fill=0.0,
                                         base=0, pattern=[[-8, 16]], channel_multiplier=1))
            then(nc.gpsimd.affine_select(out=group[:], in_=group[:], compare_op=ALU.is_ge, fill=0.0,
                                         base=7, pattern=[[8, 16]], channel_multiplier=-1))
            then(nc.gpsimd.tensor_tensor(group8[:], group[:, 0:8], group[:, 8:16], ALU.add))
            then(nc.gpsimd.memset(tri[:], 0.0))
            then(nc.gpsimd.affine_select(out=tri[:], in_=tri[:], compare_op=ALU.is_ge, fill=NEG,
                                         base=0, pattern=[[-1, NK], [1, 8]], channel_multiplier=0))
            then(nc.gpsimd.tensor_tensor(tri_p[:], tri[:],
                                         group8[:, :].unsqueeze(1).broadcast_to([P, NK, 8]), ALU.mult))
            then(nc.gpsimd.memset(near[:], 0.0))
            then(nc.gpsimd.affine_select(out=near[:], in_=near[:], compare_op=ALU.not_equal, fill=NEG,
                                         base=0, pattern=[[-1, 2], [-8, 16]], channel_multiplier=1))
            then(nc.gpsimd.affine_select(out=near[:, 1], in_=near[:, 1], compare_op=ALU.not_equal, fill=NEG,
                                         base=0, pattern=[[-S, 16]], channel_multiplier=1))
            for e in range(E):
                nc.gpsimd.memset(iota_e[:, e:e + 1], float(e)).then_inc(c_mask, 1)

            for c in range(1, C):
                pool.wait_ge(s_xsq, 2 * c + 2)
                for half in range(2):
                    if c > 1:
                        pool.wait_ge(s_sqsum, 2 * (c - 2) + half + 1)
                    nc.gpsimd.tensor_tensor(sq[:, 0, half], sq[:, 0, half], sq[:, c, half],
                                            ALU.add).then_inc(s_sqsum, 1)
            pool.wait_ge(s_hsq, 1)
            nc.gpsimd.tensor_tensor(sq_halo[0:HALO, 0], sq_halo[0:HALO, 0], sq_halo[0:HALO, 1],
                                    ALU.add).then_inc(s_sqsum, 1)
            pool.wait_ge(c_ones, 4)
            pool.wait_ge(s_stat, 1)
            nc.gpsimd.tensor_tensor(st4[:, 5], st4[:, 4], neg_half[:], ALU.pow).then_inc(s_pow, 1)
            for t in range(TT):
                pool.wait_ge(s_ve, t + 1)
                nc.gpsimd.tensor_tensor(rs[:, 0, t:t + 1], ve[:, 0, t:t + 1], neg_half[:, 0:1],
                                        ALU.pow).then_inc(s_rs, 1)
            split_low(pool, 0, 0)
            pool.wait_ge(d_rows, 16 * 3)
            pool.wait_ge(s_h, TT)
            pool.wait_ge(s_watps, 4)
            nc.gpsimd.tensor_tensor(hb[:], h[:], outb_row[:, :].unsqueeze(1).broadcast_to([P, TT, D]),
                                    ALU.add).then_inc(s_hb, 1)
            for t in range(TT):
                pool.wait_ge(s_ve, TT + t + 1)
                nc.gpsimd.tensor_tensor(rs[:, 1, t:t + 1], ve[:, 1, t:t + 1], neg_half[:, 0:1],
                                        ALU.pow).then_inc(s_rs, 1)
            split_low(pool, 1, 1)
            with pool.Fori(1, E // 2) as i:
                for slot in range(2):
                    split_low(pool, i * 2 + slot, slot)

        @block.scalar
        def _(act):
            gv = tok_gamma.rearrange("(h p k) -> p h k", h=2, k=SHIFTS * C)
            bv = tok_beta.rearrange("(h p k) -> p h k", h=2, k=SHIFTS * C)
            act.dma_start(gb_nat[:, :, 0, :], gv).then_inc(d_gb, 16)
            act.dma_start(gb_nat[:, :, 1, :], bv).then_inc(d_gb, 16)
            act.wait_ge(d_img, 16 * B)
            retile(copy, 1)
            for g in range(XGROUPS):
                c, wh = g // 2, g % 2
                act.wait_ge(s_xt, g + 1)
                src = ps[:, XB[g], :].rearrange("p (w r k) -> p k r w", w=4, k=2)
                for out_t, s_done in ((xh, s_xhi), (sq, s_xsq)):
                    if out_t is xh:
                        dst = xh[:, c:2 * C:C, :]
                    else:
                        dst = sq[:, c]
                    dst = dst.rearrange("p k (r w) -> p k r w", w=GRID)[:, :, :, 4 * wh:4 * wh + 4]
                    nc.scalar.activation(dst, src, ACT.Copy if out_t is xh else ACT.Square).then_inc(s_done, 1)
            for k in range(2):
                for wh in range(2):
                    act.wait_ge(s_ht, 2 * k + wh + 1)
                    src = ps[:, HB[2 * k + wh], :].rearrange("p (w b y h) -> p h b y w", w=4, b=B, h=2)
                    dst = x_halo[:, k].rearrange("p (b y w) -> p b y w", b=B, y=GRID)[:, :, :, 4 * wh:4 * wh + 4]
                    copy(dst[0:64], src[0:64, k]).then_inc(s_hcopy, 1)
                    to, of = ((1, 0), (0, 1))[k]
                    rows = GRID - 1
                    copy(dst[64:HALO, :, to:to + rows], src[64:HALO, 1 - k, :, of:of + rows]).then_inc(s_hcopy, 1)
            act.wait_ge(s_hcopy, 8)
            act.wait_ge(s_hedge, 2)
            copy(xh[0:HALO, 2 * C:NX], x_halo[0:HALO]).then_inc(s_hhi, 1)
            nc.scalar.activation(sq_halo[0:HALO], x_halo[0:HALO], ACT.Square).then_inc(s_hsq, 1)
            for half in range(2):
                act.wait_ge(s_merge, C * SHIFTS * (half + 1))
                copy(wlmh[:, half * C:half * C + C, HIGH0:], w_sum[:, half]).then_inc(s_whi, 1)
            act.wait_ge(s_merge, 2 * C * SHIFTS + 2)
            copy(wlmh[0:HALO, 2 * C:NX, HIGH0:], wm_halo[0:HALO]).then_inc(s_whi, 1)
            act.wait_ge(d_small, 16 * SMALL_DMAS)
            copy(wraw[:, 0:8, D:], wraw[:, 0:8, P:D]).then_inc(s_wdup, 1)
            copy(wraw[0:E, 8, D:], wraw[0:E, 8, P:D]).then_inc(s_wdup, 1)
            for n, (rem, _, _, col) in enumerate(WGROUPS):
                act.wait_ge(s_watps, n + 1)
                width = 384 if col == 0 else SPAN - 384
                copy(wat[:, 2 if rem else 0, col:col + width], ps[:, WB[n], 0:width]).then_inc(s_wathi, 1)
                if n == 3:
                    copy(b1t[:], ps[:, WB[n], 400:400 + E * FC]).then_inc(s_wathi, 1)
            act.wait_ge(s_emb, 1)
            copy(u_part[:], ps[:, UB, 0:D]).then_inc(s_u, 1)
            act.wait_ge(d_stage[0], 16 * STAGE_DMAS)
            for part in range(4):
                split_high(0, part)

            def high_parts(ps_ready, banks, dst, done):
                act.wait_ge(ps_ready, 1)
                copy(dst[:, 0], ps[:, banks[0], :]).then_inc(done, 1)
                act.wait_ge(ps_ready, 2)
                copy(dst[:, 2], ps[:, banks[1], :]).then_inc(done, 1)

            high_parts(s_nt, (5, 6), nt[:, :, NT0:], s_nhi)
            act.wait_ge(s_qt, 1)
            act.wait_ge(d_bqk, 16 * BQK_DMAS)
            nc.scalar.activation(qt[:, 0], ps[:, 1, :], ACT.Identity, bias=bqk[:, 0:1]).then_inc(s_qtsb, 1)
            act.wait_ge(s_qt, 2)
            nc.scalar.activation(qt[0:REM, 1], ps[0:REM, 2, :], ACT.Identity,
                                 bias=bqk[0:REM, 1:2]).then_inc(s_qtsb, 1)
            act.wait_ge(s_qt, 3)
            nc.scalar.activation(kts[:, 0], ps[:, 3, 0:S], ACT.Identity, bias=bqk[:, 2:3]).then_inc(s_qtsb, 1)
            nc.scalar.activation(kts[0:REM, 1], ps[0:REM, 3, S:2 * S], ACT.Identity,
                                 bias=bqk[0:REM, 3:4]).then_inc(s_qtsb, 1)
            act.wait_ge(s_vs, 1)
            copy(v_s[:], ps[0:S, 4, 0:D]).then_inc(s_vssb, 1)
            for t in range(TT):
                b0 = 3 * (t % 2)
                act.wait_ge(s_tok, t + 1)
                copy(kv[:, t, 0], ps[:, b0, 0:2 * D]).then_inc(s_kvsb, 1)
                copy(kv[:, t, 1], ps[:, b0 + 1, 0:2 * D]).then_inc(s_kvsb, 1)
                copy(qtok[:, t], ps[:, b0 + 2, 0:D]).then_inc(s_kvsb, 1)
            for t in range(TT):
                act.wait_ge(s_sub, t + 1)
                nc.scalar.activation(pr[:, t], sc[:, t], ACT.Exp, scale=float(HD) ** -0.5).then_inc(s_exp, 1)
                act.wait_ge(s_ptps, t + 1)
                if t >= 2:
                    act.wait_ge(s_pv, t - 1)
                copy(ptsb[:, t % 2], ps[0:WROWS, 7, 0:P]).then_inc(s_pt, 1)
                if t >= 1:
                    act.wait_ge(s_o, t)
                    copy(ao[:, t - 1, D:], ao[:, t - 1, P:D]).then_inc(s_ao, 1)
            act.wait_ge(s_o, TT)
            copy(ao[:, TT - 1, D:], ao[:, TT - 1, P:D]).then_inc(s_ao, 1)
            high_parts(s_at, (0, 1), aot, s_ahi)
            high_parts(s_n2t, (0, 1), n2t, s_n2hi)
            act.wait_ge(s_rl, 1)
            copy(lgt[:], ps[0:E, 6, :]).then_inc(s_rlsb, 1)
            act.wait_ge(s_gsub, 1)
            nc.scalar.activation(ex[:], lg[:], ACT.Exp).then_inc(s_gexp, 1)

            def pair(i, last):
                for j in range(2 * FC):
                    k, f, slot = i * (2 * FC) + j, j % FC, j // FC
                    act.wait_ge(s_mm1, k + 1)
                    nc.scalar.activation(gf[:, j % NG], ps[:, HPB[j % 4], :], ACT.Gelu,
                                         bias=b1t[:, bass.ds(k, 1)]).then_inc(s_gelu, 1)
                    act.wait_ge(s_gelu, k + 1)
                    copy(g_hi[:, j % NG], gf[:, j % NG]).then_inc(s_ghi, 1)
                    if last and slot == 1:
                        continue
                    if f == 1:
                        act.wait_ge(d_stage[1 - slot], (i + 1 + slot) * (16 * STAGE_DMAS))
                    if 1 <= f <= 4:
                        split_high(1 - slot, f - 1)

            with act.Fori(0, E // 2 - 1) as i:
                pair(i, False)
            pair(E // 2 - 1, True)

        @block.tensor
        def _(pe):
            pe.wait_ge(d_gb, 32)
            pe.wait_ge(c_ones, 1)
            pe.wait_ge(c_pool, 3)
            pe.wait_ge(c_shiftm, 2)

            def shift(n):
                return band[:, BAND0 + n:BAND0 + n + P]

            dst = ps[:, 0, 0:2 * (SHIFTS - 1) * 9].rearrange("p (h s k) -> p s h k", h=2, s=SHIFTS - 1)
            for s, m in enumerate((from_right[:], from_left[:])):
                nc.tensor.matmul(dst[:, s].rearrange("p h (k c) -> p h k c", c=C), m,
                                 gb_nat[:, :, :, (s + 1) * C:(s + 2) * C], start=True, stop=True)
            for s, half, mats in ((2, 0, ((1, PATCH - P), (0, PATCH))), (2, 1, ((1, PATCH),)),
                                  (3, 0, ((0, -PATCH),)), (3, 1, ((0, P - PATCH), (1, -PATCH)))):
                for n, (of, by) in enumerate(mats):
                    mm = nc.tensor.matmul(dst[:, s, half], shift(by), gb_nat[:, of, :, (s + 1) * C:(s + 2) * C],
                                          start=(n == 0), stop=(n == len(mats) - 1))
            mm.then_inc(s_gbps, 1)
            pe.wait_ge(s_tile, C)
            for g in range(XGROUPS):
                c, wh = g // 2, g % 2
                for w in range(4):
                    wx = 4 * wh + w
                    mm = nc.tensor.transpose(ps[:, XB[g], w * P:(w + 1) * P],
                                             tiles[c][:, wx].rearrange("p q x -> p (q x)"), ident)
                mm.then_inc(s_xt, 1)
            pe.wait_ge(c_pick, 4)
            dst = ps[0:HALO, 0, GBH0:GBH0 + 4]
            for c in range(C):
                left = PICK0 - QR * c
                right = left - C * QR
                nc.tensor.matmul(dst, pick_left[:, left:left + HALO], gb_nat[:, :, 0:2, C + c],
                                 start=(c == 0), stop=False)
                nc.tensor.matmul(dst, pick_right[:, right:right + HALO], gb_nat[:, :, 0:2, 2 * C + c],
                                 start=False, stop=False)
            for c in range(C):
                above = BAND0 - 64 - PATCH * c
                nc.tensor.matmul(dst[:, 0:2], band[0:PATCH, above:above + HALO], gb_nat[0:PATCH, 0, 0:2, 3 * C + c],
                                 start=False, stop=False)
            for c in range(C):
                below = PICK0 - 64 - PATCH * c
                mm = nc.tensor.matmul(dst[:, 2:4], pick_last[:, below:below + HALO], gb_nat[:, 1, 0:2, 4 * C + c],
                                      start=False, stop=(c == C - 1))
            mm.then_inc(s_gbps, 1)
            pe.wait_ge(s_gather, 2 * GATHERS)
            for n in range(4):
                k, wh = n // 2, n % 2
                pe.wait_ge(s_xsq, n + 1)
                pe.wait_ge(s_xlo, n + 1)
                for w in range(4):
                    mm = nc.tensor.transpose(ps[0:HALO, HB[n], w * P:(w + 1) * P], halo_g[:, k, 4 * wh + w, :], ident)
                mm.then_inc(s_ht, 1)
            def beta_times(half):
                for s in range(SHIFTS):
                    pe.wait_ge(d_wsh[half][s], 16)
                    for c in range(C):
                        nc.tensor.matmul(ps[:, BETAB, 0:D],
                                         gb[:, half, s, C + c:C + c + 1].broadcast_to([P, P]),
                                         wsh[:, s, half, c * D:(c + 1) * D],
                                         start=(half + s + c == 0), stop=False)

            def embed(chunks):
                for ch in chunks:
                    if ch % C == 0:
                        pe.wait_ge(s_wlo, ch // C + 1)
                    K = P if ch < 2 * C else HALO
                    mm = nc.tensor.matmul(ps[:, UB, 0:LMH], ones_r[0:K, :], wlmh[0:K, ch, :],
                                          start=(ch == 0), stop=(ch == NX - 1))
                    if ch == NX - 1:
                        mm.then_inc(s_emb, 1)
                    for t in range(TT):
                        tok = slice(t * P, (t + 1) * P)
                        nc.tensor.matmul(ps[:, EMB0 + t, 0:LMH], xh[0:K, ch, tok], wlmh[0:K, ch, :],
                                         start=(ch == 0), stop=False)
                        mm = nc.tensor.matmul(ps[:, EMB0 + t, D:LMH], xl[0:K, ch, tok], wlmh[0:K, ch, D:],
                                              start=False, stop=(ch == NX - 1))
                return mm

            pe.wait_ge(s_gb, 3)
            beta_times(0)
            pe.wait_ge(s_hcopy, 8)
            pe.wait_ge(s_xlo, XGROUPS)
            pe.wait_ge(s_xhi, XGROUPS)
            pe.wait_ge(s_m, 4)
            embed(range(C))
            beta_times(1)
            pe.wait_ge(d_halo_w, 16 * HALO_W_DMAS)
            for k in range(2):
                mm = nc.tensor.matmul(ps[:, BETAB, 0:D], gb_halo[0:HALO, k, 1:2].broadcast_to([HALO, P]),
                                      w_halo[0:HALO, k], start=False, stop=(k == 1))
            mm.then_inc(s_beta, 1)
            pe.wait_ge(s_sqsum, 5)
            for t in range(TT):
                tok = slice(t * P, (t + 1) * P)
                for n in range(3):
                    lhs = sq[:, 0, n, tok] if n < 2 else sq_halo[0:HALO, 0, tok]
                    rhs = mcol[:, n, :] if n < 2 else ones_f[0:HALO, 0:2]
                    mm = nc.tensor.matmul(ps[:, SQB, SQ0 + 2 * t:SQ0 + 2 * t + 2], lhs, rhs,
                                          start=(n == 0), stop=(n == 2))
            mm.then_inc(s_sumsq, 1)
            pe.wait_ge(s_wdup, 2)
            for n, (rem, r0, nr, _) in enumerate(WGROUPS):
                if n >= 2:
                    pe.wait_ge(s_watlo, n - 1)
                for r in range(nr):
                    mm = nc.tensor.transpose(ps[:, WB[n], r * WROWS:(r + 1) * WROWS],
                                             wraw[:, r0 + r, rem * P:(rem + 1) * P], ident[0:WROWS, 0:WROWS])
                if r0:
                    mm = nc.tensor.transpose(ps[:, WB[n], 384:384 + E], wraw[0:E, 8, rem * P:(rem + 1) * P],
                                             ident[0:E, 0:E])
                if n == 3:
                    mm = nc.tensor.transpose(ps[:, WB[n], 400:400 + E * FC], b1raw[:], ident[0:E * FC, 0:E * FC])
                mm.then_inc(s_watps, 1)
            embed(range(C, 2 * C))
            pe.wait_ge(s_hhi, 1)
            pe.wait_ge(s_hlo, 1)
            embed(range(2 * C, NX)).then_inc(s_emb, 1)
            def transposes(src, ready, count, banks, done):
                for r in range(2):
                    for t in range(TT):
                        if r == 0:
                            pe.wait_ge(ready, count(t))
                        mm = nc.tensor.transpose(ps[:, banks[r], t * P:(t + 1) * P], src[:, t, r * P:(r + 1) * P],
                                                 ident)
                    mm.then_inc(done, 1)

            pe.wait_ge(s_watlo, 4)
            pe.wait_ge(s_wathi, 5)
            pe.wait_ge(s_stat, 1)
            transposes(n1, s_n, lambda t: 2 * t + 2, (5, 6), s_nt)

            def nx(cols):
                return lambda a: nt[:, a, cols]

            def wx_(cols):
                return lambda b: wat[:, b, cols]

            every = slice(NT0, NT0 + T)
            pe.wait_ge(s_h, TT)
            pe.wait_ge(s_nhi, 2)
            pe.wait_ge(s_nlo, 2)
            triple(ps[:, 1, :], nx(every), wx_(slice(0, P)), False).then_inc(s_qt, 1)
            triple(ps[:, 2, :], nx(every), wx_(slice(P, 2 * P)), False).then_inc(s_qt, 1)
            strided = slice(NT0, NT0 + T, STRIDE)
            triple(ps[:, 3, 0:S], nx(strided), wx_(slice(D, D + P)), False)
            triple(ps[:, 3, S:2 * S], nx(strided), wx_(slice(D + P, D + 2 * P)), False).then_inc(s_qt, 1)
            triple(ps[0:S, 4, 0:D], nx(strided), wx_(slice(2 * D, 3 * D)), True).then_inc(s_vs, 1)

            def token_major(t):
                b0 = 3 * (t % 2)
                if t == 0:
                    pe.wait_ge(s_urow, 2)
                    pe.wait_ge(s_qtsb, 4)
                if t == 1:
                    pe.wait_ge(s_vssb, 1)
                if t >= 2:
                    pe.wait_ge(s_kvsb, 3 * (t - 1))
                own = slice(NT0 + t * P, NT0 + (t + 1) * P)
                before = slice(NT0 + t * P - 1, NT0 + (t + 1) * P - 1)
                triple(ps[:, b0, 0:2 * D], nx(own), wx_(slice(D, 3 * D)), True)
                triple(ps[:, b0 + 1, 0:2 * D], nx(before), wx_(slice(D, 3 * D)), True)
                triple(ps[:, b0 + 2, 0:D], nx(own), wx_(slice(0, D)), True).then_inc(s_tok, 1)

            token_major(0)
            token_major(1)
            pe.wait_ge(s_vssb, 1)
            for b in range(B):
                bank, off = 6 + (b // 2) % 2, (b % 2) * D
                if b >= 4 and b % 2 == 0:
                    pe.wait_ge(s_vbd, b // 2 - 1)
                mm = nc.tensor.matmul(ps[0:WROWS, bank, off:off + D], key_rep[:, b].rearrange("p j g -> p (j g)"),
                                      v_s[:], start=True, stop=True)
                if b % 2:
                    mm.then_inc(s_vps, 1)
            token_major(2)
            token_major(3)
            pe.wait_ge(s_vbd, 4)
            pe.wait_ge(s_kbd, 2)
            for t in range(TT):
                if t >= 1:
                    pe.wait_ge(s_pvn, t)
                for n in range(2):
                    b = 2 * t + n
                    tok = slice(b * S, (b + 1) * S)
                    rows = slice(n * S, (n + 1) * S)
                    nc.tensor.matmul(ps[rows, 6, 0:64], qt[:, 0, tok],
                                     kbd_a[:, b].rearrange("p g j -> p (g j)"), start=True, stop=True)
                    mm = nc.tensor.matmul(ps[rows, 6, 64:96], qt[0:REM, 1, tok],
                                          kbd_b[0:REM, b].rearrange("p g j -> p (g j)"), start=True, stop=True)
                mm.then_inc(s_sps, 1)
                pe.wait_ge(s_exp, t + 1)
                if t >= 1:
                    pe.wait_ge(s_pt, t)
                nc.tensor.transpose(ps[0:WROWS, 7, 0:P], pr[:, t, 0:NK].rearrange("p j g -> p (j g)"), ident).then_inc(s_ptps, 1)
                pe.wait_ge(s_pt, t + 1)
                for n in range(2):
                    b = 2 * t + n
                    mm = nc.tensor.matmul(ps[n * S:(n + 1) * S, 6, 128:128 + D], ptsb[:, t % 2, n * S:(n + 1) * S],
                                          vbd[0:WROWS, b], start=True, stop=True)
                mm.then_inc(s_pv, 1)
            transposes(ao, s_ao, lambda t: t + 1, (0, 1), s_at)
            pe.wait_ge(s_ahi, 2)
            pe.wait_ge(s_alo, 2)
            for t in range(TT):
                tok = slice(t * P, (t + 1) * P)
                triple(ps[:, 2 + t, 0:D], lambda a: aot[:, a, tok], wx_(slice(OUT0, OUT0 + D)), True)\
                    .then_inc(s_op, 1)
            transposes(n2, s_n, lambda t: 2 * TT + 2 * t + 2, (0, 1), s_n2t)
            pe.wait_ge(s_n2hi, 2)
            pe.wait_ge(s_n2lo, 2)
            triple(ps[0:E, 6, :], lambda a: n2t[:, a, :], wx_(slice(ROUT0, ROUT0 + E)), False).then_inc(s_rl, 1)

            def layer1(i, j):
                ws = wsplit[j // FC]
                c0 = (j % FC) * P
                if j % FC == 0:
                    pe.wait_ge(s_w1m, i * 2 + j // FC + 1)
                    pe.wait_ge(s_w1lo, i * 2 + j // FC + 1)
                offs = (W1H, W1L, W1R)
                triple(ps[:, HPB[j % 4], :], lambda a: n2t[:, a, :],
                       lambda b: ws[:, offs[b] + c0:offs[b] + c0 + P], False).then_inc(s_mm1, 1)

            def layer2(i, j):
                f, slot = j % FC, j // FC
                w2c = wsplit[slot][:, W2S + f * 2 * D:W2S + (f + 1) * 2 * D]
                if f == 0:
                    pe.wait_ge(s_w2lo, i * 2 + slot + 1)
                pe.wait_ge(s_glo, i * (2 * FC) + j + 1)
                for t in range(TT):
                    tok = slice(t * P, (t + 1) * P)
                    if f == 0:
                        pe.wait_ge(s_acc, (i * 2 + slot) * TT + t + 1)
                    nc.tensor.matmul(ps[:, AB[t], 0:2 * D], g_hi[:, j % NG, tok], w2c,
                                     start=(f == 0), stop=False)
                    nc.tensor.matmul(ps[:, AB[t], D:2 * D], g_lo[:, j % NG, tok], w2c[:, D:],
                                     start=False, stop=(f == FC - 1)).then_inc(s_mm2, 1)

            layer1(0, 0)
            pe.wait_ge(s_rlsb, 1)
            for t in range(TT):
                mm = nc.tensor.transpose(ps[:, 7, t * E:(t + 1) * E], lgt[:, t * P:(t + 1) * P], ident[0:E, 0:E])
            mm.then_inc(s_rt, 1)
            for j in range(1, LAG):
                layer1(0, j)

            def gated_biases():
                for t in range(TT):
                    nc.tensor.matmul(ps[:, HPB[t // 2], (t % 2) * D:(t % 2 + 1) * D], gt[:, t], b2sb[:],
                                     start=True, stop=True).then_inc(s_b2, 1)

            def steps(i, last):
                for j in range(2 * FC):
                    if j % FC == FC - 1:
                        layer2(i, j)
                    if j + LAG < 2 * FC:
                        layer1(i, j + LAG)
                    elif not last:
                        layer1(i + 1, j + LAG - 2 * FC)
                    if j % FC < FC - 1:
                        layer2(i, j)
                    if last and j == 2 * FC - LAG - 1:
                        pe.wait_ge(s_gate, 1)
                        for t in range(TT):
                            mm = nc.tensor.transpose(ps[0:E, HPB[j % 4], t * P:(t + 1) * P], gates[:, t], ident)
                        mm.then_inc(s_gtps, 1)
                    if last and j == 2 * FC - LAG:
                        pe.wait_ge(s_gt, 1)
                        gated_biases()

            with pe.Fori(0, E // 2 - 1) as i:
                steps(i, False)
            steps(E // 2 - 1, True)


        @block.vector
        def _(dve):
            def tt(o, a, b, op):
                return nc.vector.tensor_tensor(o, a, b, op)

            for edge in (wsh[0:32, 2, 0], wsh[0:32, 4, 0], wsh[96:P, 1, 1], wsh[96:P, 3, 1]):
                nc.vector.memset(edge, 0.0).then_inc(c_edge, 1)
            nc.vector.memset(w_halo[:], 0.0).then_inc(c_halo0, 1)
            dve.wait_ge(s_gbps, 1)
            nc.vector.tensor_copy(gb[:, :, 1:], ps[:, 0, 0:2 * (SHIFTS - 1) * 9]
                                  .rearrange("p (h s k) -> p h s k", h=2, s=SHIFTS - 1)).then_inc(s_gb, 1)
            nc.vector.tensor_copy(gb[:, :, 0].rearrange("p h (k c) -> p h k c", c=C),
                                  gb_nat[:, :, :, 0:C]).then_inc(s_gb, 1)
            dve.wait_ge(s_gb, 2)
            nc.vector.tensor_reduce(mcol[:], gb[:, :, :, 6:8].rearrange("p h s k -> p h k s"), AX_X,
                                    ALU.add).then_inc(s_m, 1)
            dve.wait_ge(s_m, 1)
            nc.vector.tensor_copy(wlmh[:, 0:2 * C, D:D + 2].rearrange("p (h c) k -> p h c k", h=2),
                                  mcol[:, :, :].unsqueeze(2).broadcast_to([P, 2, C, 2])).then_inc(s_m, 1)
            dve.wait_ge(c_ones, 4)
            nc.vector.tensor_copy(wlmh[0:HALO, 2 * C:NX, D:D + 2],
                                  ones_f[0:HALO, 0:4].rearrange("p (k n) -> p k n", k=2)).then_inc(s_m, 1)
            nc.vector.tensor_copy(ones_r[:], ones_f[:]).then_inc(s_m, 1)
            dve.wait_ge(d_img, 16 * B)
            dve.wait_ge(c_gath0, 1)
            retile(nc.vector.tensor_copy, 0)
            retile(nc.vector.tensor_copy, 2)
            gather_halo(dve, 0)
            gather_halo(dve, 1)
            halo_rows = x_halo[64:HALO].rearrange("p k (b y w) -> p k b y w", b=B, y=GRID)
            nc.vector.memset(halo_rows[:, 0, :, 0], 0.0).then_inc(s_hedge, 1)
            nc.vector.memset(halo_rows[:, 1, :, GRID - 1], 0.0).then_inc(s_hedge, 1)
            for g in range(XGROUPS):
                c, wh = g // 2, g % 2
                dve.wait_ge(s_xt, g + 1)
                dve.wait_ge(s_xhi, g + 1)
                dve.wait_ge(s_xsq, g + 1)
                src = ps[:, XB[g], :].rearrange("p (w r k) -> p k r w", w=4, k=2)

                def part(tensor):
                    return tensor[:, c:2 * C:C, :].rearrange("p k (r w) -> p k r w", w=GRID)[
                        :, :, :, 4 * wh:4 * wh + 4]
                tt(part(xl), src, part(xh).bitcast(F32), ALU.subtract).then_inc(s_xlo, 1)
            dve.wait_ge(s_gbps, 2)
            nc.vector.tensor_copy(gb_halo[0:HALO].rearrange("p k g -> p (k g)"),
                                  ps[0:HALO, 0, GBH0:GBH0 + 4]).then_inc(s_gb, 1)
            for half in range(2):
                for s in range(SHIFTS):
                    dve.wait_ge(d_wsh[half][s], 16)
                    for c in range(C):
                        src = wsh[:, s, half, c * D:(c + 1) * D]
                        dst = w_sum[:, half, c]
                        gam = gb[:, half, s, c:c + 1]
                        if s == 0:
                            ins = nc.vector.tensor_scalar(dst, src, gam, None, ALU.mult)
                        else:
                            dve.wait_ge(s_merge, half * C * SHIFTS + (s - 1) * C + c + 1)
                            ins = nc.vector.scalar_tensor_tensor(out=dst, in0=src, scalar=gam, in1=dst,
                                                                 op0=ALU.mult, op1=ALU.add)
                        ins.then_inc(s_merge, 1)
                if half == 1:
                    dve.wait_ge(d_halo_w, 16 * HALO_W_DMAS)
                    for k in range(2):
                        nc.vector.tensor_scalar(wm_halo[0:HALO, k], w_halo[0:HALO, k], gb_halo[0:HALO, k, 0:1],
                                                None, ALU.mult).then_inc(s_merge, 1)
                dve.wait_ge(s_whi, half + 1)
                ch = slice(half * C, half * C + C)
                tt(wlmh[:, ch, 0:D], w_sum[:, half], wlmh[:, ch, HIGH0:].bitcast(F32),
                   ALU.subtract).then_inc(s_wlo, 1)
                if half == 0:
                    dve.wait_ge(s_hhi, 1)
                    tt(xl[0:HALO, 2 * C:NX], x_halo[0:HALO], xh[0:HALO, 2 * C:NX].bitcast(F32),
                       ALU.subtract).then_inc(s_hlo, 1)
            dve.wait_ge(s_whi, 3)
            ch = slice(2 * C, NX)
            tt(wlmh[0:HALO, ch, 0:D], wm_halo[0:HALO], wlmh[0:HALO, ch, HIGH0:].bitcast(F32),
               ALU.subtract).then_inc(s_wlo, 1)

            n_chain = [0]

            def link(ins):
                n_chain[0] += 1
                ins.then_inc(s_dve, 1)
                dve.wait_ge(s_dve, n_chain[0])

            dve.wait_ge(c_mask, E)
            link(nc.vector.tensor_reduce(mask[:, 0:NK], tri_p[:], AX_X, ALU.add))
            link(nc.vector.tensor_reduce(mask[:, NK:], near[:], AX_X, ALU.min))

            for n, (rem, _, _, col) in enumerate(WGROUPS):
                width = 384 if col == 0 else SPAN - 384
                dve.wait_ge(s_wathi, n + 1 + (n == 3))
                rows = slice(REM, P) if rem else slice(0, P)
                tt(wat[rows, 2 if rem else 1, col:col + width], ps[rows, WB[n], 0:width],
                   wat[rows, 2 if rem else 0, col:col + width].bitcast(F32), ALU.subtract).then_inc(s_watlo, 1)

            dve.wait_ge(s_beta, 1)
            dve.wait_ge(s_sumsq, 1)
            dve.wait_ge(d_rows, 16 * 3)
            tt(bias_row[:], ps[:, BETAB, 0:D], tokb_row[:], ALU.add).then_inc(s_urow, 1)
            dve.wait_ge(s_emb, 1)
            dve.wait_ge(s_u, 1)
            tt(u_sum[:], ps[:, UB, HIGH0:LMH], u_part[:], ALU.add).then_inc(s_urow, 1)
            dve.wait_ge(s_emb, 2)
            link(nc.vector.tensor_scalar(st4[:, 0].unsqueeze(2), ps[:, EMB0:EMB0 + TT, D:D + 1], -1.0 / FEAT, None,
                                         ALU.mult))
            link(nc.vector.tensor_scalar(st4[:, 1], ps[:, SQB, SQ0:SQ0 + 2 * TT:2], 1.0 / FEAT, None, ALU.mult))
            link(tt(st4[:, 2], st4[:, 0], st4[:, 0], ALU.mult))
            link(tt(st4[:, 3], st4[:, 1], st4[:, 2], ALU.subtract))
            nc.vector.tensor_scalar(st4[:, 4], st4[:, 3], LN_EPS, None, ALU.add).then_inc(s_stat, 1)
            dve.wait_ge(s_urow, 2)
            for t in range(TT):
                nc.vector.scalar_tensor_tensor(out=t_a[:, t], in0=u_sum[:], scalar=st4[:, 0, t:t + 1],
                                               in1=ps[:, EMB0 + t, HIGH0:LMH], op0=ALU.mult,
                                               op1=ALU.add).then_inc(s_t1, 1)
            for t in range(TT):
                dve.wait_ge(s_t1, t + 1)
                tt(t_a[:, t], t_a[:, t], ps[:, EMB0 + t, 0:D], ALU.add).then_inc(s_t2, 1)
            dve.wait_ge(s_pow, 1)
            for t in range(TT):
                dve.wait_ge(s_t2, t + 1)
                nc.vector.scalar_tensor_tensor(out=h[:, t], in0=t_a[:, t], scalar=st4[:, 5, t:t + 1],
                                               in1=bias_row[:], op0=ALU.mult, op1=ALU.add).then_inc(s_h, 1)

            def layer_norm(which, src, ready, dst):
                base = which * TT
                for t in range(TT):
                    dve.wait_ge(ready, t + 1)
                    nc.vector.bn_stats(bn[:, which, t], src[:, t]).then_inc(s_bn, 1)
                for t in range(TT):
                    dve.wait_ge(s_bn, base + t + 1)
                    nc.vector.bn_aggr(mv[:, which, t], bn[:, which, t]).then_inc(s_mv, 1)
                for t in range(TT):
                    dve.wait_ge(s_mv, base + t + 1)
                    nc.vector.tensor_scalar(ve[:, which, t:t + 1], mv[:, which, t, 1:2], LN_EPS, None,
                                            ALU.add).then_inc(s_ve, 1)
                for t in range(TT):
                    dve.wait_ge(s_rs, base + t + 1)
                    for o, a, n in ((0, 0, D), (D, P, REM)):
                        nc.vector.tensor_scalar(dst[:, t, o:o + n], src[:, t, a:a + n], mv[:, which, t, 0:1],
                                                rs[:, which, t:t + 1], ALU.subtract, ALU.mult).then_inc(s_n, 1)

            def low_parts(hi_ready, banks, dst, done):
                for r in range(2):
                    dve.wait_ge(hi_ready, r + 1)
                    tt(dst[:, 2 * r + 1], ps[:, banks[r], :], dst[:, 2 * r].bitcast(F32), ALU.subtract)\
                        .then_inc(done, 1)

            layer_norm(0, h, s_h, n1)
            low_parts(s_nhi, (5, 6), nt[:, :, NT0:], s_nlo)
            dve.wait_ge(s_qtsb, 4)
            for kbd, m, n, g in ((kbd_a, P, 0, 8), (kbd_b, REM, 1, 4)):
                tt(kbd[0:m], kts[0:m, n].rearrange("p (b j) -> p b j", b=B).unsqueeze(2).broadcast_to([m, B, g, NK]),
                   head_of_row[0:m, 0:g].unsqueeze(1).unsqueeze(3).broadcast_to([m, B, g, NK]),
                   ALU.mult).then_inc(s_kbd, 1)

            def near_scores(t):
                dve.wait_ge(s_kvsb, 3 * t + 3)
                r = t % 2
                tt(kb[:, r], kv[:, t, :, 0:D], qkvb_row[:, D:2 * D].unsqueeze(1).broadcast_to([P, 2, D]),
                   ALU.add).then_inc(s_kb, 1)
                tt(qb[:, r], qtok[:, t], qkvb_row[:, 0:D], ALU.add).then_inc(s_kb, 1)
                dve.wait_ge(s_kb, 2 * t + 2)
                tt(prod[:, r], kb[:, r], qb[:, r].unsqueeze(1).broadcast_to([P, 2, D]),
                   ALU.mult).then_inc(s_prod, 1)
                dve.wait_ge(s_prod, t + 1)
                nc.vector.tensor_reduce(sc[:, t, NK:],
                                        prod[:, r].rearrange("p s (g d) -> p s g d", d=HD), AX_X,
                                        ALU.add).then_inc(s_near, 1)

            def v_blocks(n):
                dve.wait_ge(s_vps, n + 1)
                tt(vbd[0:WROWS, 2 * n:2 * n + 2].rearrange("p b (g d) -> p b g d", d=HD),
                   ps[0:WROWS, 6 + n % 2, 0:2 * D].rearrange("p (b g d) -> p b g d", b=2, d=HD),
                   head_of_key[0:WROWS, :].unsqueeze(1).unsqueeze(3).broadcast_to([WROWS, 2, HEADS, HD]),
                   ALU.mult).then_inc(s_vbd, 1)

            near_scores(0)
            v_blocks(0)
            v_blocks(1)
            near_scores(1)
            v_blocks(2)
            v_blocks(3)
            near_scores(2)
            near_scores(3)
            for t in range(TT):
                dve.wait_ge(s_sps, t + 1)
                dve.wait_ge(s_near, t + 1)
                m3 = mask[:, :].unsqueeze(2).broadcast_to([P, NS, HEADS])
                tt(sc[:, t, 0:NK], ps[:, 6, 0:HEADS * NK].rearrange("p (g j) -> p j g", j=NK), m3[:, 0:NK],
                   ALU.add).then_inc(s_sc, 1)
                tt(sc[:, t, NK:], sc[:, t, NK:], m3[:, NK:], ALU.add).then_inc(s_sc, 1)
                dve.wait_ge(s_sc, 2 * t + 2)
                nc.vector.tensor_reduce(mx[:, t], sc[:, t].rearrange("p s g -> p g s"), AX_X,
                                        ALU.max).then_inc(s_mx, 1)
                dve.wait_ge(s_mx, t + 1)
                tt(sc[:, t], sc[:, t], mx[:, t].unsqueeze(1).broadcast_to([P, NS, HEADS]),
                   ALU.subtract).then_inc(s_sub, 1)
                dve.wait_ge(s_exp, t + 1)
                link(nc.vector.tensor_reduce(den[:, t], pr[:, t].rearrange("p s g -> p g s"), AX_X, ALU.add))
                nc.vector.reciprocal(rden[:, t], den[:, t]).then_inc(s_rden, 1)
                link(tt(prod[:, t % 2].rearrange("p s (g d) -> p s g d", d=HD),
                        kv[:, t, :, D:].rearrange("p s (g d) -> p s g d", d=HD),
                        pr[:, t, NK:].unsqueeze(3).broadcast_to([P, 2, HEADS, HD]),
                        ALU.mult))
                link(tt(prod[:, t % 2, 0], prod[:, t % 2, 0], prod[:, t % 2, 1], ALU.add))
                dve.wait_ge(s_pv, t + 1)
                tt(prod[:, t % 2, 1], prod[:, t % 2, 0], ps[:, 6, 128:128 + D], ALU.add).then_inc(s_pvn, 1)
                dve.wait_ge(s_pvn, t + 1)
                dve.wait_ge(s_rden, t + 1)
                link(tt(prod[:, t % 2, 0].rearrange("p (g d) -> p g d", d=HD),
                        prod[:, t % 2, 1].rearrange("p (g d) -> p g d", d=HD),
                        rden[:, t].unsqueeze(2).broadcast_to([P, HEADS, HD]), ALU.mult))
                tt(ao[:, t, 0:D], prod[:, t % 2, 0], qkvb_row[:, 2 * D:], ALU.add).then_inc(s_o, 1)
            low_parts(s_ahi, (0, 1), aot, s_alo)
            dve.wait_ge(s_hb, 1)
            for t in range(TT):
                dve.wait_ge(s_op, t + 1)
                tt(h2[:, t], hb[:, t], ps[:, 2 + t, 0:D], ALU.add).then_inc(s_h2, 1)
            layer_norm(1, h2, s_h2, n2)
            low_parts(s_n2hi, (0, 1), n2t, s_n2lo)

            dve.wait_ge(s_rt, 1)
            nc.vector.tensor_copy(lg[:, :, :], ps[:, 7, 0:TT * E].rearrange("p (t e) -> p t e", t=TT))\
                .then_inc(s_acc, TT)
            dve.wait_ge(s_acc, TT)
            link(nc.vector.tensor_reduce(gs[:, 0], lg[:], AX_X, ALU.max))
            tt(lg[:], lg[:], gs[:, 0].unsqueeze(2).broadcast_to([P, TT, E]), ALU.subtract).then_inc(s_gsub, 1)
            dve.wait_ge(s_gexp, 1)
            for t in range(TT):
                nc.vector.max(top[:, t], ex[:, t]).then_inc(s_gtop, 1)
            for t in range(TT):
                dve.wait_ge(s_gtop, t + 1)
                nc.vector.max_index(topi[:, t], top[:, t], ex[:, t]).then_inc(s_gidx, 1)
            dve.wait_ge(s_gidx, TT)
            link(nc.vector.tensor_copy(topf[:], topi[:]))
            iota3 = iota_e[:, :].unsqueeze(1).broadcast_to([P, TT, E])
            for n in range(2):
                link(tt(oh[:, n], iota3, topf[:, :, n:n + 1].broadcast_to([P, TT, E]), ALU.is_equal))
                link(tt(oh[:, n], oh[:, n], top[:, :, n:n + 1].broadcast_to([P, TT, E]), ALU.mult))
            link(tt(oh[:, 0], oh[:, 0], oh[:, 1], ALU.add))
            link(tt(gs[:, 0], top[:, :, 0], top[:, :, 1], ALU.add))
            link(nc.vector.reciprocal(gs[:, 1], gs[:, 0]))
            tt(gates[:], oh[:, 0], gs[:, 1].unsqueeze(2).broadcast_to([P, TT, E]), ALU.mult).then_inc(s_gate, 1)

            def add_biases():
                dve.wait_ge(s_gtps, 1)
                nc.vector.tensor_copy(gt[:], ps[0:E, GTB, :].rearrange("e (t p) -> e t p", t=TT)).then_inc(s_gt, 1)
                for t in range(TT):
                    dve.wait_ge(s_b2, t // 2 * 2 + 2)
                    tt(acc[:, t], acc[:, t], ps[:, HPB[t // 2], (t % 2) * D:(t % 2 + 1) * D],
                       ALU.add).then_inc(s_b2add, 1)
                dve.wait_ge(s_b2add, TT)

            def low_hidden(i, j):
                dve.wait_ge(s_ghi, i * (2 * FC) + j + 1)
                tt(g_lo[:, j % NG], gf[:, j % NG], g_hi[:, j % NG].bitcast(F32), ALU.subtract).then_inc(s_glo, 1)

            def add_expert(e):
                for t0 in range(0, TT, 2):
                    for t in (t0, t0 + 1):
                        dve.wait_ge(s_mm2, e * (FC * TT) + (FC - 1) * TT + t + 1)
                        nc.vector.scalar_tensor_tensor(out=t_a[:, t], in0=ps[:, AB[t], 0:D],
                                                       scalar=gates[:, t, bass.ds(e, 1)], in1=acc[:, t],
                                                       op0=ALU.mult, op1=ALU.add).then_inc(s_evl, 1)
                    for t in (t0, t0 + 1):
                        dve.wait_ge(s_evl, e * TT + t + 1)
                        nc.vector.scalar_tensor_tensor(out=acc[:, t], in0=ps[:, AB[t], D:2 * D],
                                                       scalar=gates[:, t, bass.ds(e, 1)], in1=t_a[:, t],
                                                       op0=ALU.mult, op1=ALU.add).then_inc(s_acc, 1)

            def pair(i, last):
                for slot in range(2):
                    for j in range(LAG, FC + LAG):
                        if j == FC + LAG - 2:
                            if last and slot == 1:
                                add_biases()
                            add_expert(i * 2 + slot)
                        if not (last and slot == 1 and j >= FC):
                            low_hidden(i, slot * FC + j)

            for j in range(LAG):
                low_hidden(0, j)
            with dve.Fori(0, E // 2 - 1) as i:
                pair(i, False)
            pair(E // 2 - 1, True)


_INS = ["x", "L0_tok_ln_gamma", "L0_tok_ln_beta", "L0_tok_w", "L0_tok_b", "L0_attn_qkv_w", "L0_attn_qkv_b",
        "L0_attn_out_w", "L0_attn_out_b", "L0_ffn_router_w", "L0_ffn_w1", "L0_ffn_b1", "L0_ffn_w2", "L0_ffn_b2"]


def kernel(**inputs):
    import numpy as np
    import concourse.bacc as bacc
    from concourse.bass_utils import run_bass_kernel_spmd

    nc = bacc.Bacc("TRN2", target_bir_lowering=False, num_devices=1)
    arrays, args = {}, []
    for name in _INS:
        a = np.ascontiguousarray(inputs[name])
        arrays[f"in_{name}"] = a
        args.append(nc.dram_tensor(f"in_{name}", a.shape, mybir.dt.from_np(a.dtype), kind="ExternalInput").ap())
    b = inputs["x"].shape[0]
    d = inputs["L0_tok_w"].shape[1]
    s = (inputs["x"].shape[2] // PATCH) ** 2
    out = nc.dram_tensor("out", (b, s, d), F32, kind="ExternalOutput").ap()
    vit_tower(nc, *args, out)
    r = run_bass_kernel_spmd(nc, [arrays], core_ids=[0])
    return r.results[0]["out"]
```

```python
from contextlib import ExitStack

import concourse.bass as bass
from concourse import mybir

F32 = mybir.dt.float32
F32R = mybir.dt.float32r
U32 = mybir.dt.uint32
ALU = mybir.AluOpType
ACT = mybir.ActivationFunctionType
AX_X = mybir.AxisListType.X

P = 128
PATCH = 16
LN_EPS = 1e-5
HEADS = 12
STRIDE = 8
NEG = -1e30


def vit_tower(nc, x, tok_gamma, tok_beta, tok_w, tok_b, qkv_w, qkv_b, out_w, out_b,
              router_w, w1, b1, w2, b2, out):
    B, C, IMG, _ = x.shape
    D = tok_w.shape[1]
    E, _, F = w1.shape
    GRID = IMG // PATCH
    S = GRID * GRID
    T = B * S
    TT = T // P
    HD = D // HEADS
    NK = S // STRIDE
    SHIFTS = 5
    FEAT = SHIFTS * C * PATCH * PATCH
    QR = PATCH // 2
    REM = D - P
    FC = F // P
    SPAN = 3 * D + D + E
    OUT0, ROUT0 = 3 * D, 4 * D
    WROWS = 96
    HALO = 112
    NX = 8
    LMH = 2 * D + 2
    HIGH0 = D + 2
    STAGE = 2 * F + FC * D
    assert (D, HD, S, T, E, F) == (192, 16, 64, 512, 8, 768)

    with ExitStack() as ctx:
        def sb(name, shape, dt=F32):
            return ctx.enter_context(nc.sbuf_tensor(name, shape, dt))

        def sem(name):
            return ctx.enter_context(nc.semaphore(name))

        ps = ctx.enter_context(nc.psum_tensor("ps", [P, 8, 512], F32))

        BAND0 = 160
        band = sb("band", [P, 432])
        from_right = sb("from_right", [P, P])
        from_left = sb("from_left", [P, P])
        ident = band[:, BAND0:BAND0 + P]
        ones_f = sb("ones_f", [P, P])
        ones_r = sb("ones_r", [P, P], F32R)
        neg_half = sb("neg_half", [P, 4])
        table_in = sb("table_in", [P, 1])
        euler = sb("euler", [P, TT])
        group = sb("group", [P, 16])
        group8 = sb("group8", [P, 8])
        tri = sb("tri", [P, NK, 8])
        tri_p = sb("tri_p", [P, NK, 8])
        near = sb("near", [P, 2, 16])
        mask = sb("mask", [P, NK + 2])
        head_of_row = sb("head_of_row", [P, 8])
        head_of_key = sb("head_of_key", [P, HEADS])
        key_rep = sb("key_rep", [S, B, NK, HEADS])
        v_s = sb("v_s", [S, D])
        iota_e = sb("iota_e", [P, E])

        early = sb("early", [P, C * QR * IMG + 2 * GRID * HALO])
        img = early[:, 0:C * QR * IMG].rearrange("p (c q w) -> p c q w", c=C, q=QR)
        halo_g = early[:, C * QR * IMG:].rearrange("p (k w r) -> p k w r", k=2, w=GRID)
        gb_nat = sb("gb_nat", [P, 2, 3, SHIFTS * C])
        gb = sb("gb", [P, 2, SHIFTS, 3 * C])
        gb_halo = sb("gb_halo", [P, 2, 2])
        shifted = sb("shifted", [P, SHIFTS * 2 * C * D])
        wsh = shifted[:, :].rearrange("p (s h n) -> p s h n", s=SHIFTS, h=2)
        merge = sb("merge", [P, (2 * C + 4) * D])
        w_sum = merge[:, 0:2 * C * D].rearrange("p (h c n) -> p h c n", h=2, c=C)
        w_halo = merge[:, 2 * C * D:(2 * C + 2) * D].rearrange("p (k n) -> p k n", k=2)
        wm_halo = merge[:, (2 * C + 2) * D:].rearrange("p (k n) -> p k n", k=2)
        big_r = sb("big_r", [P, 2 * NX * T], F32R)
        xh = big_r[:, 0:NX * T].rearrange("p (k t) -> p k t", k=NX)
        xl = big_r[:, NX * T:].rearrange("p (k t) -> p k t", k=NX)
        sq = sb("sq", [P, 3, 2, T])
        halo = sb("halo", [P, 4 * T])
        x_halo = halo[:, 0:2 * T].rearrange("p (k t) -> p k t", k=2)
        sq_halo = halo[:, 2 * T:].rearrange("p (k t) -> p k t", k=2)
        W1H, W1L, W1R, W2S = 0, F, 2 * F, 3 * F
        wsplit = [sb(f"wsplit{i}", [P, 3 * F + FC * 2 * D], F32R) for i in range(2)]
        wlmh = wsplit[1][:, 0:NX * LMH].rearrange("p (k n) -> p k n", k=NX)
        stage0 = sb("stage0", [P, STAGE])
        staged = [stage0[:, :], early[:, 0:STAGE]]
        mcol = sb("mcol", [P, 2, 2])
        u_part = sb("u_part", [P, D])
        u_sum = sb("u_sum", [P, D])
        bias_row = sb("bias_row", [P, D])
        tokb_row = sb("tokb_row", [1, D])
        qkvb_row = sb("qkvb_row", [P, 3 * D])
        outb_row = sb("outb_row", [P, D])
        st4 = sb("st4", [P, 6, TT])
        h_raw = sb("h", [P, TT * D])
        h = h_raw[:, :].rearrange("p (t d) -> p t d", t=TT)
        PICK0, PICKW = HALO - QR, 2 * HALO - QR
        pick_left, pick_right, pick_last = (h_raw[:, n * PICKW:(n + 1) * PICKW] for n in range(3))
        t_a = sb("t_a", [P, TT, D])
        w_beta = t_a[:, 0:C]

        raw = sb("raw", [P, 9 * 2 * P])
        wraw = raw[0:WROWS, :].rearrange("p (n d) -> p n d", n=9)
        hb = raw[:, 0:TT * D].rearrange("p (t d) -> p t d", t=TT)
        wat = sb("wat", [P, 3, SPAN], F32R)
        b1raw = sb("b1raw", [E * FC, P])
        b1t = sb("b1t", [P, E * FC])
        b2sb = sb("b2sb", [E, D])
        bqk = sb("bqk", [P, 4])
        bias_v = sb("bias_v", [P, 2])
        const_row = sb("const_row", [P, D])

        bn = sb("bn", [P, 2, TT, 6])
        mv = sb("mv", [P, 2, TT, 2])
        ve = sb("ve", [P, 2, TT])
        rs = sb("rs", [P, 2, TT])
        norm = sb("norm", [P, TT * 2 * P])
        n1 = n2 = norm[:, :].rearrange("p (t n) -> p t n", t=TT)
        tiles = [a.rearrange("p (w q x) -> p w q x", w=GRID, q=QR)
                 for a in (stage0[:, 0:TT * 2 * P], stage0[:, TT * 2 * P:2 * TT * 2 * P], norm[:, :])]
        nt = sb("nt", [P, 4, T], F32R)

        qkv = shifted[:, 0:TT * 5 * D].rearrange("p (t n) -> p t n", t=TT)
        kv = qkv[:, :, D:].rearrange("p t (s n) -> p t s n", s=2)
        vbd = shifted[:, TT * 5 * D:TT * 5 * D + B * D].rearrange("p (b n) -> p b n", b=B)
        G, TG = 2, 2 * P
        prod = halo[:, 0:4 * D].rearrange("p (r s n) -> p r s n", r=2, s=2)
        part_sum = [a.rearrange("p (r t n) -> p r t n", r=2, t=2) for a in (halo[:, 4 * D:8 * D], raw[:, 8 * D:12 * D])]
        ptsb = halo[0:WROWS, 3 * T:4 * T]
        qt = sq[:, 0, :, :]
        kts = sq[:, 1, 0, 0:2 * S].rearrange("p (k n) -> p k n", k=2)
        kbd_a = sq[:, 1, 1, :].rearrange("p (b g j) -> p b g j", b=B, g=8)
        kbd_b = sq[:, 2, 0, 0:B * 4 * NK].rearrange("p (b g j) -> p b g j", b=B, g=4)
        NS = NK + 2
        sc = sb("sc", [P, TT, NS, HEADS])
        pr = sb("pr", [P, TT, NS, HEADS])
        mx = sb("mx", [P, TT, HEADS])
        den = sb("den", [P, TT, HEADS])
        rden = sb("rden", [P, TT, HEADS])
        ao = merge[:, 0:TT * 2 * P].rearrange("p (t n) -> p t n", t=TT)
        aot = big_r[:, 0:4 * T].rearrange("p (k t) -> p k t", k=4)
        h2 = merge[:, TT * 2 * P:TT * (2 * P + D)].rearrange("p (t n) -> p t n", t=TT)
        acc = h2

        n2t = big_r[:, 4 * T:8 * T].rearrange("p (k t) -> p k t", k=4)
        g_hi = big_r[:, 8 * T:12 * T].rearrange("p (k t) -> p k t", k=4)
        g_lo = big_r[:, 12 * T:16 * T].rearrange("p (k t) -> p k t", k=4)
        NG = 4
        gf = early[:, STAGE:STAGE + NG * T].rearrange("p (k t) -> p k t", k=NG)
        lg = sb("lg", [P, TT, E])
        top = sb("top", [P, TT, 8])
        topi = sb("topi", [P, TT, 8], U32)
        topf = sb("topf", [P, TT, 8])
        oh = sb("oh", [P, 2, TT, E])
        gs = sb("gs", [P, 4, TT])
        gates = sb("gates", [P, TT, E])
        gt = halo[0:E, 0:T].rearrange("e (t p) -> e t p", t=TT)
        lgt = halo[0:E, T:2 * T]

        d_img, d_gb, d_halo_w, d_rows, d_small, d_bqk, d_out = (
            sem(n) for n in ("d_img", "d_gb", "d_halo_w", "d_rows", "d_small", "d_bqk", "d_out"))
        d_wsh = [[sem(f"d_wsh{half}_{s}") for s in range(SHIFTS)] for half in range(2)]
        d_stage = [sem("d_stage0"), sem("d_stage1")]
        d_prev = [sem(f"d_prev{t}") for t in range(TT)]
        c_edge, c_pick, c_halo0, c_gath0, c_pool, c_band, c_shiftm, c_ones, c_mask, c_euler = (
            sem(n) for n in ("c_edge", "c_pick", "c_halo0", "c_gath0", "c_pool", "c_band", "c_shiftm", "c_ones",
                             "c_mask", "c_euler"))
        s_gbps, s_gb, s_m, s_gather = (sem(n) for n in ("s_gbps", "s_gb", "s_m", "s_gather"))
        s_tile = [sem(f"s_tile{c}") for c in range(C)]
        s_xt, s_xhi, s_xlo, s_xsq, s_sqsum = (sem(n) for n in ("s_xt", "s_xhi", "s_xlo", "s_xsq", "s_sqsum"))
        s_ht, s_hcopy, s_hedge, s_hhi, s_hlo, s_hsq = (
            sem(n) for n in ("s_ht", "s_hcopy", "s_hedge", "s_hhi", "s_hlo", "s_hsq"))
        s_merge, s_whi, s_wlo, s_wbeta = (sem(n) for n in ("s_merge", "s_whi", "s_wlo", "s_wbeta"))
        s_wdup, s_watps, s_wathi, s_watlo = (sem(n) for n in ("s_wdup", "s_watps", "s_wathi", "s_watlo"))
        s_beta, s_bias, s_emb, s_sumsq, s_meansq = (sem(n) for n in ("s_beta", "s_bias", "s_emb", "s_sumsq", "s_meansq"))
        s_stat, s_pow, s_u, s_urow = (sem(n) for n in ("s_stat", "s_pow", "s_u", "s_urow"))
        s_t1, s_t2, s_h, s_hb = (sem(n) for n in ("s_t1", "s_t2", "s_h", "s_hb"))
        s_bn, s_mv, s_ve, s_rs, s_n, s_ndup = (sem(n) for n in ("s_bn", "s_mv", "s_ve", "s_rs", "s_n", "s_ndup"))
        s_nt, s_nhi, s_nlo = (sem(n) for n in ("s_nt", "s_nhi", "s_nlo"))
        s_qt, s_qtsb, s_kst, s_ktsb, s_kbd = (sem(n) for n in ("s_qt", "s_qtsb", "s_kst", "s_ktsb", "s_kbd"))
        s_vssb, s_vps, s_vbd = (sem(n) for n in ("s_vssb", "s_vps", "s_vbd"))
        s_first, s_tok, s_vtok, s_qk = (sem(n) for n in ("s_first", "s_tok", "s_vtok", "s_qk"))
        s_prod, s_near, s_sps, s_sc, s_mx, s_sub, s_exp, s_rden = (
            sem(n) for n in ("s_prod", "s_near", "s_sps", "s_sc", "s_mx", "s_sub", "s_exp", "s_rden"))
        s_ptps, s_pt, s_pv, s_nvp, s_nv, s_pvn, s_ao, s_aodup = (
            sem(n) for n in ("s_ptps", "s_pt", "s_pv", "s_nvp", "s_nv", "s_pvn", "s_ao", "s_aodup"))
        s_vbias, s_row, s_at, s_ahi, s_alo, s_op, s_h2 = (
            sem(n) for n in ("s_vbias", "s_row", "s_at", "s_ahi", "s_alo", "s_op", "s_h2"))
        s_n2t, s_n2hi, s_n2lo = (sem(n) for n in ("s_n2t", "s_n2hi", "s_n2lo"))
        s_rl, s_rlsb, s_rt, s_gsub, s_gexp, s_gtop, s_gidx, s_gate = (
            sem(n) for n in ("s_rl", "s_rlsb", "s_rt", "s_gsub", "s_gexp", "s_gtop", "s_gidx", "s_gate"))
        s_gtps, s_gt, s_b2, s_b2add = (sem(n) for n in ("s_gtps", "s_gt", "s_b2", "s_b2add"))
        s_mm1, s_gelu, s_ghi, s_glo, s_mm2 = (sem(n) for n in ("s_mm1", "s_gelu", "s_ghi", "s_glo", "s_mm2"))
        s_w1hi, s_w2hi, s_w1m, s_w1lo, s_w2lo = (
            sem(n) for n in ("s_w1hi", "s_w2hi", "s_w1m", "s_w1lo", "s_w2lo"))
        s_evl, s_acc, s_dve = (sem(n) for n in ("s_evl", "s_acc", "s_dve"))

        block = ctx.enter_context(nc.Block())

        XB = [1, 2, 3, 4, 5, 6]
        HB = [1, 2, 3, 4]
        WB = [5, 6, 5, 6]
        EMB0, SQB, UB, BETAB = 1, 7, 0, 7
        BETA0 = 300
        SQ0 = 256
        NTB, QB, KB, VB, SB = (5, 6), 7, 6, (6, 1, 2, 3), (4, 7)
        PTB, PVB, ATB, OB, N2B = (6, 2), (0, 1), (3, 4), (5, 6), (7, 4)
        RB = 5
        EARLY = 2
        LAG = 3
        HPB = [0, 1, 2, 3]
        GTB = HPB[(2 * FC - LAG - 1) % 4]
        AB = [4, 5, 6, 7]
        WGROUPS = [(0, 0, 4, 0), (1, 0, 4, 0), (0, 4, 4, 384), (1, 4, 4, 384)]
        XGROUPS = 2 * C

        def gather_halo(k):
            px = img.rearrange("p c q (w x) -> p w c q x", x=PATCH)
            q_edge = QR - 1 if k == 0 else 0
            nc.vector.tensor_copy(halo_g[:, k, 1:GRID, 0:3 * QR].rearrange("p w (c q) -> p w c q", c=C),
                                  px[:, 0:GRID - 1, :, :, PATCH - 1]).then_inc(s_gather, 1)
            nc.vector.tensor_copy(halo_g[:, k, 0:GRID - 1, 3 * QR:6 * QR].rearrange("p w (c q) -> p w c q", c=C),
                                  px[:, 1:GRID, :, :, 0]).then_inc(s_gather, 1)
            nc.vector.tensor_copy(halo_g[:, k, :, 64:HALO].rearrange("p w (c x) -> p w c x", c=C),
                                  px[:, :, :, q_edge, :]).then_inc(s_gather, 1)
        GATHERS = 3

        def retile(copy_op, c):
            copy_op(tiles[c], img[:, c].rearrange("p q (w x) -> p w q x", x=PATCH)).then_inc(s_tile[c], 1)

        def split_low(pool, e, slot):
            st, ws = staged[slot], wsplit[slot]
            pool.wait_ge(s_w1hi, e * 2 + 1)
            nc.gpsimd.tensor_tensor(ws[:, W1L:W1L + F], st[:, 0:F], ws[:, W1H:W1H + F].bitcast(F32),
                                    ALU.subtract).then_inc(s_w1m, 1)
            pool.wait_ge(s_w1m, e + 1)
            pool.wait_ge(s_w1hi, e * 2 + 2)
            nc.gpsimd.tensor_tensor(ws[REM:P, W1R:W1R + F], st[REM:P, F:2 * F],
                                    ws[REM:P, W1R:W1R + F].bitcast(F32), ALU.subtract).then_inc(s_w1lo, 1)
            pool.wait_ge(s_w1lo, e + 1)
            pool.wait_ge(s_w2hi, e * 2 + 2)
            w2v = ws[:, W2S:].rearrange("p (c n) -> p c n", c=FC)
            nc.gpsimd.tensor_tensor(w2v[:, :, 0:D], st[:, 2 * F:].rearrange("p (c n) -> p c n", c=FC),
                                    w2v[:, :, D:].bitcast(F32), ALU.subtract).then_inc(s_w2lo, 1)

        def copy(o, a):
            return nc.scalar.activation(o, a, ACT.Copy)

        def split_high(slot, part):
            st, ws = staged[slot], wsplit[slot]
            if part < 2:
                to = (W1H, W1R)[part]
                copy(ws[:, to:to + F], st[:, part * F:(part + 1) * F]).then_inc(s_w1hi, 1)
            else:
                c = slice((part - 2) * FC // 2, (part - 1) * FC // 2)
                copy(ws[:, W2S:].rearrange("p (c n) -> p c n", c=FC)[:, c, D:],
                     st[:, 2 * F:].rearrange("p (c n) -> p c n", c=FC)[:, c]).then_inc(s_w2hi, 1)

        def small_dmas(sp):
            def every(ap):
                return ap.unsqueeze(0).broadcast_to([P, ap.shape[0]])
            sp.dma_start(wraw[:, 0:6, 0:D], qkv_w.rearrange("(n p) d -> p n d", p=WROWS)).then_inc(d_small, 16)
            sp.dma_start(wraw[:, 6:8, 0:D], out_w.rearrange("(n p) d -> p n d", p=WROWS)).then_inc(d_small, 16)
            sp.dma_start(wraw[0:E, 8, 0:D], router_w).then_inc(d_small, 16)
            sp.dma_start(b1raw[:], b1.rearrange("e (c p) -> (e c) p", p=P)).then_inc(d_small, 16)
            sp.dma_start(tokb_row[:], tok_b.unsqueeze(0)).then_inc(d_rows, 16)
            sp.dma_start(qkvb_row[:], every(qkv_b)).then_inc(d_rows, 16)
            sp.dma_start(outb_row[:], every(out_b)).then_inc(d_rows, 16)
            for n, (o, m) in enumerate(((0, P), (P, REM), (D, P), (D + P, REM))):
                sp.dma_start(bqk[0:m, n:n + 1], qkv_b[o:o + m].unsqueeze(1),
                             allow_slow_non_contiguous=True).then_inc(d_bqk, 16)
            for rows, n, o in ((slice(0, P), 0, 2 * D), (slice(0, REM), 1, 2 * D + P), (slice(REM, P), 1, 2 * D + P)):
                sp.dma_start(bias_v[rows, n:n + 1], qkv_b[o:o + rows.stop - rows.start].unsqueeze(1),
                             allow_slow_non_contiguous=True).then_inc(d_bqk, 16)
            sp.dma_start(b2sb[:], b2).then_inc(d_bqk, 16)
        SMALL_DMAS, BQK_DMAS = 4, 8

        def triple(dst, x_of, w_of, x_stationary):
            order = ((0, 0), (0, 1), (1, 0), (2, 2), (3, 2)) if x_stationary else \
                ((0, 0), (1, 0), (0, 1), (2, 2), (3, 2))
            for n, (a, b) in enumerate(order):
                lhs, rhs = (x_of(a), w_of(b)) if x_stationary else (w_of(b), x_of(a))
                mm = nc.tensor.matmul(dst, lhs, rhs, start=(n == 0), stop=(n == 4))
            return mm

        HALO_W_DMAS = 3 * C

        def load_expert(sp, e, slot):
            st = staged[slot]
            w1e, w2e = w1[bass.ds(e, 1)], w2[bass.ds(e, 1)]
            sp.dma_start(st[:, 0:F], w1e[:, 0:P, :].rearrange("o p f -> (o p) f")).then_inc(d_stage[slot], 16)
            for half in range(2):
                sp.dma_start(st[half * REM:half * REM + REM, F:2 * F],
                             w1e[:, P:D, :].rearrange("o p f -> (o p) f")).then_inc(d_stage[slot], 16)
            sp.dma_start(st[:, 2 * F:].rearrange("p (c n) -> p c n", c=FC),
                         w2e.rearrange("o (c p) n -> (o p) c n", p=P)).then_inc(d_stage[slot], 16)
        STAGE_DMAS = 4

        @block.sync
        def _(sp):
            wv = tok_w.rearrange("(p k) e -> p (k e)", k=SHIFTS * C)
            for b in range(B):
                sp.dma_start(img[b * 2 * GRID:(b + 1) * 2 * GRID],
                             x[b].rearrange("c (r q) w -> r c q w", q=QR)).then_inc(d_img, 16)
            OFF = [0, 1, -1, PATCH, -PATCH]
            sp.wait_ge(c_edge, 4)
            for half in range(2):
                for s in range(SHIFTS):
                    lo = half * P + OFF[s]
                    first, last = max(0, lo), min(2 * P, lo + P)
                    sp.dma_start(wsh[first - lo:last - lo, s, half],
                                 wv[first:last, s * C * D:(s + 1) * C * D]).then_inc(d_wsh[half][s], 16)
            sp.wait_ge(c_halo0, 1)
            pv = tok_w.rearrange("(k y x s c) e -> y x s c k e", k=2, x=PATCH, s=SHIFTS, c=C)
            last_row = ((PATCH - 1) * PATCH * SHIFTS + 1) * C
            for c in range(C):
                sp.dma_start(w_halo[QR * c:QR * (c + 1)], pv[:, 0, 1, c]).then_inc(d_halo_w, 16)
                sp.dma_start(w_halo[QR * (C + c):QR * (C + c + 1)], pv[:, PATCH - 1, 2, c]).then_inc(d_halo_w, 16)
                above_below = bass.AP(tensor=tok_w.tensor, offset=(3 * C + c) * D,
                                      ap=[[SHIFTS * C * D, PATCH], [last_row * D, 2], [1, D]])
                sp.dma_start(w_halo[64 + PATCH * c:64 + PATCH * (c + 1)], above_below).then_inc(d_halo_w, 16)
            small_dmas(sp)
            sp.wait_ge(s_xt, XGROUPS)
            load_expert(sp, 0, 0)
            sp.wait_ge(s_ht, 4)
            load_expert(sp, 1, 1)
            for t in range(TT):
                sp.wait_ge(s_qk, t + 1)
                sp.wait_ge(s_vtok, t + 1)
                if t == 0:
                    sp.wait_ge(s_first, 1)
                sp.dma_start(kv[1:P, t, 1], kv[0:P - 1, t, 0]).then_inc(d_prev[t], 16)
                if t > 0:
                    sp.dma_start(kv[0:1, t, 1], kv[P - 1:P, t - 1, 0]).then_inc(d_prev[t], 16)
            with sp.Fori(1, E // 2) as i:
                for slot in range(2):
                    sp.wait_ge(s_w1lo, i * 2 + slot - 1)
                    sp.wait_ge(s_w2lo, i * 2 + slot - 1)
                    load_expert(sp, i * 2 + slot, slot)
            for t in range(TT):
                sp.wait_ge(s_acc, E * TT + t + 1)
                sp.dma_start(out[t * 2:t * 2 + 2].rearrange("b s d -> (b s) d"),
                             acc[:, t]).then_inc(d_out, 16)
            sp.wait_ge(d_out, 16 * TT)

        @block.gpsimd
        def _(pool):
            nc.gpsimd.memset(gb_nat[:, :, 2, :], 1.0).then_inc(c_ones, 1)
            step = [0]

            def then(ins):
                step[0] += 1
                ins.then_inc(c_pool, 1)
                pool.wait_ge(c_pool, step[0])

            then(nc.gpsimd.memset(band[:], 0.0))
            then(nc.gpsimd.affine_select(out=band[:], in_=band[:], compare_op=ALU.not_equal, fill=1.0,
                                         base=BAND0, pattern=[[-1, 432]], channel_multiplier=1))
            nc.gpsimd.tensor_copy(from_right[:], band[:, BAND0 + 1:BAND0 + 1 + P]).then_inc(c_band, 1)
            then(nc.gpsimd.tensor_copy(from_left[:], band[:, BAND0 - 1:BAND0 - 1 + P]))
            pool.wait_ge(c_band, 1)
            nc.gpsimd.memset(from_right[:, :].rearrange("p (q x) -> p q x", x=PATCH)[:, :, PATCH - 1:PATCH],
                             0.0).then_inc(c_shiftm, 1)
            nc.gpsimd.memset(from_left[:, :].rearrange("p (q x) -> p q x", x=PATCH)[:, :, 0:1],
                             0.0).then_inc(c_shiftm, 1)
            then(nc.gpsimd.memset(h_raw[:, 0:3 * PICKW], 0.0))
            for pick, base, per in ((pick_left, PICK0 * PATCH, PATCH),
                                    (pick_right, PICK0 * PATCH - (PATCH - 1), PATCH),
                                    (pick_last, PICK0 - (P - PATCH), 1)):
                nc.gpsimd.affine_select(out=pick, in_=pick, compare_op=ALU.not_equal, fill=1.0, base=base,
                                        pattern=[[-per, PICKW]], channel_multiplier=1).then_inc(c_pick, 1)
            pool.wait_ge(c_pick, 3)
            nc.gpsimd.memset(pick_last[:, 0:PICK0], 0.0).then_inc(c_pick, 1)
            nc.gpsimd.memset(halo_g, 0.0).then_inc(c_gath0, 1)
            nc.gpsimd.memset(ones_f[:], 1.0).then_inc(c_ones, 1)
            nc.gpsimd.memset(euler[:], 2.718281828459045).then_inc(c_euler, 1)
            nc.gpsimd.memset(neg_half[:], -0.5).then_inc(c_ones, 1)
            then(nc.gpsimd.memset(head_of_row[:], 1.0))
            then(nc.gpsimd.affine_select(out=head_of_row[:], in_=head_of_row[:], compare_op=ALU.is_ge, fill=0.0,
                                         base=0, pattern=[[-HD, 8]], channel_multiplier=1))
            then(nc.gpsimd.affine_select(out=head_of_row[:], in_=head_of_row[:], compare_op=ALU.is_ge, fill=0.0,
                                         base=HD - 1, pattern=[[HD, 8]], channel_multiplier=-1))
            then(nc.gpsimd.memset(head_of_key[:], 0.0))
            for j in range(NK):
                then(nc.gpsimd.affine_select(out=head_of_key[:], in_=head_of_key[:], compare_op=ALU.not_equal,
                                             fill=1.0, base=-HEADS * j, pattern=[[-1, HEADS]],
                                             channel_multiplier=1))
            then(nc.gpsimd.memset(key_rep[:], 0.0))
            then(nc.gpsimd.affine_select(out=key_rep[:], in_=key_rep[:], compare_op=ALU.not_equal, fill=1.0,
                                         base=0, pattern=[[-NK, B], [-1, NK], [0, HEADS]],
                                         channel_multiplier=1))
            then(nc.gpsimd.memset(group[:], 1.0))
            then(nc.gpsimd.affine_select(out=group[:], in_=group[:], compare_op=ALU.is_ge, fill=0.0,
                                         base=0, pattern=[[-8, 16]], channel_multiplier=1))
            then(nc.gpsimd.affine_select(out=group[:], in_=group[:], compare_op=ALU.is_ge, fill=0.0,
                                         base=7, pattern=[[8, 16]], channel_multiplier=-1))
            then(nc.gpsimd.tensor_tensor(group8[:], group[:, 0:8], group[:, 8:16], ALU.add))
            then(nc.gpsimd.memset(tri[:], 0.0))
            then(nc.gpsimd.affine_select(out=tri[:], in_=tri[:], compare_op=ALU.is_ge, fill=NEG,
                                         base=0, pattern=[[-1, NK], [1, 8]], channel_multiplier=0))
            then(nc.gpsimd.tensor_tensor(tri_p[:], tri[:],
                                         group8[:, :].unsqueeze(1).broadcast_to([P, NK, 8]), ALU.mult))
            then(nc.gpsimd.memset(near[:], 0.0))
            then(nc.gpsimd.affine_select(out=near[:], in_=near[:], compare_op=ALU.not_equal, fill=NEG,
                                         base=0, pattern=[[-1, 2], [-8, 16]], channel_multiplier=1))
            then(nc.gpsimd.affine_select(out=near[:, 1], in_=near[:, 1], compare_op=ALU.not_equal, fill=NEG,
                                         base=0, pattern=[[-S, 16]], channel_multiplier=1))
            for e in range(E):
                nc.gpsimd.memset(iota_e[:, e:e + 1], float(e)).then_inc(c_mask, 1)

            for c in range(1, C):
                pool.wait_ge(s_xsq, 2 * c + 2)
                for half in range(2):
                    if c > 1:
                        pool.wait_ge(s_sqsum, 2 * (c - 2) + half + 1)
                    nc.gpsimd.tensor_tensor(sq[:, 0, half], sq[:, 0, half], sq[:, c, half],
                                            ALU.add).then_inc(s_sqsum, 1)
            pool.wait_ge(s_hsq, 1)
            nc.gpsimd.tensor_tensor(sq_halo[0:HALO, 0], sq_halo[0:HALO, 0], sq_halo[0:HALO, 1],
                                    ALU.add).then_inc(s_sqsum, 1)
            split_low(pool, 0, 0)
            pool.wait_ge(s_wbeta, 4 * SHIFTS)
            pool.wait_ge(s_merge, 2 * C * SHIFTS)
            nc.gpsimd.memset(kv[0:1, 0, 1], 0.0).then_inc(s_first, 1)

            def rstd(which, g):
                pool.wait_ge(s_ve, which * G + g + 1)
                nc.gpsimd.tensor_tensor(rs[:, which, 2 * g:2 * g + 2], ve[:, which, 2 * g:2 * g + 2],
                                        neg_half[:, 0:2], ALU.pow).then_inc(s_rs, 1)

            pool.wait_ge(c_ones, 3)
            for g in range(G):
                ts = slice(2 * g, 2 * g + 2)
                pool.wait_ge(s_stat, g + 1)
                nc.gpsimd.tensor_tensor(st4[:, 5, ts], st4[:, 4, ts], neg_half[:, ts], ALU.pow).then_inc(s_pow, 1)
                if g == 0:
                    rstd(0, 0)
            rstd(0, 1)
            pool.wait_ge(s_row, 1)
            pool.wait_ge(s_h, TT)
            pool.wait_ge(s_watps, 4)
            nc.gpsimd.tensor_tensor(hb[:], h[:], const_row[:, :].unsqueeze(1).broadcast_to([P, TT, D]),
                                    ALU.add).then_inc(s_hb, 1)

            def near_values(g):
                ts = slice(2 * g, 2 * g + 2)
                pool.wait_ge(s_exp, g + 1)
                for s in range(2):
                    nc.gpsimd.tensor_tensor(part_sum[g][:, s].rearrange("p t (g d) -> p t g d", d=HD),
                                            kv[:, ts, s, D:].rearrange("p t (g d) -> p t g d", d=HD),
                                            pr[:, ts, NK + s].unsqueeze(3).broadcast_to([P, 2, HEADS, HD]),
                                            ALU.mult).then_inc(s_nvp, 1)
                pool.wait_ge(s_nvp, 2 * g + 2)
                nc.gpsimd.tensor_tensor(part_sum[g][:, 0], part_sum[g][:, 0], part_sum[g][:, 1],
                                        ALU.add).then_inc(s_nv, 1)

            pool.wait_ge(s_vtok, TT)
            near_values(0)
            near_values(1)
            rstd(1, 0)
            rstd(1, 1)
            pool.wait_ge(c_euler, 1)
            pool.wait_ge(s_gsub, 1)
            nc.gpsimd.tensor_tensor(gs[:, 1], euler[:], gs[:, 0], ALU.pow).then_inc(s_gexp, 1)
            split_low(pool, 1, 1)
            with pool.Fori(1, E // 2) as i:
                for slot in range(2):
                    split_low(pool, i * 2 + slot, slot)

        @block.scalar
        def _(act):
            gv = tok_gamma.rearrange("(h p k) -> p h k", h=2, k=SHIFTS * C)
            bv = tok_beta.rearrange("(h p k) -> p h k", h=2, k=SHIFTS * C)
            act.dma_start(gb_nat[:, :, 0, :], gv).then_inc(d_gb, 16)
            act.dma_start(gb_nat[:, :, 1, :], bv).then_inc(d_gb, 16)
            act.wait_ge(d_img, 16 * B)
            retile(copy, 1)
            for g in range(XGROUPS):
                c, wh = g // 2, g % 2
                act.wait_ge(s_xt, g + 1)
                src = ps[:, XB[g], :].rearrange("p (w r k) -> p k r w", w=4, k=2)
                for out_t, s_done in ((xh, s_xhi), (sq, s_xsq))[c == C - 1:]:
                    if out_t is xh:
                        dst = xh[:, c:2 * C:C, :]
                    else:
                        dst = sq[:, c]
                    dst = dst.rearrange("p k (r w) -> p k r w", w=GRID)[:, :, :, 4 * wh:4 * wh + 4]
                    nc.scalar.activation(dst, src, ACT.Copy if out_t is xh else ACT.Square).then_inc(s_done, 1)
            for k in range(2):
                for wh in range(2):
                    act.wait_ge(s_ht, 2 * k + wh + 1)
                    src = ps[:, HB[2 * k + wh], :].rearrange("p (w b y h) -> p h b y w", w=4, b=B, h=2)
                    dst = x_halo[:, k].rearrange("p (b y w) -> p b y w", b=B, y=GRID)[:, :, :, 4 * wh:4 * wh + 4]
                    copy(dst[0:64], src[0:64, k]).then_inc(s_hcopy, 1)
                    to, of = ((1, 0), (0, 1))[k]
                    rows = GRID - 1
                    copy(dst[64:HALO, :, to:to + rows], src[64:HALO, 1 - k, :, of:of + rows]).then_inc(s_hcopy, 1)
            act.wait_ge(s_hcopy, 8)
            act.wait_ge(s_hedge, 2)
            copy(xh[0:HALO, 2 * C:NX], x_halo[0:HALO]).then_inc(s_hhi, 1)
            nc.scalar.activation(sq_halo[0:HALO], x_halo[0:HALO], ACT.Square).then_inc(s_hsq, 1)
            act.wait_ge(d_small, 16 * SMALL_DMAS)
            copy(wraw[:, 0:8, D:], wraw[:, 0:8, P:D]).then_inc(s_wdup, 1)
            copy(wraw[0:E, 8, D:], wraw[0:E, 8, P:D]).then_inc(s_wdup, 1)
            for half in range(2):
                act.wait_ge(s_merge, C * SHIFTS * (half + 1))
                copy(wlmh[:, half * C:half * C + C, HIGH0:], w_sum[:, half]).then_inc(s_whi, 1)
            act.wait_ge(s_merge, 2 * C * SHIFTS + 2)
            copy(wlmh[0:HALO, 2 * C:NX, HIGH0:], wm_halo[0:HALO]).then_inc(s_whi, 1)
            for n, (rem, _, _, col) in enumerate(WGROUPS):
                act.wait_ge(s_watps, n + 1)
                width = 384 if col == 0 else SPAN - 384
                copy(wat[:, 2 if rem else 0, col:col + width], ps[:, WB[n], 0:width]).then_inc(s_wathi, 1)
                if n == 1:
                    act.wait_ge(d_stage[0], 16 * STAGE_DMAS)
                    split_high(0, 0)
                    split_high(0, 1)
            copy(b1t[:], ps[:, WB[3], 400:400 + E * FC]).then_inc(s_wathi, 1)
            split_high(0, 2)
            split_high(0, 3)
            act.wait_ge(s_emb, 1)
            copy(u_part[:], ps[:, UB, 0:D]).then_inc(s_u, 1)
            act.wait_ge(s_beta, 1)
            copy(bias_row[:], ps[:, BETAB, 0:D]).then_inc(s_bias, 1)

            def high_parts(g, ps_ready, banks, dst, done):
                act.wait_ge(ps_ready, g + 1)
                copy(dst[:, 0:4:2, g * TG:(g + 1) * TG],
                     ps[:, banks[g], :].rearrange("p (k t) -> p k t", k=2)).then_inc(done, 1)

            def transposed_q(g):
                cols = slice(g * TG, (g + 1) * TG)
                act.wait_ge(s_qt, g + 1)
                nc.scalar.activation(qt[:, 0, cols], ps[:, QB, 0:TG], ACT.Identity,
                                     bias=bqk[:, 0:1]).then_inc(s_qtsb, 1)
                nc.scalar.activation(qt[0:REM, 1, cols], ps[0:REM, QB, TG:2 * TG], ACT.Identity,
                                     bias=bqk[0:REM, 1:2]).then_inc(s_qtsb, 1)

            def token_major(t):
                act.wait_ge(s_tok, t + 1)
                copy(kv[:, t, 0, D:], ps[:, 3 * (t % 2) + 2, 0:D]).then_inc(s_vtok, 1)

            def exponentials(g):
                act.wait_ge(s_sub, g + 1)
                nc.scalar.activation(pr[:, 2 * g:2 * g + 2], sc[:, 2 * g:2 * g + 2], ACT.Exp,
                                     scale=float(HD) ** -0.5).then_inc(s_exp, 1)

            def transposed_p(g):
                act.wait_ge(s_ptps, g + 1)
                copy(ptsb[:, g * TG:(g + 1) * TG], ps[0:WROWS, PTB[g], 0:TG]).then_inc(s_pt, 1)

            def last_columns_again(which, g, dst):
                for t in (2 * g, 2 * g + 1):
                    act.wait_ge(s_n, which * TT + t + 1)
                    copy(dst[:, t, D:], dst[:, t, P:D]).then_inc(s_ndup, 1)

            last_columns_again(0, 0, n1)
            high_parts(0, s_nt, NTB, nt, s_nhi)
            last_columns_again(0, 1, n1)
            act.wait_ge(d_bqk, 16 * BQK_DMAS)
            transposed_q(0)
            high_parts(1, s_nt, NTB, nt, s_nhi)
            token_major(0)
            act.wait_ge(s_kst, 1)
            nc.scalar.activation(kts[:, 0], ps[:, KB, 0:S], ACT.Identity, bias=bqk[:, 2:3]).then_inc(s_ktsb, 1)
            nc.scalar.activation(kts[0:REM, 1], ps[0:REM, KB, S:2 * S], ACT.Identity,
                                 bias=bqk[0:REM, 3:4]).then_inc(s_ktsb, 1)
            copy(v_s[:], ps[0:S, KB, 2 * S:2 * S + D]).then_inc(s_vssb, 1)
            token_major(1)
            transposed_q(1)
            token_major(2)
            token_major(3)
            exponentials(0)
            transposed_p(0)
            exponentials(1)
            transposed_p(1)
            for g in range(G):
                act.wait_ge(s_ao, g + 1)
                copy(ao[:, 2 * g:2 * g + 2, D:], ao[:, 2 * g:2 * g + 2, P:D]).then_inc(s_aodup, 1)
                high_parts(g, s_at, ATB, aot, s_ahi)
            for g in range(G):
                last_columns_again(1, g, n2)
                high_parts(g, s_n2t, N2B, n2t, s_n2hi)
            nc.scalar.activation(table_in[:], neg_half[:, 0:1], ACT.Gelu)

            def pair(i, last):
                for j in range(2 * FC):
                    k, f, slot = i * (2 * FC) + j, j % FC, j // FC
                    act.wait_ge(s_mm1, k + 1)
                    nc.scalar.activation(gf[:, j % NG], ps[:, HPB[j % 4], :], ACT.Gelu,
                                         bias=b1t[:, bass.ds(k, 1)]).then_inc(s_gelu, 1)
                    act.wait_ge(s_gelu, k + 1)
                    copy(g_hi[:, j % NG], gf[:, j % NG]).then_inc(s_ghi, 1)
                    if last and slot == 1:
                        continue
                    if f == 1:
                        act.wait_ge(d_stage[1 - slot], (i + 1 + slot) * (16 * STAGE_DMAS))
                    if 1 <= f <= 4:
                        split_high(1 - slot, f - 1)

            with act.Fori(0, E // 2 - 1) as i:
                pair(i, False)
            pair(E // 2 - 1, True)

        @block.tensor
        def _(pe):
            pe.wait_ge(d_gb, 32)
            pe.wait_ge(c_ones, 1)
            pe.wait_ge(c_pool, 3)
            pe.wait_ge(c_shiftm, 2)

            def shift(n):
                return band[:, BAND0 + n:BAND0 + n + P]

            dst = ps[:, 0, 0:2 * (SHIFTS - 1) * 9].rearrange("p (h s k) -> p s h k", h=2, s=SHIFTS - 1)
            for s, m in enumerate((from_right[:], from_left[:])):
                nc.tensor.matmul(dst[:, s].rearrange("p h (k c) -> p h k c", c=C), m,
                                 gb_nat[:, :, :, (s + 1) * C:(s + 2) * C], start=True, stop=True)
            for s, half, mats in ((2, 0, ((1, PATCH - P), (0, PATCH))), (2, 1, ((1, PATCH),)),
                                  (3, 0, ((0, -PATCH),)), (3, 1, ((0, P - PATCH), (1, -PATCH)))):
                for n, (of, by) in enumerate(mats):
                    mm = nc.tensor.matmul(dst[:, s, half], shift(by), gb_nat[:, of, :, (s + 1) * C:(s + 2) * C],
                                          start=(n == 0), stop=(n == len(mats) - 1))
            mm.then_inc(s_gbps, 1)
            for g in range(XGROUPS):
                c, wh = g // 2, g % 2
                pe.wait_ge(s_tile[c], 1)
                for w in range(4):
                    wx = 4 * wh + w
                    mm = nc.tensor.transpose(ps[:, XB[g], w * P:(w + 1) * P],
                                             tiles[c][:, wx].rearrange("p q x -> p (q x)"), ident)
                mm.then_inc(s_xt, 1)
            pe.wait_ge(c_pick, 4)
            dst = ps[0:HALO, BETAB, 0:4]
            for c in range(C):
                left = PICK0 - QR * c
                right = left - C * QR
                nc.tensor.matmul(dst, pick_left[:, left:left + HALO], gb_nat[:, :, 0:2, C + c],
                                 start=(c == 0), stop=False)
                nc.tensor.matmul(dst, pick_right[:, right:right + HALO], gb_nat[:, :, 0:2, 2 * C + c],
                                 start=False, stop=False)
            for c in range(C):
                above = BAND0 - 64 - PATCH * c
                nc.tensor.matmul(dst[:, 0:2], band[0:PATCH, above:above + HALO], gb_nat[0:PATCH, 0, 0:2, 3 * C + c],
                                 start=False, stop=False)
            for c in range(C):
                below = PICK0 - 64 - PATCH * c
                mm = nc.tensor.matmul(dst[:, 2:4], pick_last[:, below:below + HALO], gb_nat[:, 1, 0:2, 4 * C + c],
                                      start=False, stop=(c == C - 1))
            mm.then_inc(s_gbps, 1)
            pe.wait_ge(s_gather, 2 * GATHERS)
            for n in range(4):
                k, wh = n // 2, n % 2
                pe.wait_ge(s_xsq, n + 1)
                pe.wait_ge(s_xlo, n + 1)
                for w in range(4):
                    mm = nc.tensor.transpose(ps[0:HALO, HB[n], w * P:(w + 1) * P], halo_g[:, k, 4 * wh + w, :], ident)
                mm.then_inc(s_ht, 1)
            def rows(ch):
                return slice(0, P if ch < 2 * C else HALO)

            def embed(ch, t):
                tok = slice(t * P, (t + 1) * P)
                nc.tensor.matmul(ps[:, EMB0 + t, 0:LMH], xh[rows(ch), ch, tok], wlmh[rows(ch), ch, :],
                                 start=(ch == 0), stop=False)
                return nc.tensor.matmul(ps[:, EMB0 + t, D:LMH], xl[rows(ch), ch, tok], wlmh[rows(ch), ch, D:],
                                        start=False, stop=(ch == NX - 1))

            def weight_sums(ch):
                return nc.tensor.matmul(ps[:, UB, 0:LMH], ones_r[rows(ch), :], wlmh[rows(ch), ch, :],
                                        start=(ch == 0), stop=(ch == NX - 1))

            pe.wait_ge(s_gb, 3)
            for s in range(SHIFTS):
                pe.wait_ge(d_wsh[0][s], 16)
                for c in range(C - 1):
                    nc.tensor.matmul(ps[:, BETAB, 0:D], gb[:, 0, s, C + c:C + c + 1].broadcast_to([P, P]),
                                     wsh[:, s, 0, c * D:(c + 1) * D], start=(s + c == 0), stop=False)
            pe.wait_ge(s_hcopy, 8)
            pe.wait_ge(s_xlo, XGROUPS)
            pe.wait_ge(s_xhi, XGROUPS)
            pe.wait_ge(s_m, 4)
            pe.wait_ge(s_wlo, 1)
            for ch in range(C):
                weight_sums(ch)
                for t in range(TT):
                    embed(ch, t)
            pe.wait_ge(d_halo_w, 16 * HALO_W_DMAS)
            for k in range(2):
                nc.tensor.matmul(ps[:, BETAB, 0:D], gb_halo[0:HALO, k, 1:2].broadcast_to([HALO, P]),
                                 w_halo[0:HALO, k], start=False, stop=(k == 1))
            def small_transposes(groups):
                for n in groups:
                    rem, r0, nr, _ = WGROUPS[n]
                    if n >= 2:
                        pe.wait_ge(s_watlo, n - 1)
                    for r in range(nr):
                        mm = nc.tensor.transpose(ps[:, WB[n], r * WROWS:(r + 1) * WROWS],
                                                 wraw[:, r0 + r, rem * P:(rem + 1) * P], ident[0:WROWS, 0:WROWS])
                    if r0:
                        mm = nc.tensor.transpose(ps[:, WB[n], 384:384 + E], wraw[0:E, 8, rem * P:(rem + 1) * P],
                                                 ident[0:E, 0:E])
                    if n == 3:
                        mm = nc.tensor.transpose(ps[:, WB[n], 400:400 + E * FC], b1raw[:], ident[0:E * FC, 0:E * FC])
                    mm.then_inc(s_watps, 1)

            pe.wait_ge(s_wdup, 2)
            small_transposes((0, 1))
            pe.wait_ge(s_sqsum, 5)
            for t in range(TT):
                tok = slice(t * P, (t + 1) * P)
                for n in range(3):
                    lhs = sq[:, 0, n, tok] if n < 2 else sq_halo[0:HALO, 0, tok]
                    rhs = mcol[:, n, :] if n < 2 else ones_f[0:HALO, 0:2]
                    mm = nc.tensor.matmul(ps[:, SQB, SQ0 + 2 * t:SQ0 + 2 * t + 2], lhs, rhs,
                                          start=(n == 0), stop=(n == 2))
            mm.then_inc(s_sumsq, 1)
            small_transposes((2, 3))
            pe.wait_ge(s_wlo, 3)
            pe.wait_ge(s_hhi, 1)
            pe.wait_ge(s_hlo, 1)
            for ch in range(C, NX):
                mm = weight_sums(ch)
            mm.then_inc(s_emb, 1)
            for g in range(G):
                for t in (2 * g, 2 * g + 1):
                    for ch in range(C, NX):
                        mm = embed(ch, t)
                mm.then_inc(s_emb, 1)
                if g == 0:
                    pe.wait_ge(s_meansq, 1)
                    pe.wait_ge(s_wbeta, 4 * SHIFTS)
                    for c in range(C):
                        nc.tensor.matmul(ps[:, BETAB, BETA0:BETA0 + D], ones_f[:], w_beta[:, c],
                                         start=(c == 0), stop=False)
                    pe.wait_ge(d_rows, 16 * 3)
                    nc.tensor.matmul(ps[:, BETAB, BETA0:BETA0 + D], ones_f[0:1, :], tokb_row[:],
                                     start=False, stop=True).then_inc(s_beta, 1)
            def transposes(g, src, ready, count, banks, done, again=None):
                for r in range(2):
                    for n in range(2):
                        t = 2 * g + n
                        if r == 0:
                            pe.wait_ge(ready, count(t))
                        elif again:
                            pe.wait_ge(again, count(t))
                        mm = nc.tensor.transpose(ps[:, banks[g], r * TG + n * P:r * TG + (n + 1) * P],
                                                 src[:, t, r * P:(r + 1) * P], ident)
                mm.then_inc(done, 1)

            pe.wait_ge(s_watlo, 4)
            pe.wait_ge(s_wathi, 5)
            pe.wait_ge(d_bqk, 16 * BQK_DMAS)
            pe.wait_ge(s_urow, 1)
            for n, (col, part) in enumerate(((0, 0), (0, 1), (1, 2))):
                mm = nc.tensor.matmul(ps[:, UB, 0:D], bias_v[:, col:col + 1].broadcast_to([P, P]),
                                      wat[:, part, OUT0:OUT0 + D].bitcast(F32), start=(n == 0), stop=(n == 2))
            mm.then_inc(s_vbias, 1)

            def nx(cols):
                return lambda a: nt[:, a, cols]

            def wx_(cols):
                return lambda b: wat[:, b, cols]

            def transposed_q(g):
                cols = slice(g * TG, (g + 1) * TG)
                triple(ps[:, QB, 0:TG], nx(cols), wx_(slice(0, P)), False)
                triple(ps[:, QB, TG:2 * TG], nx(cols), wx_(slice(P, 2 * P)), False).then_inc(s_qt, 1)

            def token_major(t):
                b0 = 3 * (t % 2)
                if t >= 2:
                    pe.wait_ge(s_qk, t - 1)
                    pe.wait_ge(s_vtok, t - 1)
                own = slice(t * P, (t + 1) * P)
                triple(ps[:, b0, 0:2 * D], nx(own), wx_(slice(0, 2 * D)), True)
                triple(ps[:, b0 + 2, 0:D], nx(own), wx_(slice(2 * D, 3 * D)), True).then_inc(s_tok, 1)

            transposes(0, n1, s_n, lambda t: t + 1, NTB, s_nt, s_ndup)
            pe.wait_ge(s_stat, 1)
            pe.wait_ge(s_urow, 2)
            pe.wait_ge(s_nhi, 1)
            pe.wait_ge(s_nlo, 1)
            transposed_q(0)
            transposes(1, n1, s_n, lambda t: t + 1, NTB, s_nt, s_ndup)
            pe.wait_ge(s_h, 2)
            pe.wait_ge(s_row, 1)
            token_major(0)
            pe.wait_ge(s_nhi, 2)
            pe.wait_ge(s_nlo, 2)
            strided = slice(0, T, STRIDE)
            triple(ps[:, KB, 0:S], nx(strided), wx_(slice(D, D + P)), False)
            triple(ps[:, KB, S:2 * S], nx(strided), wx_(slice(D + P, D + 2 * P)), False)
            triple(ps[0:S, KB, 2 * S:2 * S + D], nx(strided), wx_(slice(2 * D, 3 * D)), True).then_inc(s_kst, 1)
            pe.wait_ge(s_h, TT)
            token_major(1)
            pe.wait_ge(s_qtsb, 2)
            transposed_q(1)

            def strided_scores(g):
                pe.wait_ge(s_qtsb, 2 * g + 2)
                pe.wait_ge(s_kbd, 2)
                for b in range(4 * g, 4 * g + 4):
                    tok = slice(b * S, (b + 1) * S)
                    rows = slice(b % 2 * S, (b % 2 + 1) * S)
                    c0 = b // 2 % 2 * HEADS * NK
                    nc.tensor.matmul(ps[rows, SB[g], c0:c0 + 64], qt[:, 0, tok],
                                     kbd_a[:, b].rearrange("p g j -> p (g j)"), start=True, stop=True)
                    mm = nc.tensor.matmul(ps[rows, SB[g], c0 + 64:c0 + 96], qt[0:REM, 1, tok],
                                          kbd_b[0:REM, b].rearrange("p g j -> p (g j)"), start=True, stop=True)
                mm.then_inc(s_sps, 1)

            def repeated_v(n):
                for b in (2 * n, 2 * n + 1):
                    mm = nc.tensor.matmul(ps[0:WROWS, VB[n], (b % 2) * D:(b % 2 + 1) * D],
                                          key_rep[:, b].rearrange("p j g -> p (j g)"), v_s[:], start=True, stop=True)
                mm.then_inc(s_vps, 1)

            strided_scores(0)
            token_major(2)
            pe.wait_ge(s_vssb, 1)
            repeated_v(0)
            token_major(3)
            strided_scores(1)
            repeated_v(1)
            pe.wait_ge(s_vtok, 3)
            repeated_v(2)
            pe.wait_ge(s_qk, TT)
            pe.wait_ge(s_vtok, TT)
            repeated_v(3)
            for g in range(G):
                pe.wait_ge(s_vbd, 2 * g + 2)
                pe.wait_ge(s_exp, g + 1)
                for n in range(2):
                    mm = nc.tensor.transpose(ps[0:WROWS, PTB[g], n * P:(n + 1) * P],
                                             pr[:, 2 * g + n, 0:NK].rearrange("p j g -> p (j g)"), ident)
                mm.then_inc(s_ptps, 1)
                pe.wait_ge(s_pt, g + 1)
                for b in range(4 * g, 4 * g + 4):
                    n = b // 2 % 2
                    mm = nc.tensor.matmul(ps[b % 2 * S:(b % 2 + 1) * S, PVB[g], n * D:(n + 1) * D],
                                          ptsb[:, b * S:(b + 1) * S], vbd[0:WROWS, b], start=True, stop=True)
                mm.then_inc(s_pv, 1)
            for g in range(G):
                transposes(g, ao, s_ao, lambda t: t // 2 + 1, ATB, s_at, s_aodup)
            for g in range(G):
                pe.wait_ge(s_ahi, g + 1)
                pe.wait_ge(s_alo, g + 1)
                for n in range(2):
                    tok = slice((2 * g + n) * P, (2 * g + n + 1) * P)
                    mm = triple(ps[:, OB[g], n * D:(n + 1) * D], lambda a: aot[:, a, tok],
                                wx_(slice(OUT0, OUT0 + D)), True)
                mm.then_inc(s_op, 1)
            offs = (W1H, W1L, W1R)

            def layer1(i, j):
                ws = wsplit[j // FC]
                c0 = (j % FC) * P
                if j % FC == 0:
                    pe.wait_ge(s_w1m, i * 2 + j // FC + 1)
                    pe.wait_ge(s_w1lo, i * 2 + j // FC + 1)
                triple(ps[:, HPB[j % 4], :], lambda a: n2t[:, a, :],
                       lambda b: ws[:, offs[b] + c0:offs[b] + c0 + P], False).then_inc(s_mm1, 1)

            def layer2(i, j):
                f, slot = j % FC, j // FC
                w2c = wsplit[slot][:, W2S + f * 2 * D:W2S + (f + 1) * 2 * D]
                if f == 0:
                    pe.wait_ge(s_w2lo, i * 2 + slot + 1)
                pe.wait_ge(s_glo, i * (2 * FC) + j + 1)
                for t in range(TT):
                    tok = slice(t * P, (t + 1) * P)
                    if f == 0:
                        pe.wait_ge(s_acc, (i * 2 + slot) * TT + t + 1)
                    nc.tensor.matmul(ps[:, AB[t], 0:2 * D], g_hi[:, j % NG, tok], w2c,
                                     start=(f == 0), stop=False)
                    nc.tensor.matmul(ps[:, AB[t], D:2 * D], g_lo[:, j % NG, tok], w2c[:, D:],
                                     start=False, stop=(f == FC - 1)).then_inc(s_mm2, 1)

            pe.wait_ge(s_w1m, 1)
            pe.wait_ge(s_w1lo, 1)
            transposes(0, n2, s_n, lambda t: TT + t + 1, N2B, s_n2t, s_ndup)
            for g in range(G):
                cols = slice(g * TG, (g + 1) * TG)
                pe.wait_ge(s_n2hi, g + 1)
                pe.wait_ge(s_n2lo, g + 1)
                triple(ps[0:E, RB, cols], lambda a: n2t[:, a, cols], wx_(slice(ROUT0, ROUT0 + E)), False)\
                    .then_inc(s_rl, 1)
                for j in range(EARLY):
                    if (g, j) == (0, 1):
                        transposes(1, n2, s_n, lambda t: TT + t + 1, N2B, s_n2t, s_ndup)
                    mm = triple(ps[:, HPB[j], cols], lambda a: n2t[:, a, cols],
                                lambda b: wsplit[0][:, offs[b] + j * P:offs[b] + (j + 1) * P], False)
                    if g == 1:
                        mm.then_inc(s_mm1, 1)
            pe.wait_ge(s_rlsb, 1)
            for t in range(TT):
                mm = nc.tensor.transpose(ps[:, 7, t * E:(t + 1) * E], lgt[:, t * P:(t + 1) * P], ident[0:E, 0:E])
            mm.then_inc(s_rt, 1)
            layer1(0, 2)

            def gated_biases():
                for t in range(TT):
                    nc.tensor.matmul(ps[:, HPB[t // 2], (t % 2) * D:(t % 2 + 1) * D], gt[:, t], b2sb[:],
                                     start=True, stop=True).then_inc(s_b2, 1)

            def steps(i, last):
                for j in range(2 * FC):
                    if j % FC == FC - 1:
                        layer2(i, j)
                    if j + LAG < 2 * FC:
                        layer1(i, j + LAG)
                    elif not last:
                        layer1(i + 1, j + LAG - 2 * FC)
                    if j % FC < FC - 1:
                        layer2(i, j)
                    if last and j == 2 * FC - LAG - 1:
                        pe.wait_ge(s_gate, 1)
                        for t in range(TT):
                            mm = nc.tensor.transpose(ps[0:E, HPB[j % 4], t * P:(t + 1) * P], gates[:, t], ident)
                        mm.then_inc(s_gtps, 1)
                    if last and j == 2 * FC - LAG:
                        pe.wait_ge(s_gt, 1)
                        gated_biases()

            with pe.Fori(0, E // 2 - 1) as i:
                steps(i, False)
            steps(E // 2 - 1, True)

        @block.vector
        def _(dve):
            def tt(o, a, b, op):
                return nc.vector.tensor_tensor(o, a, b, op)

            for edge in (wsh[0:32, 2, 0], wsh[0:32, 4, 0], wsh[96:P, 1, 1], wsh[96:P, 3, 1]):
                nc.vector.memset(edge, 0.0).then_inc(c_edge, 1)
            nc.vector.memset(w_halo[:], 0.0).then_inc(c_halo0, 1)
            dve.wait_ge(d_img, 16 * B)
            retile(nc.vector.tensor_copy, 0)
            retile(nc.vector.tensor_copy, 2)
            dve.wait_ge(s_gbps, 1)
            nc.vector.tensor_copy(gb[:, :, 1:], ps[:, 0, 0:2 * (SHIFTS - 1) * 9]
                                  .rearrange("p (h s k) -> p h s k", h=2, s=SHIFTS - 1)).then_inc(s_gb, 1)
            nc.vector.tensor_copy(gb[:, :, 0].rearrange("p h (k c) -> p h k c", c=C),
                                  gb_nat[:, :, :, 0:C]).then_inc(s_gb, 1)
            dve.wait_ge(s_gb, 2)
            nc.vector.tensor_reduce(mcol[:], gb[:, :, :, 6:8].rearrange("p h s k -> p h k s"), AX_X,
                                    ALU.add).then_inc(s_m, 1)
            dve.wait_ge(s_m, 1)
            nc.vector.tensor_copy(wlmh[:, 0:2 * C, D:D + 2].rearrange("p (h c) k -> p h c k", h=2),
                                  mcol[:, :, :].unsqueeze(2).broadcast_to([P, 2, C, 2])).then_inc(s_m, 1)
            dve.wait_ge(c_ones, 3)
            nc.vector.tensor_copy(wlmh[0:HALO, 2 * C:NX, D:D + 2],
                                  ones_f[0:HALO, 0:4].rearrange("p (k n) -> p k n", k=2)).then_inc(s_m, 1)
            nc.vector.tensor_copy(ones_r[:], ones_f[:]).then_inc(s_m, 1)
            dve.wait_ge(c_gath0, 1)
            gather_halo(0)
            gather_halo(1)
            halo_rows = x_halo[64:HALO].rearrange("p k (b y w) -> p k b y w", b=B, y=GRID)
            nc.vector.memset(halo_rows[:, 0, :, 0], 0.0).then_inc(s_hedge, 1)
            nc.vector.memset(halo_rows[:, 1, :, GRID - 1], 0.0).then_inc(s_hedge, 1)
            for g in range(XGROUPS):
                c, wh = g // 2, g % 2
                dve.wait_ge(s_xt, g + 1)
                src = ps[:, XB[g], :].rearrange("p (w r k) -> p k r w", w=4, k=2)

                def part(tensor):
                    return tensor[:, c:2 * C:C, :].rearrange("p k (r w) -> p k r w", w=GRID)[
                        :, :, :, 4 * wh:4 * wh + 4]
                dve.wait_ge(s_xsq, g + 1)
                if c == C - 1:
                    nc.vector.tensor_copy(part(xh), src).then_inc(s_xhi, 1)
                dve.wait_ge(s_xhi, g + 1)
                tt(part(xl), src, part(xh).bitcast(F32), ALU.subtract).then_inc(s_xlo, 1)
            dve.wait_ge(s_gbps, 2)
            nc.vector.tensor_copy(gb_halo[0:HALO].rearrange("p k g -> p (k g)"),
                                  ps[0:HALO, BETAB, 0:4]).then_inc(s_gb, 1)
            for half in range(2):
                for s in range(SHIFTS):
                    dve.wait_ge(d_wsh[half][s], 16)
                    for c in range(C):
                        src = wsh[:, s, half, c * D:(c + 1) * D]
                        dst = w_sum[:, half, c]
                        gam = gb[:, half, s, c:c + 1]
                        if s == 0:
                            ins = nc.vector.tensor_scalar(dst, src, gam, None, ALU.mult)
                        else:
                            dve.wait_ge(s_merge, half * C * SHIFTS + (s - 1) * C + c + 1)
                            ins = nc.vector.scalar_tensor_tensor(out=dst, in0=src, scalar=gam, in1=dst,
                                                                 op0=ALU.mult, op1=ALU.add)
                        ins.then_inc(s_merge, 1)
                if half == 1:
                    dve.wait_ge(d_halo_w, 16 * HALO_W_DMAS)
                    for k in range(2):
                        nc.vector.tensor_scalar(wm_halo[0:HALO, k], w_halo[0:HALO, k], gb_halo[0:HALO, k, 0:1],
                                                None, ALU.mult).then_inc(s_merge, 1)
                dve.wait_ge(s_whi, half + 1)
                ch = slice(half * C, half * C + C)
                tt(wlmh[:, ch, 0:D], w_sum[:, half], wlmh[:, ch, HIGH0:].bitcast(F32),
                   ALU.subtract).then_inc(s_wlo, 1)
                if half == 0:
                    dve.wait_ge(s_hhi, 1)
                    tt(xl[0:HALO, 2 * C:NX], x_halo[0:HALO], xh[0:HALO, 2 * C:NX].bitcast(F32),
                       ALU.subtract).then_inc(s_hlo, 1)
            dve.wait_ge(s_whi, 3)
            ch = slice(2 * C, NX)
            tt(wlmh[0:HALO, ch, 0:D], wm_halo[0:HALO], wlmh[0:HALO, ch, HIGH0:].bitcast(F32),
               ALU.subtract).then_inc(s_wlo, 1)

            n_chain = [0]

            def link(ins):
                n_chain[0] += 1
                ins.then_inc(s_dve, 1)
                dve.wait_ge(s_dve, n_chain[0])

            dve.wait_ge(c_mask, E)
            link(nc.vector.tensor_reduce(mask[:, 0:NK], tri_p[:], AX_X, ALU.add))
            link(nc.vector.tensor_reduce(mask[:, NK:], near[:], AX_X, ALU.min))

            def small_low_parts(groups):
                for n in groups:
                    rem, _, _, col = WGROUPS[n]
                    width = 384 if col == 0 else SPAN - 384
                    dve.wait_ge(s_wathi, n + 1 + (n == 3))
                    rows = slice(REM, P) if rem else slice(0, P)
                    tt(wat[rows, 2 if rem else 1, col:col + width], ps[rows, WB[n], 0:width],
                       wat[rows, 2 if rem else 0, col:col + width].bitcast(F32), ALU.subtract).then_inc(s_watlo, 1)

            def beta_rows(s, count):
                last = C - 1
                for half, c, before in ((1, last, 2), (1, 0, 4), (0, last, 2), (1, 1, 4)):
                    src, bet = wsh[:, s, half, c * D:(c + 1) * D], gb[:, half, s, C + c:C + c + 1]
                    if s == 0 and half == 1:
                        ins = nc.vector.tensor_scalar(w_beta[:, c], src, bet, None, ALU.mult)
                    else:
                        dve.wait_ge(s_wbeta, count + 1 - before)
                        ins = nc.vector.scalar_tensor_tensor(out=w_beta[:, c], in0=src, scalar=bet, in1=w_beta[:, c],
                                                             op0=ALU.mult, op1=ALU.add)
                    ins.then_inc(s_wbeta, 1)
                    count += 1

            small_low_parts((0, 1))
            beta_rows(0, 0)
            beta_rows(1, 4)
            small_low_parts((2, 3))
            for s in range(2, SHIFTS):
                beta_rows(s, 4 * s)
            dve.wait_ge(s_sumsq, 1)
            nc.vector.tensor_scalar(st4[:, 1], ps[:, SQB, SQ0:SQ0 + 2 * TT:2], 1.0 / FEAT, None, ALU.mult)\
                .then_inc(s_meansq, 1)
            dve.wait_ge(s_emb, 1)
            dve.wait_ge(s_u, 1)
            tt(u_sum[:], ps[:, UB, HIGH0:LMH], u_part[:], ALU.add).then_inc(s_urow, 1)

            def bias():
                dve.wait_ge(s_bias, 1)
                tt(bias_row[:], ps[:, BETAB, BETA0:BETA0 + D], bias_row[:], ALU.add).then_inc(s_urow, 1)

            def patch_statistics(g):
                ts = slice(2 * g, 2 * g + 2)
                dve.wait_ge(s_emb, g + 2)
                link(nc.vector.tensor_scalar(st4[:, 0, ts].unsqueeze(2), ps[:, EMB0 + 2 * g:EMB0 + 2 * g + 2, D:D + 1],
                                             -1.0 / FEAT, None, ALU.mult))
                dve.wait_ge(s_meansq, 1)
                link(tt(st4[:, 2, ts], st4[:, 0, ts], st4[:, 0, ts], ALU.mult))
                link(tt(st4[:, 3, ts], st4[:, 1, ts], st4[:, 2, ts], ALU.subtract))
                nc.vector.tensor_scalar(st4[:, 4, ts], st4[:, 3, ts], LN_EPS, None, ALU.add).then_inc(s_stat, 1)

            def less_mean(g):
                for t in (2 * g, 2 * g + 1):
                    nc.vector.scalar_tensor_tensor(out=t_a[:, t], in0=u_sum[:], scalar=st4[:, 0, t:t + 1],
                                                   in1=ps[:, EMB0 + t, HIGH0:LMH], op0=ALU.mult,
                                                   op1=ALU.add).then_inc(s_t1, 1)
                for t in (2 * g, 2 * g + 1):
                    dve.wait_ge(s_t1, t + 1)
                    tt(t_a[:, t], t_a[:, t], ps[:, EMB0 + t, 0:D], ALU.add).then_inc(s_t2, 1)

            def embedding(g):
                dve.wait_ge(s_pow, g + 1)
                for t in (2 * g, 2 * g + 1):
                    dve.wait_ge(s_t2, t + 1)
                    nc.vector.scalar_tensor_tensor(out=h[:, t], in0=t_a[:, t], scalar=st4[:, 5, t:t + 1],
                                                   in1=bias_row[:], op0=ALU.mult, op1=ALU.add).then_inc(s_h, 1)

            def statistics(which, g, src, ready, count):
                for t in (2 * g, 2 * g + 1):
                    dve.wait_ge(ready, count(t))
                    nc.vector.bn_stats(bn[:, which, t], src[:, t]).then_inc(s_bn, 1)
                for t in (2 * g, 2 * g + 1):
                    dve.wait_ge(s_bn, which * TT + t + 1)
                    nc.vector.bn_aggr(mv[:, which, t], bn[:, which, t]).then_inc(s_mv, 1)
                dve.wait_ge(s_mv, which * TT + 2 * g + 2)
                nc.vector.tensor_scalar(ve[:, which, 2 * g:2 * g + 2].unsqueeze(2), mv[:, which, 2 * g:2 * g + 2, 1:2],
                                        LN_EPS, None, ALU.add).then_inc(s_ve, 1)

            def normalised(which, g, src, dst):
                dve.wait_ge(s_rs, which * G + g + 1)
                for t in (2 * g, 2 * g + 1):
                    nc.vector.tensor_scalar(dst[:, t, 0:D], src[:, t], mv[:, which, t, 0:1],
                                            rs[:, which, t:t + 1], ALU.subtract, ALU.mult).then_inc(s_n, 1)

            def low_parts(g, hi_ready, banks, dst, done):
                dve.wait_ge(hi_ready, g + 1)
                cols = slice(g * TG, (g + 1) * TG)
                tt(dst[:, 1:4:2, cols], ps[:, banks[g], :].rearrange("p (k t) -> p k t", k=2),
                   dst[:, 0:4:2, cols].bitcast(F32), ALU.subtract).then_inc(done, 1)

            patch_statistics(0)
            dve.wait_ge(s_beta, 1)
            less_mean(0)
            bias()
            dve.wait_ge(s_urow, 2)
            embedding(0)
            statistics(0, 0, h, s_h, lambda t: t + 1)
            patch_statistics(1)
            normalised(0, 0, h, n1)
            less_mean(1)
            low_parts(0, s_nhi, NTB, nt, s_nlo)
            embedding(1)
            statistics(0, 1, h, s_h, lambda t: t + 1)
            normalised(0, 1, h, n1)
            dve.wait_ge(s_vbias, 1)
            dve.wait_ge(d_rows, 16 * 3)
            tt(const_row[:], ps[:, UB, 0:D], outb_row[:], ALU.add).then_inc(s_row, 1)
            low_parts(1, s_nhi, NTB, nt, s_nlo)

            def biased_q_k(t):
                dve.wait_ge(s_tok, t + 1)
                tt(qkv[:, t, 0:2 * D], ps[:, 3 * (t % 2), 0:2 * D], qkvb_row[:, 0:2 * D], ALU.add).then_inc(s_qk, 1)

            def near_scores(t):
                dve.wait_ge(s_qk, t + 1)
                dve.wait_ge(d_prev[t], 16 * (1 if t == 0 else 2))
                tt(prod[:, t % 2], kv[:, t, :, 0:D], qkv[:, t, 0:D].unsqueeze(1).broadcast_to([P, 2, D]),
                   ALU.mult).then_inc(s_prod, 1)
                dve.wait_ge(s_prod, t + 1)
                nc.vector.tensor_reduce(sc[:, t, NK:],
                                        prod[:, t % 2].rearrange("p s (g d) -> p s g d", d=HD), AX_X,
                                        ALU.add).then_inc(s_near, 1)

            def key_blocks():
                dve.wait_ge(s_ktsb, 2)
                for kbd, m, n, gs_ in ((kbd_a, P, 0, 8), (kbd_b, REM, 1, 4)):
                    tt(kbd[0:m],
                       kts[0:m, n].rearrange("p (b j) -> p b j", b=B).unsqueeze(2).broadcast_to([m, B, gs_, NK]),
                       head_of_row[0:m, 0:gs_].unsqueeze(1).unsqueeze(3).broadcast_to([m, B, gs_, NK]),
                       ALU.mult).then_inc(s_kbd, 1)

            def v_blocks(n):
                dve.wait_ge(s_vps, n + 1)
                tt(vbd[0:WROWS, 2 * n:2 * n + 2].rearrange("p b (g d) -> p b g d", d=HD),
                   ps[0:WROWS, VB[n], 0:2 * D].rearrange("p (b g d) -> p b g d", b=2, d=HD),
                   head_of_key[0:WROWS, :].unsqueeze(1).unsqueeze(3).broadcast_to([WROWS, 2, HEADS, HD]),
                   ALU.mult).then_inc(s_vbd, 1)

            def scores(g):
                ts = slice(2 * g, 2 * g + 2)
                m4 = mask[:, :].unsqueeze(1).unsqueeze(3).broadcast_to([P, 2, NS, HEADS])
                dve.wait_ge(s_sps, g + 1)
                dve.wait_ge(s_near, 2 * g + 2)
                tt(sc[:, ts, 0:NK], ps[:, SB[g], 0:2 * HEADS * NK]
                   .rearrange("p (t g j) -> p t j g", t=2, j=NK), m4[:, :, 0:NK], ALU.add).then_inc(s_sc, 1)
                tt(sc[:, ts, NK:], sc[:, ts, NK:], m4[:, :, NK:], ALU.add).then_inc(s_sc, 1)
                dve.wait_ge(s_sc, 2 * g + 2)
                nc.vector.tensor_reduce(mx[:, ts], sc[:, ts].rearrange("p t s g -> p t g s"), AX_X,
                                        ALU.max).then_inc(s_mx, 1)
                dve.wait_ge(s_mx, g + 1)
                tt(sc[:, ts], sc[:, ts], mx[:, ts].unsqueeze(2).broadcast_to([P, 2, NS, HEADS]),
                   ALU.subtract).then_inc(s_sub, 1)

            def denominators(g):
                ts = slice(2 * g, 2 * g + 2)
                dve.wait_ge(s_exp, g + 1)
                link(nc.vector.tensor_reduce(den[:, ts], pr[:, ts].rearrange("p t s g -> p t g s"), AX_X, ALU.add))
                nc.vector.reciprocal(rden[:, ts], den[:, ts]).then_inc(s_rden, 1)

            def outputs(g):
                ts = slice(2 * g, 2 * g + 2)
                acc_g = part_sum[g]
                dve.wait_ge(s_pv, g + 1)
                dve.wait_ge(s_nv, g + 1)
                tt(acc_g[:, 1], acc_g[:, 0], ps[:, PVB[g], 0:2 * D].rearrange("p (t n) -> p t n", t=2),
                   ALU.add).then_inc(s_pvn, 1)
                dve.wait_ge(s_pvn, g + 1)
                dve.wait_ge(s_rden, g + 1)
                tt(ao[:, ts, 0:D].rearrange("p t (g d) -> p t g d", d=HD),
                   acc_g[:, 1].rearrange("p t (g d) -> p t g d", d=HD),
                   rden[:, ts].unsqueeze(3).broadcast_to([P, 2, HEADS, HD]), ALU.mult).then_inc(s_ao, 1)

            biased_q_k(0)
            key_blocks()
            biased_q_k(1)
            near_scores(0)
            biased_q_k(2)
            near_scores(1)
            biased_q_k(3)
            scores(0)
            near_scores(2)
            v_blocks(0)
            v_blocks(1)
            near_scores(3)
            scores(1)
            v_blocks(2)
            v_blocks(3)
            denominators(0)
            outputs(0)
            denominators(1)
            outputs(1)
            low_parts(0, s_ahi, ATB, aot, s_alo)
            low_parts(1, s_ahi, ATB, aot, s_alo)

            def residual(g):
                dve.wait_ge(s_hb, 1)
                dve.wait_ge(s_op, g + 1)
                ts = slice(2 * g, 2 * g + 2)
                tt(h2[:, ts], hb[:, ts], ps[:, OB[g], 0:2 * D].rearrange("p (t n) -> p t n", t=2),
                   ALU.add).then_inc(s_h2, 1)
                statistics(1, g, h2, s_h2, lambda t: t // 2 + 1)

            residual(0)
            normalised(1, 0, h2, n2)
            residual(1)
            low_parts(0, s_n2hi, N2B, n2t, s_n2lo)
            normalised(1, 1, h2, n2)
            low_parts(1, s_n2hi, N2B, n2t, s_n2lo)

            def two_largest():
                dve.wait_ge(s_rt, 1)
                nc.vector.tensor_copy(lg[:, :, :], ps[:, 7, 0:TT * E].rearrange("p (t e) -> p t e", t=TT))\
                    .then_inc(s_acc, TT)
                dve.wait_ge(s_acc, TT)
                for t in range(TT):
                    nc.vector.max(top[:, t], lg[:, t]).then_inc(s_gtop, 1)
                dve.wait_ge(s_gtop, TT)
                tt(gs[:, 0], top[:, :, 1], top[:, :, 0], ALU.subtract).then_inc(s_gsub, 1)

            def their_experts():
                for t in range(TT):
                    nc.vector.max_index(topi[:, t], top[:, t], lg[:, t]).then_inc(s_gidx, 1)
                dve.wait_ge(s_gidx, TT)
                link(nc.vector.tensor_copy(topf[:], topi[:]))
                iota3 = iota_e[:, :].unsqueeze(1).broadcast_to([P, TT, E])
                for n in range(2):
                    link(tt(oh[:, n], iota3, topf[:, :, n:n + 1].broadcast_to([P, TT, E]), ALU.is_equal))

            def gate_values():
                dve.wait_ge(s_gexp, 1)
                link(nc.vector.tensor_scalar(gs[:, 0], gs[:, 1], 1.0, None, ALU.add))
                link(nc.vector.reciprocal(gs[:, 2], gs[:, 0]))
                link(tt(gs[:, 3], gs[:, 1], gs[:, 2], ALU.mult))
                for n in range(2):
                    link(tt(oh[:, n], oh[:, n], gs[:, 2 + n].unsqueeze(2).broadcast_to([P, TT, E]), ALU.mult))
                tt(gates[:], oh[:, 0], oh[:, 1], ALU.add).then_inc(s_gate, 1)
                dve.wait_ge(s_gate, 1)

            def add_biases():
                dve.wait_ge(s_gtps, 1)
                nc.vector.tensor_copy(gt[:], ps[0:E, GTB, :].rearrange("e (t p) -> e t p", t=TT)).then_inc(s_gt, 1)
                for t in range(TT):
                    dve.wait_ge(s_b2, t // 2 * 2 + 2)
                    tt(acc[:, t], acc[:, t], ps[:, HPB[t // 2], (t % 2) * D:(t % 2 + 1) * D],
                       ALU.add).then_inc(s_b2add, 1)
                dve.wait_ge(s_b2add, TT)

            def low_hidden(i, j):
                dve.wait_ge(s_ghi, i * (2 * FC) + j + 1)
                tt(g_lo[:, j % NG], gf[:, j % NG], g_hi[:, j % NG].bitcast(F32), ALU.subtract).then_inc(s_glo, 1)

            def add_expert(e):
                for t0 in range(0, TT, 2):
                    for t in (t0, t0 + 1):
                        dve.wait_ge(s_mm2, e * (FC * TT) + (FC - 1) * TT + t + 1)
                        nc.vector.scalar_tensor_tensor(out=t_a[:, t], in0=ps[:, AB[t], 0:D],
                                                       scalar=gates[:, t, bass.ds(e, 1)], in1=acc[:, t],
                                                       op0=ALU.mult, op1=ALU.add).then_inc(s_evl, 1)
                    for t in (t0, t0 + 1):
                        dve.wait_ge(s_evl, e * TT + t + 1)
                        nc.vector.scalar_tensor_tensor(out=acc[:, t], in0=ps[:, AB[t], D:2 * D],
                                                       scalar=gates[:, t, bass.ds(e, 1)], in1=t_a[:, t],
                                                       op0=ALU.mult, op1=ALU.add).then_inc(s_acc, 1)

            def pair(i, last):
                for slot in range(2):
                    for j in range(LAG, FC + LAG):
                        if j == FC + LAG - 2:
                            if last and slot == 1:
                                add_biases()
                            add_expert(i * 2 + slot)
                        if not (last and slot == 1 and j >= FC):
                            low_hidden(i, slot * FC + j)

            dve.wait_ge(s_rl, 2)
            nc.vector.tensor_copy(lgt[:], ps[0:E, RB, :]).then_inc(s_rlsb, 1)
            low_hidden(0, 0)
            two_largest()
            low_hidden(0, 1)
            their_experts()
            low_hidden(0, 2)
            gate_values()
            with dve.Fori(0, E // 2 - 1) as i:
                pair(i, False)
            pair(E // 2 - 1, True)


_INS = ["x", "L0_tok_ln_gamma", "L0_tok_ln_beta", "L0_tok_w", "L0_tok_b", "L0_attn_qkv_w", "L0_attn_qkv_b",
        "L0_attn_out_w", "L0_attn_out_b", "L0_ffn_router_w", "L0_ffn_w1", "L0_ffn_b1", "L0_ffn_w2", "L0_ffn_b2"]


def kernel(**inputs):
    import numpy as np
    import concourse.bacc as bacc
    from concourse.bass_utils import run_bass_kernel_spmd

    nc = bacc.Bacc("TRN2", target_bir_lowering=False, num_devices=1)
    arrays, args = {}, []
    for name in _INS:
        a = np.ascontiguousarray(inputs[name])
        arrays[f"in_{name}"] = a
        args.append(nc.dram_tensor(f"in_{name}", a.shape, mybir.dt.from_np(a.dtype), kind="ExternalInput").ap())
    b = inputs["x"].shape[0]
    d = inputs["L0_tok_w"].shape[1]
    s = (inputs["x"].shape[2] // PATCH) ** 2
    out = nc.dram_tensor("out", (b, s, d), F32, kind="ExternalOutput").ap()
    vit_tower(nc, *args, out)
    r = run_bass_kernel_spmd(nc, [arrays], core_ids=[0])
    return r.results[0]["out"]
```
